# Optimizing a Trainium2 kernel written in Bass

```python
import numpy as np
import jax
import jax.numpy as jnp

def _softmax(x, axis=-1):
    return jax.nn.softmax(x, axis=axis)

def _gelu(x):
    return jax.nn.gelu(x, approximate=True)

def _silu(x):
    return jax.nn.silu(x)

def _sigmoid(x):
    return jax.nn.sigmoid(x)

def _layernorm(x, axis=-1, eps=1e-05):
    m = jnp.mean(x, axis=axis, keepdims=True)
    v = jnp.var(x, axis=axis, keepdims=True)
    return (x - m) / jnp.sqrt(v + eps)

def _scatter_add(tgt, idx, src, axis=0):
    return tgt.at[idx].add(src)

def _segment_sum(src, seg, n):
    return jax.ops.segment_sum(src, seg, n)
kernel_name = 'mk_seq_postln_d2_jaxref_r4_a55edf'

def setup_inputs(seed: int=0):
    np.random.seed(seed)
    _w = jnp.asarray

    def _L0_attn_setup():
        import jax, jax.numpy as jnp
        import numpy as np
        D_MODEL = 512
        N_HEAD = 16
        SEM_DIM = 256
        GEO_DIM = 256
        ATTN_DIM = 512
        ROPE_BASE = 10000.0

        def _rope(x, base=ROPE_BASE):
            S, d = (x.shape[-2], x.shape[-1])
            inv_freq = 1.0 / base ** (jnp.arange(0, d, 2, dtype=jnp.float32) / d)
            t = jnp.arange(S, dtype=jnp.float32)
            freqs = jnp.einsum('s,f->sf', t, inv_freq)
            cos, sin = (jnp.cos(freqs), jnp.sin(freqs))
            x1, x2 = (x[..., :d // 2], x[..., d // 2:])
            return jnp.concatenate([x1 * cos - x2 * sin, x1 * sin + x2 * cos], axis=-1).astype(x.dtype)

        def _split_heads(y, H):
            B, S, dim = y.shape
            return y.reshape(B, S, H, dim // H).transpose(0, 2, 1, 3)
        key = jax.random.key(seed)
        ks = jax.random.split(key, 7)
        B, S = (2, 512)
        sd = 0.02
        return {'x': jax.random.normal(ks[0], (B, S, D_MODEL), dtype=jnp.float32), 'Wq_sem': jax.random.normal(ks[1], (SEM_DIM, D_MODEL), dtype=jnp.float32) * sd, 'Wk_sem': jax.random.normal(ks[2], (SEM_DIM, D_MODEL), dtype=jnp.float32) * sd, 'Wq_geo': jax.random.normal(ks[3], (GEO_DIM, D_MODEL), dtype=jnp.float32) * sd, 'Wk_geo': jax.random.normal(ks[4], (GEO_DIM, D_MODEL), dtype=jnp.float32) * sd, 'Wv': jax.random.normal(ks[5], (ATTN_DIM, D_MODEL), dtype=jnp.float32) * sd, 'Wo': jax.random.normal(ks[6], (D_MODEL, ATTN_DIM), dtype=jnp.float32) * sd}
    _L0_attn_in = _L0_attn_setup()

    def _L0_ffn_setup():
        import jax, jax.numpy as jnp
        import numpy as np
        DIM = 512
        HID = 256
        E = 8
        K = 2
        SHID = HID * 1
        INIT = 0.02
        key = jax.random.key(seed)
        ks = jax.random.split(key, 9)
        return {'x': jax.random.normal(ks[0], (2, 256, DIM), jnp.float32), 'expert_bias': jnp.zeros((E,), jnp.float32), 'gate_w': jax.random.normal(ks[1], (E, DIM), jnp.float32) * INIT, 'w1': jax.random.normal(ks[2], (E, HID, DIM), jnp.float32) * INIT, 'w2': jax.random.normal(ks[3], (E, DIM, HID), jnp.float32) * INIT, 'w3': jax.random.normal(ks[4], (E, HID, DIM), jnp.float32) * INIT, 'sw1': jax.random.normal(ks[5], (SHID, DIM), jnp.float32) * INIT, 'sw2': jax.random.normal(ks[6], (DIM, SHID), jnp.float32) * INIT, 'sw3': jax.random.normal(ks[7], (SHID, DIM), jnp.float32) * INIT}
    _L0_ffn_in = _L0_ffn_setup()

    def _L1_attn_setup():
        import jax, jax.numpy as jnp
        import numpy as np
        HEAD_DIM = 128
        ROPE_BASE = 10000.0

        def _rope(x):
            B, S, E = x.shape
            H = E // HEAD_DIM
            xh = x.reshape(B, S, H, HEAD_DIM)
            half = HEAD_DIM // 2
            inv_freq = 1.0 / ROPE_BASE ** (jnp.arange(0, half, dtype=jnp.float32) / half)
            pos = jnp.arange(S, dtype=jnp.float32)
            freqs = pos[:, None] * inv_freq[None, :]
            emb = jnp.concatenate([freqs, freqs], axis=-1)
            cos = jnp.cos(emb)[None, :, None, :].astype(x.dtype)
            sin = jnp.sin(emb)[None, :, None, :].astype(x.dtype)
            x1, x2 = (xh[..., :half], xh[..., half:])
            rot = jnp.concatenate([-x2, x1], axis=-1)
            out = xh * cos + rot * sin
            return out.reshape(B, S, E)
        key = jax.random.key(seed)
        ks = jax.random.split(key, 6)
        B, S, E = (2, 1024, 512)
        s = lambda d: 1.0 / np.sqrt(d)
        return {'x': jax.random.normal(ks[0], (B, S, E), jnp.float32), 'q_w': jax.random.normal(ks[1], (E, E), jnp.float32) * s(E), 'q_b': jax.random.normal(ks[2], (E,), jnp.float32) * 0.02, 'kv_w': jax.random.normal(ks[3], (2 * E, E), jnp.float32) * s(E), 'kv_b': jax.random.normal(ks[4], (2 * E,), jnp.float32) * 0.02, 'o_w': jax.random.normal(ks[5], (E, E), jnp.float32) * s(E)}
    _L1_attn_in = _L1_attn_setup()

    def _L1_ffn_setup():
        import jax, jax.numpy as jnp
        import numpy as np

        def _sparsify_2to4(h):
            B, S, I = h.shape
            g = h.reshape(B, S, I // 4, 4)
            a = jnp.abs(g)
            _, idx = jax.lax.top_k(a, 2)
            pos = jnp.arange(4)
            mask = (pos == idx[..., 0:1]) | (pos == idx[..., 1:2])
            return (g * mask.astype(g.dtype)).reshape(B, S, I)
        key = jax.random.key(seed)
        k1, k2, k3, k4 = jax.random.split(key, 4)
        B, S, H, I = (4, 512, 512, 2048)
        x = jax.random.normal(k1, (B, S, H), dtype=jnp.float32)
        w_gate = jax.random.normal(k2, (H, I), dtype=jnp.float32) / np.sqrt(H)
        w_up = jax.random.normal(k3, (H, I), dtype=jnp.float32) / np.sqrt(H)
        w_down = jax.random.normal(k4, (I, H), dtype=jnp.float32) / np.sqrt(I)
        return {'x': x, 'w_gate': w_gate, 'w_up': w_up, 'w_down': w_down}
    _L1_ffn_in = _L1_ffn_setup()
    _d = {'L0_attn_x': _L0_attn_in['x'], 'L0_attn_Wq_sem': _L0_attn_in['Wq_sem'], 'L0_attn_Wk_sem': _L0_attn_in['Wk_sem'], 'L0_attn_Wq_geo': _L0_attn_in['Wq_geo'], 'L0_attn_Wk_geo': _L0_attn_in['Wk_geo'], 'L0_attn_Wv': _L0_attn_in['Wv'], 'L0_attn_Wo': _L0_attn_in['Wo'], 'L0_ffn_expert_bias': _L0_ffn_in['expert_bias'], 'L0_ffn_gate_w': _L0_ffn_in['gate_w'], 'L0_ffn_w1': _L0_ffn_in['w1'], 'L0_ffn_w2': _L0_ffn_in['w2'], 'L0_ffn_w3': _L0_ffn_in['w3'], 'L0_ffn_sw1': _L0_ffn_in['sw1'], 'L0_ffn_sw2': _L0_ffn_in['sw2'], 'L0_ffn_sw3': _L0_ffn_in['sw3'], 'L1_attn_q_w': _L1_attn_in['q_w'], 'L1_attn_q_b': _L1_attn_in['q_b'], 'L1_attn_kv_w': _L1_attn_in['kv_w'], 'L1_attn_kv_b': _L1_attn_in['kv_b'], 'L1_attn_o_w': _L1_attn_in['o_w'], 'L1_ffn_w_gate': _L1_ffn_in['w_gate'], 'L1_ffn_w_up': _L1_ffn_in['w_up'], 'L1_ffn_w_down': _L1_ffn_in['w_down']}
    _x0 = _d['L0_attn_x']
    _d['L0_attn_x'] = jax.random.normal(jax.random.fold_in(jax.random.key(seed), 1), (1, 2048, 512), dtype=_x0.dtype)
    del _x0
    return _d

def reference(L0_attn_x, L0_attn_Wq_sem, L0_attn_Wk_sem, L0_attn_Wq_geo, L0_attn_Wk_geo, L0_attn_Wv, L0_attn_Wo, L0_ffn_expert_bias, L0_ffn_gate_w, L0_ffn_w1, L0_ffn_w2, L0_ffn_w3, L0_ffn_sw1, L0_ffn_sw2, L0_ffn_sw3, L1_attn_q_w, L1_attn_q_b, L1_attn_kv_w, L1_attn_kv_b, L1_attn_o_w, L1_ffn_w_gate, L1_ffn_w_up, L1_ffn_w_down):

    def _L0_attn_ref(x, Wq_sem, Wk_sem, Wq_geo, Wk_geo, Wv, Wo):
        import jax, jax.numpy as jnp
        import numpy as np
        D_MODEL = 512
        N_HEAD = 16
        SEM_DIM = 256
        GEO_DIM = 256
        ATTN_DIM = 512
        ROPE_BASE = 10000.0

        def _rope(x, base=ROPE_BASE):
            S, d = (x.shape[-2], x.shape[-1])
            inv_freq = 1.0 / base ** (jnp.arange(0, d, 2, dtype=jnp.float32) / d)
            t = jnp.arange(S, dtype=jnp.float32)
            freqs = jnp.einsum('s,f->sf', t, inv_freq)
            cos, sin = (jnp.cos(freqs), jnp.sin(freqs))
            x1, x2 = (x[..., :d // 2], x[..., d // 2:])
            return jnp.concatenate([x1 * cos - x2 * sin, x1 * sin + x2 * cos], axis=-1).astype(x.dtype)

        def _split_heads(y, H):
            B, S, dim = y.shape
            return y.reshape(B, S, H, dim // H).transpose(0, 2, 1, 3)
        B, S, _ = x.shape
        H = N_HEAD
        q_sem = _split_heads(x @ Wq_sem.T, H)
        k_sem = _split_heads(x @ Wk_sem.T, H)
        q_geo = _rope(_split_heads(x @ Wq_geo.T, H))
        k_geo = _rope(_split_heads(x @ Wk_geo.T, H))
        v = _split_heads(x @ Wv.T, H)
        q = jnp.concatenate([q_sem, q_geo], axis=-1)
        k = jnp.concatenate([k_sem, k_geo], axis=-1)
        scale = 1.0 / jnp.sqrt(jnp.asarray(q.shape[-1], dtype=jnp.float32))
        scores = jnp.einsum('bhqd,bhkd->bhqk', q, k).astype(jnp.float32) * scale
        causal = jnp.tril(jnp.ones((S, S), dtype=bool))
        scores = jnp.where(causal, scores, jnp.finfo(jnp.float32).min)
        attn = jax.nn.softmax(scores, axis=-1).astype(v.dtype)
        out = jnp.einsum('bhqk,bhkd->bhqd', attn, v)
        out = out.transpose(0, 2, 1, 3).reshape(B, S, ATTN_DIM)
        return out @ Wo.T

    def _L0_ffn_ref(x, expert_bias, gate_w, w1, w2, w3, sw1, sw2, sw3):
        import jax, jax.numpy as jnp
        import numpy as np
        DIM = 512
        HID = 256
        E = 8
        K = 2
        SHID = HID * 1
        INIT = 0.02
        B, S, D = x.shape
        xf = x.reshape(-1, D)
        N = xf.shape[0]
        scores = jax.nn.sigmoid((xf @ gate_w.T).astype(jnp.float32))
        _, sel = jax.lax.top_k(scores + expert_bias[None, :], K)
        top_scores = jnp.take_along_axis(scores, sel, axis=1)
        flat_exp = sel.reshape(-1)
        order = jnp.argsort(flat_exp, stable=True)
        sorted_exp = flat_exp[order]
        tok_idx = order // K
        sc_sorted = top_scores.reshape(-1)[order]
        rin = xf[tok_idx] * sc_sorted[:, None].astype(x.dtype)
        out_sorted = jnp.zeros_like(rin)
        for e in range(E):
            m = (sorted_exp == e)[:, None].astype(rin.dtype)
            h = jax.nn.silu(rin @ w1[e].T) * (rin @ w3[e].T)
            out_sorted = out_sorted + m * (h @ w2[e].T)
        routed = jnp.zeros((N, D), x.dtype).at[tok_idx].add(out_sorted)
        shared = jax.nn.silu(xf @ sw1.T) * (xf @ sw3.T) @ sw2.T
        return (routed + shared).reshape(B, S, D)

    def _L1_attn_ref(x, q_w, q_b, kv_w, kv_b, o_w):
        import jax, jax.numpy as jnp
        import numpy as np
        HEAD_DIM = 128
        ROPE_BASE = 10000.0

        def _rope(x):
            B, S, E = x.shape
            H = E // HEAD_DIM
            xh = x.reshape(B, S, H, HEAD_DIM)
            half = HEAD_DIM // 2
            inv_freq = 1.0 / ROPE_BASE ** (jnp.arange(0, half, dtype=jnp.float32) / half)
            pos = jnp.arange(S, dtype=jnp.float32)
            freqs = pos[:, None] * inv_freq[None, :]
            emb = jnp.concatenate([freqs, freqs], axis=-1)
            cos = jnp.cos(emb)[None, :, None, :].astype(x.dtype)
            sin = jnp.sin(emb)[None, :, None, :].astype(x.dtype)
            x1, x2 = (xh[..., :half], xh[..., half:])
            rot = jnp.concatenate([-x2, x1], axis=-1)
            out = xh * cos + rot * sin
            return out.reshape(B, S, E)
        scale = HEAD_DIM ** (-0.5)
        E = x.shape[-1]
        q = (x @ q_w.T + q_b) * scale
        kv = x @ kv_w.T + kv_b
        k, v = (kv[..., :E], kv[..., E:])
        q = _rope(q)
        k = _rope(k)
        scores = jnp.einsum('bse,bte->bst', q, k)
        attn = jax.nn.softmax(scores, axis=-1)
        o = jnp.einsum('bst,bte->bse', attn, v)
        return o @ o_w.T

    def _L1_ffn_ref(x, w_gate, w_up, w_down):
        import jax, jax.numpy as jnp
        import numpy as np

        def _sparsify_2to4(h):
            B, S, I = h.shape
            g = h.reshape(B, S, I // 4, 4)
            a = jnp.abs(g)
            _, idx = jax.lax.top_k(a, 2)
            pos = jnp.arange(4)
            mask = (pos == idx[..., 0:1]) | (pos == idx[..., 1:2])
            return (g * mask.astype(g.dtype)).reshape(B, S, I)
        h = jax.nn.silu(jnp.einsum('bsh,hi->bsi', x, w_gate)) * jnp.einsum('bsh,hi->bsi', x, w_up)
        h_sparse = _sparsify_2to4(h)
        return jnp.einsum('bsi,ih->bsh', h_sparse, w_down)
    x = L0_attn_x
    x = _layernorm(x + _L0_attn_ref(x, L0_attn_Wq_sem, L0_attn_Wk_sem, L0_attn_Wq_geo, L0_attn_Wk_geo, L0_attn_Wv, L0_attn_Wo), axis=-1)
    x = _layernorm(x + _L0_ffn_ref(x, L0_ffn_expert_bias, L0_ffn_gate_w, L0_ffn_w1, L0_ffn_w2, L0_ffn_w3, L0_ffn_sw1, L0_ffn_sw2, L0_ffn_sw3), axis=-1)
    x = _layernorm(x + _L1_attn_ref(x, L1_attn_q_w, L1_attn_q_b, L1_attn_kv_w, L1_attn_kv_b, L1_attn_o_w), axis=-1)
    x = _layernorm(x + _L1_ffn_ref(x, L1_ffn_w_gate, L1_ffn_w_up, L1_ffn_w_down), axis=-1)
    return x

_drawn_inputs = setup_inputs


def setup_inputs(seed=0):
    import zlib

    import numpy as np

    out = dict(_drawn_inputs(seed))
    spreads = {'L0_ffn_expert_bias': (0.0, 0.298)}
    factors = {'L0_attn_Wq_sem': 7.35,
     'L0_attn_Wk_sem': 6.858,
     'L0_attn_Wq_geo': 8.0,
     'L0_attn_Wk_geo': 8.0,
     'L1_attn_q_b': 4.792,
     'L0_ffn_gate_w': 4.068}
    for name, (base, spread) in spreads.items():
        noise = np.random.default_rng([zlib.crc32(name.encode()), seed]).standard_normal(out[name].shape)
        drawn = base * np.exp(spread * noise) if base else spread * noise
        out[name] = jnp.asarray(drawn.astype(out[name].dtype))
    for name, factor in factors.items():
        out[name] = (out[name] * factor).astype(out[name].dtype)
    return out
```

```python
import concourse.bass as bass
from concourse import mybir
from concourse.alu_op_type import AluOpType as ALU
from contextlib import ExitStack

F32 = mybir.dt.float32
F32R = mybir.dt.float32r
BF16 = mybir.dt.bfloat16
ACT = mybir.ActivationFunctionType
AX = mybir.AxisListType.X

P = 128
S = 2048
D = 512
ND = D // P
CH = 512
NC = S // CH
TC = CH // P
NT = S // P
EPS = 1e-5

H0, HD0 = 16, 32
GH = P // HD0
NG = H0 // GH
SCALE0 = float(HD0) ** -0.5
BIG = -float(2 ** 100)

NE, HID = 8, 256
NJ = HID // P
EW = ND * HID * 2 + NJ * D

SCALE1 = 128.0 ** -0.5

INTER = 2048
NQ = INTER // (4 * P)


def mm3(nc, out, wh, wl, xh, xl, start=True, stop=True):
    nc.tensor.matmul(out, wh, xh, start=start, stop=False, skip_group_check=True)
    nc.tensor.matmul(out, wh, xl, start=False, stop=False, skip_group_check=True)
    return nc.tensor.matmul(out, wl, xh, start=False, stop=stop, skip_group_check=True)


def f32(ap):
    return ap.bitcast(F32)


class Mem:

    def __init__(self, nc, ctx, stage):
        self.nc, self.ctx, self.stage = nc, ctx, stage

    def sb(self, name, shape, dt=F32):
        return self.ctx.enter_context(self.nc.sbuf_tensor(f"{self.stage}_{name}", shape, dt))

    def ps(self, name, shape):
        return self.ctx.enter_context(self.nc.psum_tensor(f"{self.stage}_{name}", shape, F32))

    def sem(self, name):
        return self.nc.alloc_semaphore(name=f"{self.stage}_{name}")


class Ring:

    def __init__(self, nc, name):
        self.sems = [nc.alloc_semaphore(name=f"{name}{i}") for i in range(TC)]
        self.before = [0] * TC

    def wait(self, eng, buf, k):
        eng.wait_ge(self.sems[buf], 16 * (self.before[buf] + k))

    def wait_turn(self, eng, buf, n, each=1):
        eng.wait_ge(self.sems[buf], 16 * self.before[buf] + 8 * each * (n - buf) + 16 * each)

    def stage_over(self, bufs, k):
        for i in range(bufs):
            self.before[i] += k


def wait_alone(eng, sem, value, held, at_least):
    if not isinstance(value, int):
        eng.compute_val(value)
    eng.wait_ge(held, at_least)
    eng.wait_ge(sem, value)


def layer0_attention(nc, loads, stores, xT, wqkv, rope, rot, eye, masks, attn_out):
    steps = [(c, p, kt) for c in range(NC) for p in range(2) for kt in range(TC * (c + 1))]
    items = [(c, p) for c in range(NC) for p in range(2)]
    units = {n: [(h, t, u) for h in range(2) for t in range(TC) for u in range(c + 1)]
             for n, (c, p) in enumerate(items)}
    first_step = {n: next(i for i, s in enumerate(steps) if s[:2] == it) for n, it in enumerate(items)}
    first_unit = {n: sum(len(units[m]) for m in range(n)) for n in units}
    NS, NU, NI = len(steps), sum(map(len, units.values())), len(items)
    events = [("proj", 0), ("split", 0)] + [("unit", 0, i) for i in range(len(units[0]))]
    for n, (c, p) in enumerate(items):
        events.append(("max", n))
        if p == 0 and c + 1 < NC:
            events.append(("proj", c + 1))
        events.append(("shift", n))
        length = TC * (c + 1)
        todo = len(units[n + 1]) if n + 1 < NI else 0
        for j in range(length):
            events.append(("step", n, first_step[n] + j))
            if j == 0 and n > 0:
                events.append(("out", n - 1))
            if j == 1 and p == 0 and c + 1 < NC:
                events.append(("split", c + 1))
            if j == 2 and n > 0:
                events.append(("turn", n - 1))
            for i in range(todo * j // length, todo * (j + 1) // length):
                events.append(("unit", n + 1, i))
    events += [("flush",), ("out", NI - 1), ("turn", NI - 1)]
    NDMA = 2 * 3 * GH

    with ExitStack() as ctx:
        m = Mem(nc, ctx, "a0")
        xh = m.sb("xh", [P, ND, S], F32R)
        xl = m.sb("xl", [P, ND, S], F32R)
        cos = m.sb("cos", [P, S])
        sin = m.sb("sin", [P, S])
        kst = m.sb("kst", [P, GH, S], F32R)
        qst = m.sb("qst", [P, 2, GH, CH], F32R)
        vaug = m.sb("vaug", [P, NT, GH, 2 * HD0])
        wst = m.sb("wst", [P, 3, ND, P])
        wh = m.sb("wh", [P, 3, ND, P], F32R)
        wl = m.sb("wl", [P, 3, ND, P], F32R)
        probs = m.sb("probs", [P, 2, 2, CH])
        qkf = m.sb("qkf", [P, 2, CH])
        t1 = m.sb("t1", [P, 2, CH])
        t2 = m.sb("t2", [P, 2, CH])
        hl = m.sb("hl", [P, 2, 2, CH], F32R)
        avs = m.sb("avs", [P, CH])
        osb = m.sb("osb", [P, 2, TC, 2 * HD0])
        rec = m.sb("rec", [P, TC * 2])
        ident = m.sb("ident", [P, P])
        rotf = m.sb("rotf", [P, P])
        maskf = m.sb("maskf", [P, 2, P])
        identr = m.sb("identr", [P, P], F32R)
        maskr = m.sb("maskr", [P, 2, P], F32R)
        mparts = m.sb("mparts", [P, 2, TC, NC])
        nm = m.sb("nm", [P, 2, TC])
        mt = m.sb("mt", [P, 2, TC, 98], F32R)
        xst = qkf
        sbank = m.ps("sbank", [P, 2, CH])
        stb = m.ps("stb", [P, 2, 2, CH])
        avb = m.ps("avb", [P, CH])
        misc = m.ps("misc", [P, CH])

        names = ("consts cready xhi xlo wload wsplit_hi wsplit projqk projv projr qkf_ok v_ok "
                 "t1_ok t2_ok sum_ok hi_ok lo_ok stacked unit_ok unit_max nm_ok mh_ok mt_ok turned "
                 "shifted st_ok exp_ok av_ok avs_ok avt_ok rec_ok out_ok inits mt_zero").split()
        s = {k: m.sem(k) for k in names}
        block = ctx.enter_context(nc.Block())

        @block.sync
        def _(sp):
            for dst, src in ((ident, eye), (rotf, rot), (cos, rope[0]), (sin, rope[1])):
                sp.dma_start(dst[:], src).then_inc(s["consts"], 16)
            sp.dma_start(maskf[:], masks).then_inc(s["consts"], 16)
            for i in range(ND * NC):
                if i >= 2:
                    sp.wait_ge(s["xlo"], i - 1)
                d, c = i % ND, i // ND
                sp.dma_start(xst[:, i % 2, :], xT[d * P:(d + 1) * P, c * CH:(c + 1) * CH])\
                  .then_inc(loads.sems[i % 2], 16)
            sp.wait_ge(s["inits"], 4)
            with sp.Fori(0, NG) as g:
                for ev in events:
                    if ev[0] == "split":
                        c = ev[1]
                        wait_alone(sp, s["lo_ok"], g * NC + c + 1, s["inits"], 4)
                        if c >= 2:
                            sp.wait_ge(s["st_ok"], g * NS + first_step[2 * (c - 1)])
                        for h in range(GH):
                            rows = slice(h * HD0, (h + 1) * HD0)
                            for r, (qp, kp) in enumerate(((0, 0), (0, 1), (1, 0))):
                                to = slice(r * HD0, (r + 1) * HD0)
                                sp.dma_start(f32(qst[to, c % 2, h, :]), f32(hl[rows, qp, 0, :]))\
                                  .then_inc(s["stacked"], 16)
                                sp.dma_start(f32(kst[to, h, c * CH:(c + 1) * CH]), f32(hl[rows, kp, 1, :]))\
                                  .then_inc(s["stacked"], 16)
                    elif ev[0] == "turn":
                        n = ev[1]
                        c, p = items[n]
                        sp.wait_ge(s["out_ok"], g * NI + n + 1)
                        dst = attn_out[c * CH:(c + 1) * CH,
                                       bass.ds(g * P + p * 2 * HD0, 2 * HD0)]
                        sp.dma_start(dst.rearrange("(t q) d -> q t d", q=P), osb[:, n % 2, :, :])\
                          .then_inc(stores.sems[n % 2], 16)
            for b in range(2):
                stores.wait(sp, b, NG * NI // 2)

        @block.gpsimd
        def _(pool):
            nc.gpsimd.memset(kst[96:128, :, :].bitcast(F32), 0.0).then_inc(s["inits"], 1)
            pool.wait_ge(s["inits"], 1)
            nc.gpsimd.memset(kst[96:98, :, :].bitcast(F32), 1.0).then_inc(s["inits"], 1)
            pool.wait_ge(s["inits"], 2)
            nc.gpsimd.memset(qst[96:128, :, :, :].bitcast(F32), 0.0).then_inc(s["inits"], 1)
            pool.wait_ge(s["inits"], 3)
            nc.gpsimd.memset(vaug[:, :, :, HD0:2 * HD0], 1.0).then_inc(s["inits"], 1)

            def split_weights(g):
                wait_alone(pool, s["wload"], g * 16 + 16, s["wload"], 16)
                nc.gpsimd.tensor_copy(wh[:], wst[:]).then_inc(s["wsplit_hi"], 1)
                pool.wait_ge(s["wsplit_hi"], g + 1)
                nc.gpsimd.tensor_tensor(wl[:], wst[:], f32(wh[:]), ALU.subtract).then_inc(s["wsplit"], 1)

            def body(g, more):
                if more:
                    pool.wait_ge(s["wsplit"], g + 1)
                    pool.dma_start(wst[:], wqkv[bass.ds(g + 1, 1)].rearrange("o p a d n -> (o p) a d n"))\
                        .then_inc(s["wload"], 16)
                for c in range(NC):
                    pool.wait_ge(s["qkf_ok"], g * NC + c + 1)
                    if c > 0:
                        pool.wait_ge(s["lo_ok"], g * NC + c)
                    nc.gpsimd.tensor_tensor(
                        t1[:], qkf[:], cos[:, c * CH:(c + 1) * CH].unsqueeze(1).broadcast_to([P, 2, CH]),
                        ALU.mult).then_inc(s["t1_ok"], 1)
                if more:
                    pool.wait_ge(s["projv"], (g + 1) * NC)
                    split_weights(g + 1)

            pool.dma_start(wst[:], wqkv[0]).then_inc(s["wload"], 16)
            split_weights(0)
            with pool.Fori(0, NG - 1) as g:
                body(g, True)
            body(NG - 1, False)

        @block.scalar
        def _(act):
            act.wait_ge(s["consts"], 80)
            nc.scalar.activation(identr[:], ident[:], ACT.Copy).then_inc(s["cready"], 1)
            nc.scalar.activation(maskr[:], maskf[:], ACT.Copy).then_inc(s["cready"], 1)
            for i in range(ND * NC):
                d, c = i % ND, i // ND
                loads.wait(act, i % 2, i // 2 + 1)
                nc.scalar.activation(xh[:, d, c * CH:(c + 1) * CH], xst[:, i % 2, :], ACT.Copy)\
                    .then_inc(s["xhi"], 1)
            act.wait_ge(s["xlo"], ND * NC)
            act.wait_ge(s["inits"], 4)
            with act.Fori(0, NG) as g:
                for ev in events:
                    if ev[0] == "proj":
                        c = ev[1]
                        act.wait_ge(s["projqk"], g * NC + c + 1)
                        nc.scalar.activation(qkf[:], stb[:, 0, :, :], ACT.Copy).then_inc(s["qkf_ok"], 1)
                        act.wait_ge(s["projv"], g * NC + c + 1)
                        nc.scalar.activation(
                            vaug[:, c * TC:(c + 1) * TC, :, 0:HD0],
                            misc[:].rearrange("p (t h d) -> p t h d", t=TC, h=GH), ACT.Copy)\
                            .then_inc(s["v_ok"], 1)
                    elif ev[0] == "split":
                        c = ev[1]
                        act.wait_ge(s["sum_ok"], g * NC + c + 1)
                        if c > 0:
                            act.wait_ge(s["stacked"], (g * NC + c) * NDMA * 16)
                        nc.scalar.activation(hl[:, 0, :, :], t1[:], ACT.Copy).then_inc(s["hi_ok"], 1)
                    elif ev[0] == "shift":
                        n = ev[1]
                        c, p = items[n]
                        for h in range(2):
                            act.wait_ge(s["turned"], g * 2 * NI + 2 * n + h + 1)
                            nc.scalar.activation(qst[96:98, c % 2, 2 * p + h, :], sbank[96:98, h, :],
                                                 ACT.Copy).then_inc(s["shifted"], 1)
                    elif ev[0] == "step":
                        i = ev[2]
                        c, p, kt = steps[i]
                        w0 = max(0, kt - TC * c) * P
                        act.wait_ge(s["st_ok"], g * NS + i + 1)
                        if i >= 2:
                            act.wait_ge(s["av_ok"], g * NS + i - 1)
                        nc.scalar.activation(probs[:, i % 2, :, w0:], stb[:, i % 2, :, w0:], ACT.Exp,
                                             scale=SCALE0).then_inc(s["exp_ok"], 1)
                    elif ev[0] == "out":
                        n = ev[1]
                        act.wait_ge(s["av_ok"], g * NS + first_step[n] + TC * (items[n][0] + 1))
                        nc.scalar.activation(avs[:], avb[:], ACT.Copy).then_inc(s["avs_ok"], 1)

        @block.vector
        def _(dve):
            dve.wait_ge(s["consts"], 80)
            for i in range(ND * NC):
                d, c = i % ND, i // ND
                dve.wait_ge(s["xhi"], i + 1)
                nc.vector.tensor_tensor(xl[:, d, c * CH:(c + 1) * CH], xst[:, i % 2, :],
                                        f32(xh[:, d, c * CH:(c + 1) * CH]), ALU.subtract)\
                    .then_inc(s["xlo"], 1)
            nc.vector.memset(mt[:].bitcast(F32), 0.0).then_inc(s["mt_zero"], 1)
            dve.wait_ge(s["mt_zero"], 1)
            with dve.Fori(0, NG) as g:
                for ev in events:
                    if ev[0] == "proj":
                        c = ev[1]
                        dve.wait_ge(s["projr"], g * NC + c + 1)
                        nc.vector.tensor_tensor(
                            t2[:], stb[:, 1, :, :],
                            sin[:, c * CH:(c + 1) * CH].unsqueeze(1).broadcast_to([P, 2, CH]),
                            ALU.mult).then_inc(s["t2_ok"], 1)
                        dve.wait_ge(s["t2_ok"], g * NC + c + 1)
                        dve.wait_ge(s["t1_ok"], g * NC + c + 1)
                        nc.vector.tensor_tensor(t1[:], t1[:], t2[:], ALU.add).then_inc(s["sum_ok"], 1)
                    elif ev[0] == "split":
                        c = ev[1]
                        dve.wait_ge(s["hi_ok"], g * NC + c + 1)
                        nc.vector.tensor_tensor(hl[:, 1, :, :], t1[:], f32(hl[:, 0, :, :]),
                                                ALU.subtract).then_inc(s["lo_ok"], 1)
                    elif ev[0] == "unit":
                        n, i = ev[1:]
                        c, _ = items[n]
                        h, t, u = units[n][i]
                        w = CH if u < c else (t + 1) * P
                        k = first_unit[n] + i
                        dve.wait_ge(s["unit_ok"], g * NU + k + 1)
                        nc.vector.reduce_max(mparts[:, h, t, u:u + 1], sbank[:, i % 2, 0:w], AX)\
                            .then_inc(s["unit_max"], 1)
                    elif ev[0] == "max":
                        n = ev[1]
                        c, _ = items[n]
                        dve.wait_ge(s["unit_max"], g * NU + first_unit[n] + len(units[n]))
                        nc.vector.tensor_reduce(nm[:], mparts[:, :, :, 0:c + 1], AX, ALU.max,
                                                negate=True).then_inc(s["nm_ok"], 1)
                        dve.wait_ge(s["nm_ok"], g * NI + n + 1)
                        if n > 0:
                            dve.wait_ge(s["turned"], g * 2 * NI + 2 * n)
                        nc.vector.tensor_copy(mt[:, :, :, 96], nm[:]).then_inc(s["mh_ok"], 1)
                        dve.wait_ge(s["mh_ok"], g * NI + n + 1)
                        nc.vector.tensor_tensor(mt[:, :, :, 97], nm[:], f32(mt[:, :, :, 96]),
                                                ALU.subtract).then_inc(s["mt_ok"], 1)
                    elif ev[0] == "turn":
                        n = ev[1]
                        tv = misc[:].rearrange("p (a b) -> p a b", b=2 * HD0)
                        dve.wait_ge(s["avt_ok"], g * NI + n + 1)
                        nc.vector.reciprocal(rec[:], tv[:, :, HD0]).then_inc(s["rec_ok"], 1)
                        dve.wait_ge(s["rec_ok"], g * NI + n + 1)
                        if n >= 2:
                            stores.wait(dve, n % 2, g * (NI // 2) + n // 2)
                        nc.vector.tensor_tensor(
                            osb[:, n % 2, :, :].rearrange("p t (h d) -> p (t h) d", h=2),
                            tv[:, :, 0:HD0],
                            rec[:].unsqueeze(2).broadcast_to([P, TC * 2, HD0]),
                            ALU.mult).then_inc(s["out_ok"], 1)
                for b in range(2):
                    stores.wait(dve, b, (g + 1) * (NI // 2))

        @block.tensor
        def _(pe):
            pe.wait_ge(s["cready"], 2)
            pe.wait_ge(s["xlo"], ND * NC)
            pe.wait_ge(s["inits"], 4)
            pe.wait_ge(s["mt_zero"], 1)

            def values(g, i):
                c, p, kt = steps[i]
                w0 = max(0, kt - TC * c) * P
                pe.wait_ge(s["exp_ok"], g * NS + i + 1)
                if kt == 0:
                    pe.wait_ge(s["v_ok"], g * NC + c + 1)
                    n = 2 * c + p
                    if n > 0:
                        pe.wait_ge(s["avs_ok"], g * NI + n)
                for h in range(2):
                    last = nc.tensor.matmul(avb[64 * h:64 * h + 64, w0:], vaug[:, kt, 2 * p + h, :],
                                            probs[:, i % 2, h, w0:], start=kt == 0,
                                            stop=kt == TC * (c + 1) - 1, tile_position=(0, 64 * h),
                                            skip_group_check=True)
                last.then_inc(s["av_ok"], 1)

            with pe.Fori(0, NG) as g:
                for ev in events:
                    if ev[0] == "proj":
                        c = ev[1]
                        cs = slice(c * CH, (c + 1) * CH)
                        if c == 0:
                            pe.wait_ge(s["wsplit"], g + 1)
                        elif c >= 2:
                            pe.wait_ge(s["exp_ok"], g * NS + first_step[2 * (c - 1)])
                        for a in range(2):
                            for d in range(ND):
                                last = mm3(nc, stb[:, 0, a, :], wh[:, a, d, :], wl[:, a, d, :],
                                           xh[:, d, cs], xl[:, d, cs], d == 0, d == ND - 1)
                        last.then_inc(s["projqk"], 1)
                        if c >= 2:
                            pe.wait_ge(s["out_ok"], g * NI + 2 * (c - 1) - 1)
                        for t in range(TC):
                            ts = slice(c * CH + t * P, c * CH + (t + 1) * P)
                            for d in range(ND):
                                last = mm3(nc, misc[:, t * P:(t + 1) * P], xh[:, d, ts], xl[:, d, ts],
                                           wh[:, 2, d, :], wl[:, 2, d, :], d == 0, d == ND - 1)
                        last.then_inc(s["projv"], 1)
                        pe.wait_ge(s["qkf_ok"], g * NC + c + 1)
                        for a in range(2):
                            last = nc.tensor.matmul(stb[:, 1, a, :], rotf[:], qkf[:, a, :],
                                                    start=True, stop=True)
                        last.then_inc(s["projr"], 1)
                    elif ev[0] == "unit":
                        n, i = ev[1:]
                        c, p = items[n]
                        h, t, u = units[n][i]
                        w = CH if u < c else (t + 1) * P
                        k = first_unit[n] + i
                        if i == 0 and p == 0:
                            pe.wait_ge(s["stacked"], (g * NC + c + 1) * NDMA * 16)
                        if i >= 2:
                            pe.wait_ge(s["unit_max"], g * NU + k - 1)
                        last = nc.tensor.matmul(sbank[:, i % 2, 0:w],
                                                qst[0:96, c % 2, 2 * p + h, t * P:(t + 1) * P],
                                                kst[0:96, 2 * p + h, u * CH:u * CH + w],
                                                start=True, stop=u < c)
                        if u == c:
                            last = nc.tensor.matmul(sbank[:, i % 2, t * P:w], identr[:], maskr[:, 0, :],
                                                    start=False, stop=True)
                        last.then_inc(s["unit_ok"], 1)
                    elif ev[0] == "shift":
                        n = ev[1]
                        pe.wait_ge(s["mt_ok"], g * NI + n + 1)
                        for h in range(2):
                            for t in range(TC):
                                last = nc.tensor.transpose(sbank[0:98, h, t * P:(t + 1) * P],
                                                           f32(mt[:, h, t, :]), ident[:])
                            last.then_inc(s["turned"], 1)
                    elif ev[0] == "step":
                        n, i = ev[1:]
                        c, p, kt = steps[i]
                        w0 = max(0, kt - TC * c) * P
                        if kt == 0:
                            pe.wait_ge(s["shifted"], g * 2 * NI + 2 * n + 2)
                            if p == 0:
                                pe.wait_ge(s["t2_ok"], g * NC + min(c + 2, NC))
                        if i >= 2:
                            pe.wait_ge(s["exp_ok"], g * NS + i - 1)
                        for h in range(2):
                            last = nc.tensor.matmul(stb[:, i % 2, h, w0:],
                                                    kst[:, 2 * p + h, kt * P:(kt + 1) * P],
                                                    qst[:, c % 2, 2 * p + h, w0:],
                                                    start=True, stop=kt < TC * c)
                            if kt >= TC * c:
                                last = nc.tensor.matmul(stb[:, i % 2, h, w0:w0 + P], identr[:],
                                                        maskr[:, 1, :], start=False, stop=True)
                        last.then_inc(s["st_ok"], 1)
                        if i > 0:
                            values(g, i - 1)
                    elif ev[0] == "flush":
                        values(g, NS - 1)
                    elif ev[0] == "turn":
                        n = ev[1]
                        pe.wait_ge(s["avs_ok"], g * NI + n + 1)
                        pe.wait_ge(s["v_ok"], g * NC + min((n + 1) // 2 + 2, NC))
                        if n > 0:
                            pe.wait_ge(s["out_ok"], g * NI + n)
                        for t in range(TC):
                            last = nc.tensor.transpose(misc[:, t * P:(t + 1) * P],
                                                       avs[:, t * P:(t + 1) * P], ident[:])
                        last.then_inc(s["avt_ok"], 1)
                pe.wait_ge(s["out_ok"], (g + 1) * NI)


class Norm:
    def __init__(self, nc, ctx):
        m = Mem(nc, ctx, "norm")
        self.nc, self.before = nc, 0
        self.stats = m.sb("stats", [P, TC, 6])
        self.mv = m.sb("mv", [P, TC, 2])
        self.std = m.sb("std", [P, TC])
        self.rstd = m.sb("rstd", [P, TC])
        self.eps = m.sb("eps", [P, 1])
        self.eps_ok, self.stats_ok, self.mv_ok, self.std_ok, self.rstd_ok, self.done = (
            m.sem(x) for x in ("eps_ok", "stats_ok", "mv_ok", "std_ok", "rstd_ok", "norm_done"))

    def init(self, dve):
        self.nc.vector.memset(self.eps[:], EPS).then_inc(self.eps_ok, 1)
        dve.wait_ge(self.eps_ok, 1)

    def stage_over(self):
        self.before += NT

    def mean_and_var(self, dve, src, t, k):
        self.nc.vector.bn_stats(self.stats[:, t, :], src).then_inc(self.stats_ok, 1)
        wait_alone(dve, self.stats_ok, self.before + k + 1, self.eps_ok, 1)
        self.nc.vector.bn_aggr(self.mv[:, t, :], self.stats[:, t, :]).then_inc(self.mv_ok, 1)

    def root(self, act, t, k):
        act.wait_ge(self.mv_ok, self.before + k + 1)
        self.nc.scalar.activation(self.std[:, t:t + 1], self.mv[:, t, 1:2], ACT.Sqrt,
                                  bias=self.eps[:]).then_inc(self.std_ok, 1)

    def apply(self, dve, dst, src, t, k):
        dve.wait_ge(self.std_ok, self.before + k + 1)
        self.nc.vector.reciprocal(self.rstd[:, t:t + 1], self.std[:, t:t + 1]).then_inc(self.rstd_ok, 1)
        dve.wait_ge(self.rstd_ok, self.before + k + 1)
        self.nc.vector.tensor_scalar(dst, src, self.mv[:, t, 0:1], self.rstd[:, t:t + 1],
                                     ALU.subtract, ALU.mult).then_inc(self.done, 1)

    def wait(self, eng, k):
        eng.wait_ge(self.done, self.before + k)


def layer0_project(nc, nrm, loads, loads2, x_in, attn_out, wo, gate_w, bias, lower, eye, X, xh, xl, weights_t):
    with ExitStack() as ctx:
        m = Mem(nc, ctx, "p0")
        wst = m.sb("wst", [P, ND, D])
        woh = m.sb("woh", [P, ND, D], F32R)
        wol = m.sb("wol", [P, ND, D], F32R)
        gst = m.sb("gst", [P, ND, NE])
        gh = m.sb("gh", [P, ND, NE], F32R)
        gl = m.sb("gl", [P, ND, NE], F32R)
        ident = m.sb("ident", [P, P])
        low = m.sb("low", [P, NE * NE])
        brow = m.sb("brow", [P, NE])
        oin = m.sb("oin", [P, TC, D])
        xin = m.sb("xin", [P, TC, D])
        oth = m.sb("oth", [P, 2, ND, P], F32R)
        otl = m.sb("otl", [P, 2, ND, P], F32R)
        y = m.sb("y", [P, TC, D])
        xn = m.sb("xn", [P, TC, D])
        gsb = m.sb("gsb", [NE, CH])
        sig = m.sb("sig", [P, TC, NE])
        val = m.sb("val", [P, TC, NE])
        gt = m.sb("gt", [P, TC, NE * NE])
        eq = m.sb("eq", [P, TC, NE * NE])
        rank = m.sb("rank", [P, TC, NE])
        sm = m.sb("sm", [P, TC, NE])
        smt = m.sb("smt", [NE, CH])
        ta = m.ps("ta", [P, 2, ND * P])
        yb = m.ps("yb", [P, 2, D])
        tb = m.ps("tb", [P, 2, ND * P])
        gb = m.ps("gb", [P, CH])
        sb8 = m.ps("sb8", [P, CH])
        names = ("consts w_hi w_lo ot_ok oh_ok ol_ok y_ok sum_ok xt_ok xh_ok xl_ok copied "
                 "g_ok gsb_ok gt_ok sig_ok val_ok cmp_ok eqm_ok add_ok rank_ok sm_ok smt_ok smts_ok stored").split()
        s = {k: m.sem(k) for k in names}
        block = ctx.enter_context(nc.Block())
        order = [("o", 0)]
        for t in range(TC):
            order += [("o", t + 1)] * (t + 1 < TC) + [("w", t)] + [("b", t - 1)] * (t > 0)
        order.append(("b", TC - 1))

        @block.sync
        def _(sp):
            sp.dma_start(wst[:], wo).then_inc(s["consts"], 16)
            sp.dma_start(gst[:], gate_w).then_inc(s["consts"], 16)
            sp.dma_start(ident[:], eye).then_inc(s["consts"], 16)
            sp.dma_start(low[:], lower.partition_broadcast(P)).then_inc(s["consts"], 16)
            sp.dma_start(brow[:], bias.partition_broadcast(P)).then_inc(s["consts"], 16)

            def body(c, first):
                for t in range(TC):
                    rows = bass.ds(c * CH + t * P, P)
                    if not first:
                        sp.wait_ge(s["ot_ok"], c * TC - TC + t + 1)
                    sp.dma_start(oin[:, t, :], attn_out[rows, :]).then_inc(loads.sems[t], 16)
                    if not first:
                        sp.wait_ge(s["sum_ok"], c * TC - TC + t + 1)
                    sp.dma_start(xin[:, t, :], x_in[rows, :]).then_inc(loads2.sems[t], 16)

            def store(c):
                sp.wait_ge(s["smts_ok"], c + 1)
                sp.dma_start(weights_t[:, bass.ds(c * CH, CH)], smt[:]).then_inc(s["stored"], 16)

            body(0, True)
            with sp.Fori(1, NC) as c:
                body(c, False)
                store(c - 1)
            store(NC - 1)
            sp.wait_ge(s["stored"], 16 * NC)

        @block.gpsimd
        def _(pool):
            pool.wait_ge(s["consts"], 80)
            nc.gpsimd.tensor_copy(woh[:], wst[:]).then_inc(s["w_hi"], 1)
            nc.gpsimd.tensor_copy(gh[:], gst[:]).then_inc(s["w_hi"], 1)
            pool.wait_ge(s["w_hi"], 2)
            nc.gpsimd.tensor_tensor(wol[:], wst[:], f32(woh[:]), ALU.subtract).then_inc(s["w_lo"], 1)
            nc.gpsimd.tensor_tensor(gl[:], gst[:], f32(gh[:]), ALU.subtract).then_inc(s["w_lo"], 1)
            with pool.Fori(0, NC) as c:
                for t in range(TC):
                    nrm.wait(pool, c * TC + t + 1)
                    nc.gpsimd.tensor_copy(X[:, bass.ds(c * TC + t, 1), :], xn[:, t:t + 1, :])\
                        .then_inc(s["copied"], 1)

        @block.scalar
        def _(act):
            with act.Fori(0, NC) as c:
                for kind, t in order:
                    k = c * TC + t
                    if kind == "o":
                        act.wait_ge(s["ot_ok"], k + 1)
                        if t >= 2:
                            act.wait_ge(s["y_ok"], k - 1)
                        nc.scalar.activation(oth[:, t % 2, :, :].rearrange("p d t -> p (d t)"),
                                             ta[:, t % 2, :], ACT.Copy).then_inc(s["oh_ok"], 1)
                    elif kind == "w":
                        nrm.root(act, t, k)
                    else:
                        act.wait_ge(s["xt_ok"], k + 1)
                        nc.scalar.activation(xh[:, :, bass.ds(c * CH + t * P, P)],
                                             tb[:, t % 2, :].rearrange("p (d t) -> p d t", d=ND),
                                             ACT.Copy).then_inc(s["xh_ok"], 1)
                act.wait_ge(s["g_ok"], c + 1)
                nc.scalar.activation(gsb[:], gb[0:NE, :], ACT.Copy).then_inc(s["gsb_ok"], 1)
                act.wait_ge(s["gt_ok"], c + 1)
                nc.scalar.activation(sig[:].rearrange("p t e -> p (t e)"), sb8[:, 0:TC * NE],
                                     ACT.Sigmoid).then_inc(s["sig_ok"], 1)
                act.wait_ge(s["smt_ok"], c + 1)
                nc.scalar.activation(smt[:], gb[0:NE, :], ACT.Copy).then_inc(s["smts_ok"], 1)
                act.wait_ge(s["stored"], (c + 1) * 16)

        @block.vector
        def _(dve):
            nrm.init(dve)
            dve.wait_ge(s["consts"], 80)
            with dve.Fori(0, NC) as c:
                for kind, t in order:
                    k = c * TC + t
                    if kind == "o":
                        dve.wait_ge(s["oh_ok"], k + 1)
                        nc.vector.tensor_tensor(
                            otl[:, t % 2, :, :].rearrange("p d t -> p (d t)"), ta[:, t % 2, :],
                            f32(oth[:, t % 2, :, :]).rearrange("p d t -> p (d t)"),
                            ALU.subtract).then_inc(s["ol_ok"], 1)
                    elif kind == "w":
                        dve.wait_ge(s["y_ok"], k + 1)
                        loads2.wait(dve, t, c + 1)
                        nc.vector.tensor_tensor(y[:, t, :], yb[:, t % 2, :], xin[:, t, :], ALU.add)\
                            .then_inc(s["sum_ok"], 1)
                        dve.wait_ge(s["sum_ok"], k + 1)
                        nrm.mean_and_var(dve, y[:, t, :], t, k)
                        nrm.apply(dve, xn[:, t, :], y[:, t, :], t, k)
                    else:
                        dve.wait_ge(s["xh_ok"], k + 1)
                        nc.vector.tensor_tensor(
                            xl[:, :, bass.ds(c * CH + t * P, P)],
                            tb[:, t % 2, :].rearrange("p (d t) -> p d t", d=ND),
                            f32(xh[:, :, bass.ds(c * CH + t * P, P)]), ALU.subtract)\
                            .then_inc(s["xl_ok"], 1)
                dve.wait_ge(s["sig_ok"], c + 1)
                nc.vector.tensor_tensor(val[:], sig[:], brow[:].unsqueeze(1).broadcast_to([P, TC, NE]),
                                        ALU.add).then_inc(s["val_ok"], 1)
                dve.wait_ge(s["val_ok"], c + 1)
                other = val[:].unsqueeze(2).broadcast_to([P, TC, NE, NE])
                own = val[:].unsqueeze(3).broadcast_to([P, TC, NE, NE])
                g4 = gt[:].rearrange("p t (a b) -> p t a b", a=NE)
                e4 = eq[:].rearrange("p t (a b) -> p t a b", a=NE)
                nc.vector.tensor_tensor(g4, other, own, ALU.is_gt).then_inc(s["cmp_ok"], 1)
                nc.vector.tensor_tensor(e4, other, own, ALU.is_equal).then_inc(s["cmp_ok"], 1)
                dve.wait_ge(s["cmp_ok"], 2 * c + 2)
                nc.vector.tensor_tensor(eq[:], eq[:], low[:].unsqueeze(1).broadcast_to([P, TC, NE * NE]),
                                        ALU.mult).then_inc(s["eqm_ok"], 1)
                dve.wait_ge(s["eqm_ok"], c + 1)
                nc.vector.tensor_tensor(gt[:], gt[:], eq[:], ALU.add).then_inc(s["add_ok"], 1)
                dve.wait_ge(s["add_ok"], c + 1)
                nc.vector.tensor_reduce(rank[:], g4, AX, ALU.add).then_inc(s["rank_ok"], 1)
                dve.wait_ge(s["rank_ok"], c + 1)
                nc.vector.scalar_tensor_tensor(out=sm[:], in0=rank[:], scalar=2.0, in1=sig[:],
                                               op0=ALU.is_lt, op1=ALU.mult).then_inc(s["sm_ok"], 1)
                dve.wait_ge(s["copied"], (c + 1) * TC)

        @block.tensor
        def _(pe):
            pe.wait_ge(s["consts"], 80)
            pe.wait_ge(s["w_lo"], 2)
            with pe.Fori(0, NC) as c:
                for kind, t in order:
                    k = c * TC + t
                    if kind == "o":
                        loads.wait(pe, t, c + 1)
                        if t >= 2:
                            pe.wait_ge(s["ol_ok"], k - 1)
                        for d in range(ND):
                            last = nc.tensor.transpose(ta[:, t % 2, d * P:(d + 1) * P],
                                                       oin[:, t, d * P:(d + 1) * P], ident[:])
                        last.then_inc(s["ot_ok"], 1)
                    elif kind == "w":
                        pe.wait_ge(s["ol_ok"], k + 1)
                        if t >= 2:
                            pe.wait_ge(s["sum_ok"], k - 1)
                        for d in range(ND):
                            last = mm3(nc, yb[:, t % 2, :], oth[:, t % 2, d, :], otl[:, t % 2, d, :],
                                       woh[:, d, :], wol[:, d, :], d == 0, d == ND - 1)
                        last.then_inc(s["y_ok"], 1)
                    else:
                        nrm.wait(pe, k + 1)
                        if t >= 2:
                            pe.wait_ge(s["xl_ok"], k - 1)
                        for d in range(ND):
                            last = nc.tensor.transpose(tb[:, t % 2, d * P:(d + 1) * P],
                                                       xn[:, t, d * P:(d + 1) * P], ident[:])
                        last.then_inc(s["xt_ok"], 1)
                pe.wait_ge(s["xl_ok"], c * TC + TC)
                for d in range(ND):
                    cols = bass.ds(c * CH, CH)
                    last = mm3(nc, gb[0:NE, :], gh[:, d, :], gl[:, d, :], xh[:, d, cols], xl[:, d, cols],
                               d == 0, d == ND - 1)
                last.then_inc(s["g_ok"], 1)
                wait_alone(pe, s["gsb_ok"], c + 1, s["consts"], 80)
                for t in range(TC):
                    last = nc.tensor.transpose(sb8[:, t * NE:(t + 1) * NE], gsb[:, t * P:(t + 1) * P],
                                               ident[0:NE, 0:NE])
                last.then_inc(s["gt_ok"], 1)
                pe.wait_ge(s["sm_ok"], c + 1)
                for t in range(TC):
                    last = nc.tensor.transpose(gb[0:NE, t * P:(t + 1) * P], sm[:, t, :], ident[:])
                last.then_inc(s["smt_ok"], 1)
                pe.wait_ge(s["smts_ok"], c + 1)


def layer0_experts(nc, loads2, w_exp, weights_t, X, xh, xl):
    with ExitStack() as ctx:
        m = Mem(nc, ctx, "e0")
        wst = m.sb("wst", [P, EW])
        wh = m.sb("wh", [P, 2, EW], F32R)
        wl = m.sb("wl", [P, 2, EW], F32R)
        sbc = m.sb("sbc", [P, 2, S])
        sa = m.sb("sa", [P, CH])
        sg = m.sb("sg", [P, CH])
        sbb = m.sb("sbb", [P, CH])
        h = m.sb("h", [P, CH])
        hh = m.sb("hh", [P, 2, NJ, CH], F32R)
        hl = m.sb("hl", [P, 2, NJ, CH], F32R)
        ab = m.ps("ab", [P, 2, 2, CH])
        yb = m.ps("yb", [P, 4, D])
        names = ("wload wsplit_hi wsplit ab_ok sa_ok sg_ok sbb_ok h_ok hh_ok hl_ok y_ok acc_ok").split()
        s = {k: m.sem(k) for k in names}
        block = ctx.enter_context(nc.Block())
        NCH = NC * NJ

        def w13(w, b, which, d, j):
            at = (which * ND + d) * HID + j * P
            return w[:, b, at:at + P]

        def w2(w, b, j):
            at = 2 * ND * HID + j * D
            return w[:, b, at:at + D]

        def order(r):
            ev = []
            q = [(e, c) for e in range(r) for c in range(NC)]
            for i, (e, c) in enumerate(q):
                for j in range(NJ):
                    ev.append(("up", e, c, j))
                    if i > 0:
                        ev.append(("down", *q[i - 1], j))
            return ev + [("down", *q[-1], j) for j in range(NJ)]

        def each(eng, work):
            work(0, 1, True)
            with eng.Fori(0, NE // 2) as i:
                work(i * 2 + 1, 2, False)

        @block.gpsimd
        def _(pool):
            def load(e):
                pool.dma_start(wst[:], w_exp[bass.ds(e, 1)].rearrange("o p n -> (o p) n"))\
                    .then_inc(s["wload"], 16)

            def split(e, half):
                wait_alone(pool, s["wload"], e * 16 + 16, s["wload"], 16)
                nc.gpsimd.tensor_copy(wh[:, half, :], wst[:]).then_inc(s["wsplit_hi"], 1)
                pool.wait_ge(s["wsplit_hi"], e + 1)
                nc.gpsimd.tensor_tensor(wl[:, half, :], wst[:], f32(wh[:, half, :]), ALU.subtract)\
                    .then_inc(s["wsplit"], 1)
                pool.wait_ge(s["wsplit"], e + 1)

            load(0)
            split(0, 0)
            load(1)
            split(1, 1)
            load(2)

            def body(i, more):
                pool.wait_ge(s["y_ok"], (i * 2 + 1) * NC * TC)
                split(i * 2 + 2, 0)
                if more:
                    load(i * 2 + 3)
                    pool.wait_ge(s["y_ok"], (i * 2 + 2) * NC * TC)
                    split(i * 2 + 3, 1)
                    load(i * 2 + 4)

            with pool.Fori(0, NE // 2 - 1) as i:
                body(i, True)
            body(NE // 2 - 1, False)

        @block.sync
        def _(sp):
            def load(e, half):
                row = weights_t[bass.ds(e - 1, 1), :].rearrange("o n -> (o n)")
                sp.dma_start(sbc[:, half, :], row.partition_broadcast(P))\
                    .then_inc(loads2.sems[half], 16)

            load(1, 0)
            load(2, 1)
            with sp.Fori(0, NE // 2 - 1) as i:
                sp.wait_ge(s["h_ok"], (i * 2 + 2) * NCH)
                load(i * 2 + 3, 0)
                sp.wait_ge(s["h_ok"], (i * 2 + 3) * NCH)
                load(i * 2 + 4, 1)

        @block.scalar
        def _(act):
            def work(e0, r, shared):
                for ev, e, c, j in order(r):
                    if ev != "up":
                        continue
                    u = c * NJ + j + e * NCH
                    act.wait_ge(s["ab_ok" if shared else "sa_ok"], e0 * NCH + u + 1 - (0 if shared else NCH))
                    if not (shared and u == 0):
                        act.wait_ge(s["h_ok"], e0 * NCH + u)
                    nc.scalar.activation(sg[:], ab[:, u % 2, 0, :] if shared else sa[:], ACT.Silu)\
                        .then_inc(s["sg_ok"], 1)
                    act.wait_ge(s["h_ok"], e0 * NCH + u + 1)
                    if not (shared and c < 2):
                        act.wait_ge(s["y_ok"], ((e0 + e) * NC + c - 1) * TC)
                    nc.scalar.activation(hh[:, c % 2, j, :], h[:], ACT.Copy).then_inc(s["hh_ok"], 1)
            each(act, work)

        @block.vector
        def _(dve):
            def work(e0, r, shared):
                for ev, e, c, j in order(r):
                    u = c * NJ + j + e * NCH
                    k = e0 * NCH + u
                    if ev == "up":
                        cs = slice(c * CH, (c + 1) * CH)
                        if shared:
                            dve.wait_ge(s["sg_ok"], k + 1)
                            if u > 0:
                                dve.wait_ge(s["hl_ok"], k)
                            nc.vector.tensor_tensor(h[:], sg[:], ab[:, u % 2, 1, :], ALU.mult)\
                                .then_inc(s["h_ok"], 1)
                            dve.wait_ge(s["hh_ok"], k + 1)
                            nc.vector.tensor_tensor(hl[:, c % 2, j, :], h[:], f32(hh[:, c % 2, j, :]),
                                                    ALU.subtract).then_inc(s["hl_ok"], 1)
                            continue
                        dve.wait_ge(s["ab_ok"], k + 1)
                        loads2.wait_turn(dve, e % 2, e0 + e - 1)
                        nc.vector.tensor_tensor(sa[:], ab[:, u % 2, 0, :], sbc[:, e % 2, cs], ALU.mult)\
                            .then_inc(s["sa_ok"], 1)
                        nc.vector.tensor_tensor(sbb[:], ab[:, u % 2, 1, :], sbc[:, e % 2, cs], ALU.mult)\
                            .then_inc(s["sbb_ok"], 1)
                        dve.wait_ge(s["hl_ok"], k)
                        dve.wait_ge(s["sbb_ok"], k + 1 - NCH)
                        dve.wait_ge(s["sg_ok"], k + 1)
                        nc.vector.tensor_tensor(h[:], sg[:], sbb[:], ALU.mult).then_inc(s["h_ok"], 1)
                        dve.wait_ge(s["hh_ok"], k + 1)
                        nc.vector.tensor_tensor(hl[:, c % 2, j, :], h[:], f32(hh[:, c % 2, j, :]),
                                                ALU.subtract).then_inc(s["hl_ok"], 1)
                    else:
                        for t in (2 * j, 2 * j + 1):
                            dve.wait_ge(s["y_ok"], ((e0 + e) * NC + c) * TC + t + 1)
                            nc.vector.tensor_tensor(X[:, c * TC + t, :], X[:, c * TC + t, :], yb[:, t, :],
                                                    ALU.add).then_inc(s["acc_ok"], 1)
            each(dve, work)

        @block.tensor
        def _(pe):
            def work(e0, r, shared):
                for ev, e, c, j in order(r):
                    u = c * NJ + j + e * NCH
                    half = 0 if shared else (e + 1) % 2
                    k = e0 * NCH + u
                    if ev == "up":
                        if c == 0 and j == 0:
                            pe.wait_ge(s["wsplit"], e0 + e + 1)
                        if not (shared and u < 2):
                            pe.wait_ge(s["h_ok"], k - 1)
                        cs = slice(c * CH, (c + 1) * CH)
                        for which in range(2):
                            for d in range(ND):
                                last = mm3(nc, ab[:, u % 2, which, :], w13(wh, half, which, d, j),
                                           w13(wl, half, which, d, j), xh[:, d, cs], xl[:, d, cs],
                                           d == 0, d == ND - 1)
                        last.then_inc(s["ab_ok"], 1)
                    else:
                        pe.wait_ge(s["hl_ok"], (e0 + e) * NCH + (c + 1) * NJ)
                        for t in (2 * j, 2 * j + 1):
                            if not (shared and c == 0):
                                pe.wait_ge(s["acc_ok"], ((e0 + e) * NC + c - 1) * TC + t + 1)
                            for i in range(NJ):
                                last = mm3(nc, yb[:, t, :], hh[:, c % 2, i, t * P:(t + 1) * P],
                                           hl[:, c % 2, i, t * P:(t + 1) * P], w2(wh, half, i),
                                           w2(wl, half, i), i == 0, i == NJ - 1)
                            last.then_inc(s["y_ok"], 1)
            each(pe, work)


def layer1_qkv(nc, nrm, w_qkv, qk_bias, v_bias, rope, rot, eye, X, kth, ktl, x2, q_dram, v_dram):
    with ExitStack() as ctx:
        m = Mem(nc, ctx, "q1")
        wst = m.sb("wst", [P, D])
        wh = m.sb("wh", [P, 3, ND, D], F32R)
        wl = m.sb("wl", [P, 3, ND, D], F32R)
        xch = m.sb("xch", [P, ND, CH], F32R)
        xcl = m.sb("xcl", [P, ND, CH], F32R)
        xn = m.sb("xn", [P, TC, D])
        cs = m.sb("cs", [P, 2, CH])
        ident = m.sb("ident", [P, P])
        rotf = m.sb("rotf", [P, P])
        bqk = m.sb("bqk", [P, 2, ND])
        bv = m.sb("bv", [P, D])
        qkf = m.sb("qkf", [P, 2, CH])
        t1 = m.sb("t1", [P, 2, CH])
        t2 = m.sb("t2", [P, 2, CH])
        vf, vhl = t2[:, 0, :], m.sb("vhl", [P, 2, D], F32R)
        qhl = m.sb("qhl", [P, 2, CH], F32R)
        qk = m.ps("qk", [P, 2, CH])
        rb = m.ps("rb", [P, 2, CH])
        vb = m.ps("vb", [P, 2, D])
        tb = m.ps("tb", [P, 2, ND * P])
        names = ("consts wload whi wlo csload xt_ok xh_ok xl_ok qk_ok qkf_ok r_ok t1_ok t2_ok sum_ok hi_ok "
                 "lo_ok v_ok vf_ok vh_ok vl_ok qstore vstore xstore").split()
        s = {k: m.sem(k) for k in names}
        block = ctx.enter_context(nc.Block())
        NW = 3 * ND

        @block.sync
        def _(sp):
            for dst, src in ((ident[:], eye), (rotf[:], rot), (bqk[:], qk_bias),
                             (bv[:], v_bias.partition_broadcast(P))):
                sp.dma_start(dst, src).then_inc(s["consts"], 16)
            sp.dma_start(cs[:], rope[:, :, 0:CH].rearrange("a p n -> p a n")).then_inc(s["csload"], 16)
            for i in range(NW):
                if i > 0:
                    sp.wait_ge(s["wlo"], i)
                sp.dma_start(wst[:], w_qkv[i // ND, :, i % ND, :]).then_inc(s["wload"], 16)

            def body(c, more):
                for t in range(TC):
                    nrm.wait(sp, c * TC + t + 1)
                    sp.dma_start(x2[bass.ds(c * CH + t * P, P), :], xn[:, t, :]).then_inc(s["xstore"], 16)
                for j in range(ND):
                    wait_alone(sp, s["lo_ok"], c * ND + j + 1, s["consts"], 16)
                    sp.dma_start(q_dram[:, :, j, bass.ds(c * CH, CH)].rearrange("a p n -> p a n"),
                                 f32(qhl[:])).then_inc(s["qstore"], 16)
                if more:
                    sp.dma_start(cs[:], rope[:, :, bass.ds((c + 1) * CH, CH)].rearrange("a p n -> p a n"))\
                        .then_inc(s["csload"], 16)
                for t in range(TC):
                    sp.wait_ge(s["vl_ok"], c * TC + t + 1)
                    sp.dma_start(v_dram[:, :, bass.ds(c * TC + t, 1), :]
                                 .rearrange("a p o n -> p a (o n)"), f32(vhl[:])).then_inc(s["vstore"], 16)

            with sp.Fori(0, NC - 1) as c:
                body(c, True)
            body(NC - 1, False)
            sp.wait_ge(s["qstore"], 16 * NC * ND)
            sp.wait_ge(s["vstore"], 16 * NC * TC)
            sp.wait_ge(s["xstore"], 16 * NC * TC)

        @block.gpsimd
        def _(pool):
            for i in range(NW):
                pool.wait_ge(s["wload"], 16 * i + 16)
                nc.gpsimd.tensor_copy(wh[:, i // ND, i % ND, :], wst[:]).then_inc(s["whi"], 1)
                pool.wait_ge(s["whi"], i + 1)
                nc.gpsimd.tensor_tensor(wl[:, i // ND, i % ND, :], wst[:], f32(wh[:, i // ND, i % ND, :]),
                                        ALU.subtract).then_inc(s["wlo"], 1)
            with pool.Fori(0, NC) as c:
                for j in range(ND):
                    k = c * ND + j
                    pool.wait_ge(s["qkf_ok"], k + 1)
                    pool.wait_ge(s["csload"], 16 * c + 16)
                    if j > 0:
                        pool.wait_ge(s["lo_ok"], k)
                    nc.gpsimd.tensor_tensor(t1[:], qkf[:], cs[:, 0, :].unsqueeze(1).broadcast_to([P, 2, CH]),
                                            ALU.mult).then_inc(s["t1_ok"], 1)

        @block.scalar
        def _(act):
            act.wait_ge(s["consts"], 64)
            with act.Fori(0, NC) as c:
                for t in range(TC):
                    nrm.root(act, t, c * TC + t)
                for t in range(TC):
                    act.wait_ge(s["xt_ok"], c * TC + t + 1)
                    nc.scalar.activation(xch[:, :, t * P:(t + 1) * P],
                                         tb[:, t % 2, :].rearrange("p (d t) -> p d t", d=ND),
                                         ACT.Copy).then_inc(s["xh_ok"], 1)

                def evict(j):
                    act.wait_ge(s["qk_ok"], c * ND + j + 1)
                    if j > 0:
                        act.wait_ge(s["sum_ok"], c * ND + j)
                    for a in range(2):
                        last = nc.scalar.activation(qkf[:, a, :], qk[:, a, :], ACT.Identity,
                                                    bias=bqk[:, a, j:j + 1])
                    last.then_inc(s["qkf_ok"], 1)

                for j in range(ND):
                    evict(j)
                    act.wait_ge(s["sum_ok"], c * ND + j + 1)
                    if j > 0:
                        act.wait_ge(s["qstore"], 16 * (c * ND + j))
                    nc.scalar.activation(qhl[:, 0, :], t1[:, 0, :], ACT.Copy)
                    nc.scalar.activation(kth[:, j, bass.ds(c * CH, CH)], t1[:, 1, :], ACT.Copy)\
                        .then_inc(s["hi_ok"], 1)
                for t in range(TC):
                    act.wait_ge(s["vf_ok"], c * TC + t + 1)
                    if t > 0:
                        act.wait_ge(s["vstore"], 16 * (c * TC + t))
                    nc.scalar.activation(vhl[:, 0, :], vf, ACT.Copy).then_inc(s["vh_ok"], 1)
                act.wait_ge(s["qstore"], 16 * (c + 1) * ND)
                act.wait_ge(s["vstore"], 16 * (c + 1) * TC)

        @block.vector
        def _(dve):
            dve.wait_ge(s["consts"], 64)
            with dve.Fori(0, NC) as c:
                for t in range(TC):
                    nrm.mean_and_var(dve, X[:, bass.ds(c * TC + t, 1), :].rearrange("p o n -> p (o n)"), t,
                                c * TC + t)
                for t in range(TC):
                    nrm.apply(dve, xn[:, t, :], X[:, bass.ds(c * TC + t, 1), :]
                              .rearrange("p o n -> p (o n)"), t, c * TC + t)
                for t in range(TC):
                    dve.wait_ge(s["xh_ok"], c * TC + t + 1)
                    nc.vector.tensor_tensor(xcl[:, :, t * P:(t + 1) * P],
                                            tb[:, t % 2, :].rearrange("p (d t) -> p d t", d=ND),
                                            f32(xch[:, :, t * P:(t + 1) * P]), ALU.subtract)\
                        .then_inc(s["xl_ok"], 1)
                dve.wait_ge(s["csload"], 16 * c + 16)
                for j in range(ND):
                    k = c * ND + j
                    dve.wait_ge(s["r_ok"], k + 1)
                    nc.vector.tensor_tensor(t2[:], rb[:], cs[:, 1, :].unsqueeze(1).broadcast_to([P, 2, CH]),
                                            ALU.mult).then_inc(s["t2_ok"], 1)
                    dve.wait_ge(s["t2_ok"], k + 1)
                    dve.wait_ge(s["t1_ok"], k + 1)
                    nc.vector.tensor_tensor(t1[:], t1[:], t2[:], ALU.add).then_inc(s["sum_ok"], 1)
                    dve.wait_ge(s["hi_ok"], k + 1)
                    nc.vector.tensor_tensor(qhl[:, 1, :], t1[:, 0, :], f32(qhl[:, 0, :]), ALU.subtract)
                    nc.vector.tensor_tensor(ktl[:, j, bass.ds(c * CH, CH)], t1[:, 1, :],
                                            f32(kth[:, j, bass.ds(c * CH, CH)]), ALU.subtract)\
                        .then_inc(s["lo_ok"], 1)
                for t in range(TC):
                    k = c * TC + t
                    dve.wait_ge(s["v_ok"], k + 1)
                    if t > 0:
                        dve.wait_ge(s["vl_ok"], k)
                    nc.vector.tensor_tensor(vf, vb[:, t % 2, :], bv[:], ALU.add).then_inc(s["vf_ok"], 1)
                    dve.wait_ge(s["vh_ok"], k + 1)
                    nc.vector.tensor_tensor(vhl[:, 1, :], vf, f32(vhl[:, 0, :]), ALU.subtract)\
                        .then_inc(s["vl_ok"], 1)
                dve.wait_ge(s["vl_ok"], (c + 1) * TC)
                dve.wait_ge(s["xstore"], 16 * (c + 1) * TC)

        @block.tensor
        def _(pe):
            pe.wait_ge(s["consts"], 64)
            with pe.Fori(0, NC) as c:
                for t in range(TC):
                    nrm.wait(pe, c * TC + t + 1)
                    if t >= 2:
                        pe.wait_ge(s["xl_ok"], c * TC + t - 1)
                    for d in range(ND):
                        last = nc.tensor.transpose(tb[:, t % 2, d * P:(d + 1) * P],
                                                   xn[:, t, d * P:(d + 1) * P], ident[:])
                    last.then_inc(s["xt_ok"], 1)
                pe.wait_ge(s["xl_ok"], (c + 1) * TC)
                pe.wait_ge(s["wlo"], NW)

                def rotate(j):
                    pe.wait_ge(s["qkf_ok"], c * ND + j + 1)
                    if j > 0:
                        pe.wait_ge(s["t2_ok"], c * ND + j)
                    for a in range(2):
                        last = nc.tensor.matmul(rb[:, a, :], rotf[:], qkf[:, a, :], start=True, stop=True)
                    last.then_inc(s["r_ok"], 1)

                def value(t):
                    if t >= 2:
                        pe.wait_ge(s["vf_ok"], c * TC + t - 1)
                    for d in range(ND):
                        last = mm3(nc, vb[:, t % 2, :], xch[:, d, t * P:(t + 1) * P],
                                   xcl[:, d, t * P:(t + 1) * P], wh[:, 2, d, :], wl[:, 2, d, :],
                                   d == 0, d == ND - 1)
                    last.then_inc(s["v_ok"], 1)

                for j in range(ND):
                    if j > 0:
                        pe.wait_ge(s["qkf_ok"], c * ND + j)
                    for a in range(2):
                        for d in range(ND):
                            last = mm3(nc, qk[:, a, :], wh[:, a, d, j * P:(j + 1) * P],
                                       wl[:, a, d, j * P:(j + 1) * P], xch[:, d, :], xcl[:, d, :],
                                       d == 0, d == ND - 1)
                    last.then_inc(s["qk_ok"], 1)
                    rotate(j)
                for t in range(TC):
                    value(t)


def layer1_attention(nc, loads, loads2, stores, wo, eye, kth, ktl, x2, q_dram, v_dram, y_dram):
    with ExitStack() as ctx:
        m = Mem(nc, ctx, "a1")
        vh = m.sb("vh", [P, NT, D], F32R)
        vl = m.sb("vl", [P, NT, D], F32R)
        woh = m.sb("woh", [P, ND, D], F32R)
        wol = m.sb("wol", [P, ND, D], F32R)
        q = m.sb("q", [P, 2, 2, ND, P], F32R)
        pr = m.sb("pr", [P, S])
        pth = m.sb("pth", [P, NT, P], F32R)
        ptl = m.sb("ptl", [P, NT, P], F32R)
        xin = m.sb("xin", [P, 2, D])
        ident = m.sb("ident", [P, P])
        nm = m.sb("nm", [P, 1])
        bias = m.sb("bias", [P, 1])
        rsum = m.sb("rsum", [P, 1])
        rinv = m.sb("rinv", [P, 1])
        o = m.sb("o", [P, D])
        oth = m.sb("oth", [P, ND, P], F32R)
        otl = m.sb("otl", [P, ND, P], F32R)
        y = m.sb("y", [P, 2, D])
        wst = pr
        sc = m.ps("sc", [P, S])
        tb = m.ps("tb", [P, 2, 4 * P])
        av = m.ps("av", [P, D])
        yb = m.ps("yb", [P, D])
        names = ("consts vload w_hi w_lo s_ok nm_ok bias_ok exp_ok rinv_ok pt_ok ph_ok pl_ok "
                 "av_ok o_ok ot_ok oh_ok ol_ok y_ok sum_ok").split()
        s = {k: m.sem(k) for k in names}
        block = ctx.enter_context(nc.Block())

        def loop(eng, tile):
            with eng.Fori(0, NT // 2 - 1) as i:
                tile(i * 2, 0, False)
                tile(i * 2 + 1, 1, False)
            tile(NT - 2, 0, False)
            tile(NT - 1, 1, True)

        @block.sync
        def _(sp):
            sp.dma_start(ident[:], eye).then_inc(s["consts"], 16)
            sp.dma_start(wst[:], wo.rearrange("p a n -> p (a n)")).then_inc(s["consts"], 16)

            def load(n, r):
                cols = bass.ds(n * P, P)
                for a in range(2):
                    sp.dma_start(f32(q[:, r, a, :, :]), q_dram[a, :, :, cols])\
                        .then_inc(loads.sems[r], 16)

            load(0, 0)
            load(1, 1)
            for a, dst in ((0, vh), (1, vl)):
                for c in range(NC):
                    ts = slice(c * TC, (c + 1) * TC)
                    sp.dma_start(f32(dst[:, ts, :]), v_dram[a, :, ts, :]).then_inc(s["vload"], 16)
            sp.dma_start(xin[:, 0, :], x2[0:P, :]).then_inc(loads2.sems[0], 16)

            def store(n, r):
                sp.wait_ge(s["sum_ok"], n + 1)
                sp.dma_start(y_dram[bass.ds(n * P, P), :], y[:, r, :]).then_inc(stores.sems[r], 16)

            def tile(n, r, first, more):
                if more:
                    sp.wait_ge(s["s_ok"], n + 1)
                    load(n + 2, r)
                if not first:
                    store(n - 1, 1 - r)
                sp.dma_start(xin[:, 1 - r, :], x2[bass.ds((n + 1) * P, P), :])\
                  .then_inc(loads2.sems[1 - r], 16)

            tile(0, 0, True, True)
            tile(1, 1, False, True)
            with sp.Fori(1, NT // 2 - 1) as i:
                tile(i * 2, 0, False, True)
                tile(i * 2 + 1, 1, False, True)
            tile(NT - 2, 0, False, False)
            store(NT - 2, 0)
            store(NT - 1, 1)
            for r in range(2):
                stores.wait(sp, r, NT // 2)

        @block.gpsimd
        def _(pool):
            pool.wait_ge(s["consts"], 32)
            flat = "p d n -> p (d n)"
            nc.gpsimd.tensor_copy(woh[:].rearrange(flat), wst[:]).then_inc(s["w_hi"], 1)
            pool.wait_ge(s["w_hi"], 1)
            nc.gpsimd.tensor_tensor(wol[:].rearrange(flat), wst[:], f32(woh[:]).rearrange(flat),
                                    ALU.subtract).then_inc(s["w_lo"], 1)

        def exps(act, n):
            act.wait_ge(s["bias_ok"], n + 1)
            nc.scalar.activation(pr[:], sc[:], ACT.Exp, bias=bias[:], scale=SCALE1,
                                 accum_out=rsum[:]).then_inc(s["exp_ok"], 1)

        @block.scalar
        def _(act):
            act.wait_ge(s["w_lo"], 1)
            exps(act, 0)

            def tile(n, r, last):
                hi_out(n, r, act)
                for g in range(4):
                    act.wait_ge(s["pt_ok"], n * 4 + g + 1)
                    nc.scalar.activation(pth[:, 4 * g:4 * g + 4, :].rearrange("p a b -> p (a b)"),
                                         tb[:, (g + 1) % 2, :], ACT.Copy).then_inc(s["ph_ok"], 1)
                if not last:
                    exps(act, n + 1)

            def hi_out(n, r, act):
                act.wait_ge(s["ot_ok"], n)
                nc.scalar.activation(oth[:].rearrange("p a b -> p (a b)"), tb[:, 0, :], ACT.Copy)\
                    .then_inc(s["oh_ok"], 1)

            def first(n, r, last):
                for g in range(4):
                    act.wait_ge(s["pt_ok"], n * 4 + g + 1)
                    nc.scalar.activation(pth[:, 4 * g:4 * g + 4, :].rearrange("p a b -> p (a b)"),
                                         tb[:, (g + 1) % 2, :], ACT.Copy).then_inc(s["ph_ok"], 1)
                exps(act, n + 1)

            first(0, 0, False)
            tile(1, 1, False)
            with act.Fori(1, NT // 2 - 1) as i:
                tile(i * 2, 0, False)
                tile(i * 2 + 1, 1, False)
            tile(NT - 2, 0, False)
            tile(NT - 1, 1, True)
            hi_out(NT, 0, act)

        @block.vector
        def _(dve):
            def peak(n):
                dve.wait_ge(s["s_ok"], n + 1)
                nc.vector.tensor_reduce(nm[:], sc[:], AX, ALU.max, negate=True).then_inc(s["nm_ok"], 1)
                dve.wait_ge(s["nm_ok"], n + 1)
                nc.vector.tensor_scalar(bias[:], nm[:], SCALE1, None, ALU.mult).then_inc(s["bias_ok"], 1)

            def lo_out(n):
                dve.wait_ge(s["oh_ok"], n)
                nc.vector.tensor_tensor(otl[:].rearrange("p a b -> p (a b)"), tb[:, 0, :],
                                        f32(oth[:]).rearrange("p a b -> p (a b)"), ALU.subtract)\
                    .then_inc(s["ol_ok"], 1)

            def add(n, r, first):
                dve.wait_ge(s["y_ok"], n + 1)
                loads2.wait_turn(dve, r, n)
                if not first:
                    stores.wait_turn(dve, r, n - 2)
                nc.vector.tensor_tensor(y[:, r, :], yb[:], xin[:, r, :], ALU.add).then_inc(s["sum_ok"], 1)

            def tile(n, r, last, no=99):
                if no > 0:
                    lo_out(n)
                for g in range(4):
                    dve.wait_ge(s["ph_ok"], n * 4 + g + 1)
                    nc.vector.tensor_tensor(ptl[:, 4 * g:4 * g + 4, :].rearrange("p a b -> p (a b)"),
                                            tb[:, (g + 1) % 2, :],
                                            f32(pth[:, 4 * g:4 * g + 4, :]).rearrange("p a b -> p (a b)"),
                                            ALU.subtract).then_inc(s["pl_ok"], 1)
                    if g == 2 and no > 0:
                        add(n - 1, 1 - r, no < 3)
                dve.wait_ge(s["exp_ok"], n + 1)
                nc.vector.reciprocal(rinv[:], rsum[:]).then_inc(s["rinv_ok"], 1)
                if not last:
                    dve.wait_ge(s["rinv_ok"], n + 1)
                    peak(n + 1)
                dve.wait_ge(s["rinv_ok"], n + 1)
                dve.wait_ge(s["av_ok"], n + 1)
                nc.vector.tensor_scalar(o[:], av[:], rinv[:], None, ALU.mult).then_inc(s["o_ok"], 1)

            peak(0)
            tile(0, 0, False, 0)
            tile(1, 1, False, 1)
            tile(2, 0, False, 2)
            tile(3, 1, False, 3)
            with dve.Fori(2, NT // 2 - 1) as i:
                tile(i * 2, 0, False)
                tile(i * 2 + 1, 1, False)
            tile(NT - 2, 0, False)
            tile(NT - 1, 1, True)
            lo_out(NT)
            add(NT - 1, 1, False)

        @block.tensor
        def _(pe):
            pe.wait_ge(s["consts"], 32)

            def scores(n, r, b):
                ks = slice(b * CH, (b + 1) * CH)
                if b == 0:
                    loads.wait_turn(pe, r, n, 2)
                for d in range(ND):
                    last = mm3(nc, sc[:, ks], q[:, r, 0, d, :], q[:, r, 1, d, :], kth[:, d, ks],
                               ktl[:, d, ks], d == 0, d == ND - 1)
                if b == 3:
                    last.then_inc(s["s_ok"], 1)

            def turn_out(n):
                pe.wait_ge(s["o_ok"], n)
                for d in range(ND):
                    last = nc.tensor.transpose(tb[:, 0, d * P:(d + 1) * P], o[:, d * P:(d + 1) * P], ident[:])
                last.then_inc(s["ot_ok"], 1)

            def project(n, no=99):
                pe.wait_ge(s["ol_ok"], n)
                if no > 1:
                    pe.wait_ge(s["sum_ok"], n - 1)
                for d in range(ND):
                    last = mm3(nc, yb[:], oth[:, d, :], otl[:, d, :], woh[:, d, :], wol[:, d, :],
                               d == 0, d == ND - 1)
                last.then_inc(s["y_ok"], 1)

            def tile(n, r, last, no=99):
                pe.wait_ge(s["exp_ok"], n + 1)
                for b in range(4):
                    if b == 0 and no > 0:
                        pe.wait_ge(s["pl_ok"], 4 * n)
                        turn_out(n)
                    if not last:
                        scores(n + 1, 1 - r, b)
                    if b == 1 and no > 0:
                        pe.wait_ge(s["ol_ok"], n)
                    if b >= 2:
                        pe.wait_ge(s["pl_ok"], 4 * n + b - 1)
                    for a in range(4):
                        kt = 4 * b + a
                        end = nc.tensor.transpose(tb[:, (b + 1) % 2, a * P:(a + 1) * P],
                                                  pr[:, kt * P:(kt + 1) * P], ident[:])
                    end.then_inc(s["pt_ok"], 1)
                    if b == 2 and no > 0:
                        project(n, no)
                if no == 0:
                    pe.wait_ge(s["vload"], 16 * 2 * NC)
                for kt in range(NT):
                    if kt % 4 == 0:
                        pe.wait_ge(s["pl_ok"], 4 * n + kt // 4 + 1)
                    end = mm3(nc, av[:], pth[:, kt, :], ptl[:, kt, :], vh[:, kt, :], vl[:, kt, :],
                              kt == 0, kt == NT - 1)
                end.then_inc(s["av_ok"], 1)

            pe.wait_ge(s["w_lo"], 1)
            for b in range(4):
                scores(0, 0, b)
            tile(0, 0, False, 0)
            tile(1, 1, False, 1)
            with pe.Fori(1, NT // 2 - 1) as i:
                tile(i * 2, 0, False)
                tile(i * 2 + 1, 1, False)
            tile(NT - 2, 0, False)
            tile(NT - 1, 1, True)
            turn_out(NT)
            project(NT)


def layer1_norm(nc, nrm, loads, y_dram, eye, X, xh, xl):
    with ExitStack() as ctx:
        m = Mem(nc, ctx, "n1")
        ident = m.sb("ident", [P, P])
        yin = m.sb("yin", [P, TC, D])
        xn = m.sb("xn", [P, TC, D])
        tb = m.ps("tb", [P, TC, ND * P])
        names = "consts copied xt_ok xh_ok xl_ok".split()
        s = {k: m.sem(k) for k in names}
        block = ctx.enter_context(nc.Block())

        @block.sync
        def _(sp):
            sp.dma_start(ident[:], eye).then_inc(s["consts"], 16)

            def body(c, first):
                for t in range(TC):
                    if not first:
                        nrm.wait(sp, c * TC - TC + t + 1)
                    sp.dma_start(yin[:, t, :], y_dram[bass.ds(c * CH + t * P, P), :])\
                      .then_inc(loads.sems[t], 16)

            body(0, True)
            with sp.Fori(1, NC) as c:
                body(c, False)

        @block.gpsimd
        def _(pool):
            with pool.Fori(0, NC) as c:
                for t in range(TC):
                    nrm.wait(pool, c * TC + t + 1)
                    nc.gpsimd.tensor_copy(X[:, bass.ds(c * TC + t, 1), :], xn[:, t:t + 1, :])\
                        .then_inc(s["copied"], 1)

        @block.scalar
        def _(act):
            with act.Fori(0, NC) as c:
                for t in range(TC):
                    nrm.root(act, t, c * TC + t)
                for t in range(TC):
                    act.wait_ge(s["xt_ok"], c * TC + t + 1)
                    nc.scalar.activation(xh[:, :, bass.ds(c * CH + t * P, P)],
                                         tb[:, t, :].rearrange("p (d t) -> p d t", d=ND),
                                         ACT.Copy).then_inc(s["xh_ok"], 1)

        @block.vector
        def _(dve):
            with dve.Fori(0, NC) as c:
                for t in range(TC):
                    loads.wait(dve, t, c + 1)
                    nrm.mean_and_var(dve, yin[:, t, :], t, c * TC + t)
                for t in range(TC):
                    nrm.apply(dve, xn[:, t, :], yin[:, t, :], t, c * TC + t)
                for t in range(TC):
                    dve.wait_ge(s["xh_ok"], c * TC + t + 1)
                    nc.vector.tensor_tensor(
                        xl[:, :, bass.ds(c * CH + t * P, P)],
                        tb[:, t, :].rearrange("p (d t) -> p d t", d=ND),
                        f32(xh[:, :, bass.ds(c * CH + t * P, P)]), ALU.subtract).then_inc(s["xl_ok"], 1)
                dve.wait_ge(s["copied"], (c + 1) * TC)

        @block.tensor
        def _(pe):
            pe.wait_ge(s["consts"], 16)
            with pe.Fori(0, NC) as c:
                for t in range(TC):
                    nrm.wait(pe, c * TC + t + 1)
                    for d in range(ND):
                        last = nc.tensor.transpose(tb[:, t, d * P:(d + 1) * P],
                                                   xn[:, t, d * P:(d + 1) * P], ident[:])
                    last.then_inc(s["xt_ok"], 1)


def layer1_mlp(nc, w_gate, w_up, w_down, X, xh, xl):
    with ExitStack() as ctx:
        m = Mem(nc, ctx, "m1")
        PW = ND * P
        wst = m.sb("wst", [P, 4, PW])
        wh = m.sb("wh", [P, 3, 4, PW], F32R)
        wl = m.sb("wl", [P, 3, 4, PW], F32R)
        sg = m.sb("sg", [P, CH])
        h = m.sb("h", [P, 4, CH])
        a = m.sb("a", [P, 4, CH])
        c0 = m.sb("c0", [P, 3, CH], BF16)
        c1 = m.sb("c1", [P, 2, CH], BF16)
        c2 = m.sb("c2", [P, CH], BF16)
        k = m.sb("k", [P, 4, CH], BF16)
        hh = m.sb("hh", [P, 4, CH], F32R)
        hl = m.sb("hl", [P, 4, CH], F32R)
        gu = m.ps("gu", [P, 2, 2, CH])
        yb = m.ps("yb", [P, 4, D])
        names = ("wload whi wlo gu_ok sg_ok h_ok a_ok cmp_ok k1_ok k2_ok k_ok hs_ok hh_ok hl_ok y_ok "
                 "acc_ok").split()
        s = {n: m.sem(n) for n in names}
        block = ctx.enter_context(nc.Block())
        ev = []
        for c in range(NC):
            ev += [("up", c, 0), ("up", c, 1)] + [("down", c - 1)] * (c > 0)
            ev += [("up", c, 2), ("up", c, 3), ("pick", c)]
        ev.append(("down", NC - 1))

        @block.sync
        def _(sp):
            def load(q, which):
                src = (w_gate, w_up, w_down)[which][bass.ds(q, 1)].rearrange("o p r n -> (o p) r n")
                sp.dma_start(wst[:], src).then_inc(s["wload"], 16)

            load(0, 0)
            for i in (1, 2):
                sp.wait_ge(s["wlo"], i)
                load(0, i)
            with sp.Fori(1, NQ) as q:
                for i in range(3):
                    sp.wait_ge(s["wlo"], q * 3 + i)
                    load(q, i)

        @block.gpsimd
        def _(pool):
            def split(q, which, first):
                wait_alone(pool, s["wload"], 16 * (q * 3 + which) + 16, s["wload"], 16)
                if not first:
                    if which < 2:
                        wait_alone(pool, s["gu_ok"], q * NC * 4, s["wload"], 16)
                    else:
                        wait_alone(pool, s["y_ok"], q * NC * TC, s["wload"], 16)
                nc.gpsimd.tensor_copy(wh[:, which, :, :], wst[:]).then_inc(s["whi"], 1)
                pool.wait_ge(s["whi"], q * 3 + which + 1)
                nc.gpsimd.tensor_tensor(wl[:, which, :, :], wst[:], f32(wh[:, which, :, :]), ALU.subtract)\
                    .then_inc(s["wlo"], 1)

            for i in range(3):
                split(0, i, True)
            with pool.Fori(1, NQ) as q:
                for i in range(3):
                    split(q, i, False)

        @block.scalar
        def _(act):
            with act.Fori(0, NQ) as q:
                for e in ev:
                    c = e[1]
                    if e[0] == "up":
                        r = e[2]
                        u = c * 4 + r
                        act.wait_ge(s["gu_ok"], q * NC * 4 + u + 1)
                        if u > 0:
                            act.wait_ge(s["h_ok"], q * NC * 4 + u)
                        nc.scalar.activation(sg[:], gu[:, u % 2, 0, :], ACT.Silu).then_inc(s["sg_ok"], 1)
                    elif e[0] == "pick":
                        act.wait_ge(s["h_ok"], q * NC * 4 + (c + 1) * 4)
                        nc.scalar.activation(a[:], h[:], ACT.Abs).then_inc(s["a_ok"], 1)
                        if c > 0:
                            act.wait_ge(s["y_ok"], q * NC * TC + c * TC)
                        for r in range(4):
                            act.wait_ge(s["hs_ok"], (q * NC + c) * 4 + r + 1)
                            nc.scalar.activation(hh[:, r, :], h[:, r, :], ACT.Copy).then_inc(s["hh_ok"], 1)

        @block.vector
        def _(dve):
            tt, stt = nc.vector.tensor_tensor, nc.vector.scalar_tensor_tensor
            with dve.Fori(0, NQ) as q:
                for e in ev:
                    c = e[1]
                    i = q * NC + c
                    if e[0] == "up":
                        r = e[2]
                        if c > 0 and r == 0:
                            dve.wait_ge(s["hl_ok"], i * 4)
                        dve.wait_ge(s["sg_ok"], i * 4 + r + 1)
                        tt(h[:, r, :], sg[:], gu[:, r % 2, 1, :], ALU.mult).then_inc(s["h_ok"], 1)
                    elif e[0] == "down":
                        for t in range(TC):
                            dve.wait_ge(s["y_ok"], i * TC + t + 1)
                            tt(X[:, c * TC + t, :], X[:, c * TC + t, :], yb[:, t, :], ALU.add)\
                                .then_inc(s["acc_ok"], 1)
                    else:
                        dve.wait_ge(s["a_ok"], i + 1)
                        tt(c0[:], a[:, 1:4, :], a[:, 0:1, :].broadcast_to([P, 3, CH]), ALU.is_gt)\
                            .then_inc(s["cmp_ok"], 1)
                        tt(c1[:], a[:, 2:4, :], a[:, 1:2, :].broadcast_to([P, 2, CH]), ALU.is_gt)\
                            .then_inc(s["cmp_ok"], 1)
                        tt(c2[:], a[:, 3, :], a[:, 2, :], ALU.is_gt).then_inc(s["cmp_ok"], 1)
                        dve.wait_ge(s["cmp_ok"], 3 * i + 3)
                        tt(k[:, 0, :], c0[:, 0, :], c0[:, 1, :], ALU.add).then_inc(s["k1_ok"], 1)
                        tt(k[:, 1, :], c1[:, 0, :], c1[:, 1, :], ALU.add).then_inc(s["k1_ok"], 1)
                        tt(k[:, 2:4, :], c0[:, 1:3, :], c1[:], ALU.add).then_inc(s["k1_ok"], 1)
                        dve.wait_ge(s["k1_ok"], 3 * i + 3)
                        tt(k[:, 0, :], k[:, 0, :], c0[:, 2, :], ALU.add).then_inc(s["k2_ok"], 1)
                        tt(k[:, 1, :], k[:, 1, :], c0[:, 0, :], ALU.subtract).then_inc(s["k2_ok"], 1)
                        tt(k[:, 2, :], c2[:], k[:, 2, :], ALU.subtract).then_inc(s["k2_ok"], 1)
                        tt(k[:, 3, :], k[:, 3, :], c2[:], ALU.add).then_inc(s["k2_ok"], 1)
                        dve.wait_ge(s["k2_ok"], 4 * i + 4)
                        keep = ((ALU.is_lt, 2.0), (ALU.is_lt, 1.0), (ALU.is_lt, 0.0), (ALU.is_gt, 1.0))
                        for r, (op, than) in enumerate(keep):
                            stt(out=h[:, r, :], in0=k[:, r, :], scalar=than, in1=h[:, r, :], op0=op,
                                op1=ALU.mult).then_inc(s["hs_ok"], 1)
                        for r in range(4):
                            dve.wait_ge(s["hh_ok"], 4 * i + r + 1)
                            tt(hl[:, r, :], h[:, r, :], f32(hh[:, r, :]), ALU.subtract)\
                                .then_inc(s["hl_ok"], 1)
                dve.wait_ge(s["hl_ok"], (q + 1) * NC * 4)

        @block.tensor
        def _(pe):
            with pe.Fori(0, NQ) as q:
                for e in ev:
                    c = e[1]
                    i = q * NC + c
                    if e[0] == "up":
                        r = e[2]
                        u = c * 4 + r
                        cs = slice(c * CH, (c + 1) * CH)
                        if u >= 2:
                            pe.wait_ge(s["h_ok"], q * NC * 4 + u - 1)
                        for which in range(2):
                            if u == 0:
                                pe.wait_ge(s["wlo"], q * 3 + which + 1)
                            for d in range(ND):
                                last = mm3(nc, gu[:, u % 2, which, :], wh[:, which, r, d * P:(d + 1) * P],
                                           wl[:, which, r, d * P:(d + 1) * P], xh[:, d, cs], xl[:, d, cs],
                                           d == 0, d == ND - 1)
                        last.then_inc(s["gu_ok"], 1)
                    elif e[0] == "down":
                        pe.wait_ge(s["hl_ok"], (i + 1) * 4)
                        if c == 0:
                            pe.wait_ge(s["wlo"], q * 3 + 3)
                        for t in range(TC):
                            if c > 0:
                                pe.wait_ge(s["acc_ok"], (i - 1) * TC + t + 1)
                            for r in range(4):
                                ts = slice(t * P, (t + 1) * P)
                                last = mm3(nc, yb[:, t, :], hh[:, r, ts], hl[:, r, ts], wh[:, 2, r, :],
                                           wl[:, 2, r, :], r == 0, r == 3)
                            last.then_inc(s["y_ok"], 1)
                pe.wait_ge(s["acc_ok"], (q + 1) * NC * TC)


def final_norm(nc, nrm, stores, X, out):
    with ExitStack() as ctx:
        m = Mem(nc, ctx, "fn")
        xo = m.sb("xo", [P, TC, D])
        block = ctx.enter_context(nc.Block())

        @block.sync
        def _(sp):
            with sp.Fori(0, NC) as c:
                for t in range(TC):
                    nrm.wait(sp, c * TC + t + 1)
                    sp.dma_start(out[bass.ds(c * CH + t * P, P), :], xo[:, t, :])\
                      .then_inc(stores.sems[t], 16)
            for t in range(TC):
                stores.wait(sp, t, NC)

        @block.scalar
        def _(act):
            with act.Fori(0, NC) as c:
                for t in range(TC):
                    nrm.root(act, t, c * TC + t)

        @block.vector
        def _(dve):

            def body(c, first):
                rows = [X[:, bass.ds(c * TC + t, 1), :].rearrange("p o n -> p (o n)") for t in range(TC)]
                for t in range(TC):
                    nrm.mean_and_var(dve, rows[t], t, c * TC + t)
                for t in range(TC):
                    if not first:
                        stores.wait(dve, t, c)
                    nrm.apply(dve, xo[:, t, :], rows[t], t, c * TC + t)

            body(0, True)
            with dve.Fori(1, NC) as c:
                body(c, False)


_INPUTS = ("xT x wqkv0 rope0 rot0 eye masks wo0 gate_w gate_bias lower w_exp wqkv1 qk_bias v_bias rope1 "
           "rot1 wo1 w_gate w_up w_down").split()


def build(nc, ins, out):
    def dram(name, shape):
        return nc.dram_tensor(name, shape, F32).ap()

    attn_out = dram("attn_out", (S, D))
    weights_t = dram("weights_t", (NE, S))
    x2, y_dram = dram("x2", (S, D)), dram("y1", (S, D))
    q_dram = dram("q1", (2, P, ND, S))
    v_dram = dram("v1", (2, P, NT, D))
    with ExitStack() as ctx:
        nrm = Norm(nc, ctx)
        loads, loads2, stores = Ring(nc, "loads"), Ring(nc, "loads2"), Ring(nc, "stores")
        layer0_attention(nc, loads, stores, ins["xT"], ins["wqkv0"], ins["rope0"], ins["rot0"],
                         ins["eye"], ins["masks"], attn_out)
        loads.stage_over(2, ND * NC // 2)
        stores.stage_over(2, H0 // 2 * NC // 2)
        hi = ctx.enter_context(nc.sbuf_tensor("hi", [P, ND, S], F32R))
        lo = ctx.enter_context(nc.sbuf_tensor("lo", [P, ND, S], F32R))
        with nc.sbuf_tensor("X", [P, NT, D], F32) as X:
            layer0_project(nc, nrm, loads, loads2, ins["x"], attn_out, ins["wo0"], ins["gate_w"],
                           ins["gate_bias"], ins["lower"], ins["eye"], X, hi, lo, weights_t)
            nrm.stage_over()
            loads.stage_over(TC, NC)
            loads2.stage_over(TC, NC)
            layer0_experts(nc, loads2, ins["w_exp"], weights_t, X, hi, lo)
            loads2.stage_over(2, NE // 2)
            layer1_qkv(nc, nrm, ins["wqkv1"], ins["qk_bias"], ins["v_bias"], ins["rope1"], ins["rot1"],
                       ins["eye"], X, hi, lo, x2, q_dram, v_dram)
            nrm.stage_over()
        layer1_attention(nc, loads, loads2, stores, ins["wo1"], ins["eye"], hi, lo, x2, q_dram, v_dram,
                         y_dram)
        loads.stage_over(2, NT)
        loads2.stage_over(2, NT // 2)
        stores.stage_over(2, NT // 2)
        with nc.sbuf_tensor("X1", [P, NT, D], F32) as X:
            layer1_norm(nc, nrm, loads, y_dram, ins["eye"], X, hi, lo)
            nrm.stage_over()
            layer1_mlp(nc, ins["w_gate"], ins["w_up"], ins["w_down"], X, hi, lo)
            final_norm(nc, nrm, stores, X, out)


def rotary(dims, freqs, base_rows):
    import numpy as np
    f = freqs[:, None] * np.arange(S, dtype=np.float32)[None, :]
    cos, sin = np.ones((P, S), np.float32), np.zeros((P, S), np.float32)
    swap = np.zeros((P, P), np.float32)
    for b in base_rows:
        for i in range(dims):
            lo, up = b + i, b + dims + i
            cos[lo], sin[lo], cos[up], sin[up] = np.cos(f[i]), np.sin(f[i]), np.cos(f[i]), np.sin(f[i])
            swap[up, lo], swap[lo, up] = -1.0, 1.0
    return np.stack([cos, sin]), swap


def layout(inputs):
    import numpy as np
    a = {k: np.asarray(v) for k, v in inputs.items()}
    x = a["L0_attn_x"].reshape(S, D)

    def turned(w, n):
        return w.T.reshape(-1, P, n).transpose(1, 0, 2)

    half = HD0 // 2
    order = np.concatenate([np.r_[h * half:(h + 1) * half, H0 * half + h * half:H0 * half + (h + 1) * half]
                            for h in range(H0)])
    q0 = np.concatenate([a["L0_attn_Wq_sem"], a["L0_attn_Wq_geo"]])[order]
    k0 = np.concatenate([a["L0_attn_Wk_sem"], a["L0_attn_Wk_geo"]])[order]
    qkv0 = np.stack([w.reshape(NG, P, ND, P).transpose(0, 3, 2, 1) for w in (q0, k0, a["L0_attn_Wv"])], 2)
    freqs0 = (1.0 / np.float32(10000.0) ** (np.arange(0, half, 2, dtype=np.float32) / np.float32(half)))
    rope0, rot0 = rotary(half // 2, freqs0.astype(np.float32), [h * HD0 + half for h in range(GH)])
    freqs1 = (1.0 / np.float32(10000.0) ** (np.arange(0, 64, dtype=np.float32) / np.float32(64)))
    rope1, rot1 = rotary(64, freqs1.astype(np.float32), [0])
    i = np.arange(P)
    hidden = i[None, :] > i[:, None]
    masks = np.stack([np.where(hidden, np.float32(BIG), np.float32(0)),
                      np.where(hidden.T, np.float32(BIG), np.float32(0))], 1).astype(np.float32)
    lower = (np.arange(NE)[None, :] < np.arange(NE)[:, None]).astype(np.float32).reshape(-1)

    def expert(w1, w3, w2):
        return np.concatenate([turned(w1, HID).reshape(P, -1), turned(w3, HID).reshape(P, -1),
                               turned(w2, D).reshape(P, -1)], 1)

    w_exp = np.stack([expert(a["L0_ffn_sw1"], a["L0_ffn_sw3"], a["L0_ffn_sw2"])] +
                     [expert(a["L0_ffn_w1"][e], a["L0_ffn_w3"][e], a["L0_ffn_w2"][e]) for e in range(NE)])
    qw, kvw = a["L1_attn_q_w"], a["L1_attn_kv_w"]
    qkv1 = np.stack([turned(w, D) for w in (qw, kvw[:D], kvw[D:])])
    kvb = a["L1_attn_kv_b"]
    qk_bias = np.stack([a["L1_attn_q_b"].reshape(ND, P).T, kvb[:D].reshape(ND, P).T], 1)

    def up(w):
        return w.reshape(ND, P, NQ, P, 4).transpose(2, 1, 4, 0, 3).reshape(NQ, P, 4, ND * P)

    down = a["L1_ffn_w_down"].reshape(NQ, P, 4, D)
    laid = dict(xT=x.T, x=x, wqkv0=qkv0, rope0=rope0, rot0=rot0, eye=np.eye(P, dtype=np.float32),
                masks=masks, wo0=turned(a["L0_attn_Wo"], D), gate_w=turned(a["L0_ffn_gate_w"], NE),
                gate_bias=a["L0_ffn_expert_bias"], lower=lower, w_exp=w_exp, wqkv1=qkv1,
                qk_bias=qk_bias, v_bias=kvb[D:], rope1=rope1, rot1=rot1, wo1=turned(a["L1_attn_o_w"], D),
                w_gate=up(a["L1_ffn_w_gate"]), w_up=up(a["L1_ffn_w_up"]), w_down=down)
    return {k: np.ascontiguousarray(v) for k, v in laid.items()}


def kernel(**inputs):
    import numpy as np
    import concourse.bacc as bacc
    from concourse.bass_utils import run_bass_kernel_spmd as run

    laid = layout(inputs)
    nc = bacc.Bacc("TRN2", target_bir_lowering=False, num_devices=1)
    ins = {n: nc.dram_tensor(f"in_{n}", laid[n].shape, mybir.dt.from_np(laid[n].dtype),
                             kind="ExternalInput").ap() for n in _INPUTS}
    out = nc.dram_tensor("out", (S, D), F32, kind="ExternalOutput").ap()
    build(nc, ins, out)
    r = run(nc, [{f"in_{n}": laid[n] for n in _INPUTS}], core_ids=[0])
    return r.results[0]["out"].reshape(1, S, D)
```

```python
import concourse.bass as bass
from concourse import mybir
from concourse.alu_op_type import AluOpType as ALU
from contextlib import ExitStack

F32 = mybir.dt.float32
F32R = mybir.dt.float32r
BF16 = mybir.dt.bfloat16
ACT = mybir.ActivationFunctionType
AX = mybir.AxisListType.X

P = 128
S = 2048
D = 512
ND = D // P
CH = 512
NC = S // CH
TC = CH // P
NT = S // P
EPS = 1e-5

H0, HD0 = 16, 32
GH = P // HD0
NG = H0 // GH
SCALE0 = float(HD0) ** -0.5
BIG = -float(2 ** 100)

NE, HID = 8, 256
NJ = HID // P
EW = ND * HID * 2 + NJ * D

SCALE1 = 128.0 ** -0.5

INTER = 2048
NQ = INTER // (4 * P)


def mm3(nc, out, wh, wl, xh, xl, start=True, stop=True):
    nc.tensor.matmul(out, wh, xh, start=start, stop=False, skip_group_check=True)
    nc.tensor.matmul(out, wh, xl, start=False, stop=False, skip_group_check=True)
    return nc.tensor.matmul(out, wl, xh, start=False, stop=stop, skip_group_check=True)


def f32(ap):
    return ap.bitcast(F32)


class Mem:

    def __init__(self, nc, ctx, stage):
        self.nc, self.ctx, self.stage = nc, ctx, stage

    def sb(self, name, shape, dt=F32):
        return self.ctx.enter_context(self.nc.sbuf_tensor(f"{self.stage}_{name}", shape, dt))

    def ps(self, name, shape):
        return self.ctx.enter_context(self.nc.psum_tensor(f"{self.stage}_{name}", shape, F32))

    def sem(self, name):
        return self.nc.alloc_semaphore(name=f"{self.stage}_{name}")


class Ring:

    def __init__(self, nc, name):
        self.sems = [nc.alloc_semaphore(name=f"{name}{i}") for i in range(TC)]
        self.before = [0] * TC

    def wait(self, eng, buf, k):
        eng.wait_ge(self.sems[buf], 16 * (self.before[buf] + k))

    def wait_turn(self, eng, buf, n, each=1):
        eng.wait_ge(self.sems[buf], 16 * self.before[buf] + 8 * each * (n - buf) + 16 * each)

    def stage_over(self, bufs, k):
        for i in range(bufs):
            self.before[i] += k


def wait_alone(eng, sem, value, held, at_least):
    if not isinstance(value, int):
        eng.compute_val(value)
    eng.wait_ge(held, at_least)
    eng.wait_ge(sem, value)


def attention0_plan():
    steps = [(c, p, kt) for c in range(NC) for p in range(2) for kt in range(TC * (c + 1))]
    items = [(c, p) for c in range(NC) for p in range(2)]
    units = [[(h, t, u) for h in range(2) for t in range(TC) for u in range(c + 1)] for c, p in items]
    first_step = [steps.index((c, p, 0)) for c, p in items]

    def proj(d, c):
        return [("queries", d, c), ("rotate", d, c), ("values", d, c), ("addrot", d, c), ("split", d, c)]

    def unit_list(d, n):
        return [("unit", d, n, i) for i in range(len(units[n]))]

    before = ([("x", 0, 0), ("x", 0, 1)] + proj(0, 0) + [("x", 0, 2)] + proj(0, 1) + [("x", 0, 3)] +
              unit_list(0, 0) + [("max", 0, 0), ("shift", 0, 0)])

    def iteration(more):
        side = [[] for _ in range(3 * len(steps))]

        def spread(work, start, stop):
            for i, ev in enumerate(work):
                side[int(3 * (start + (stop - start) * i / len(work)))].append(ev)

        def at(d, which, at_steps):
            names = ("queries", "rotate", "values", "addrot", "split") if len(at_steps) > 2 else ("max", "shift")
            for name, k in sorted(zip(names, at_steps), key=lambda x: x[1]):
                side[int(3 * k)].append((name, d, which))

        at(0, 2, (4.4, 5.4, 6.0, 6.7, 8.4))
        at(0, 3, (24.4, 25.4, 26.0, 26.7, 28.4))
        if more:
            at(1, 0, (61.4, 62.7, 69.0, 63.7, 68.4))
            at(1, 1, (70.0, 71.4, 73.0, 72.4, 79.0))
        for n, start, stop in ((1, 0, 2.7), (2, 2.7, 7.0), (3, 8.0, 14.0), (4, 14.4, 22.7), (5, 24.0, 34.0),
                               (6, 35.0, 46.4), (7, 47.0, 60.0)):
            spread(unit_list(0, n), start, stop)
            at(0, n, (stop, stop + 0.7))
        if more:
            spread(unit_list(1, 0), 75.0, 77.7)
            at(1, 0, (78.0, 78.7))
        events = []
        for k, (c, p, kt) in enumerate(steps):
            n = items.index((c, p))
            events.append(("step", 0, n, k))
            events += side[3 * k]
            if k > 0:
                events.append(("probs", 0, k - 1, 0))
            events += side[3 * k + 1]
            if k > 0:
                events.append(("probs", 0, k - 1, 1))
            if n > 0 and kt == 0:
                events.append(("out", 0, n - 1))
            if n > 0 and kt == 2:
                events.append(("turn", 0, n - 1))
            events += side[3 * k + 2]
        last = len(items) - 1
        events += [("probs", 0, len(steps) - 1, 0), ("probs", 0, len(steps) - 1, 1), ("out", 0, last)]
        return events + [("turn", 0, last)]

    return steps, items, units, first_step, before, iteration(True), iteration(False)


def layer0_attention(nc, loads, xT, wqkv, rope, rot, eye, masks, attn_out):
    steps, items, units, first_step, before, middle, final = attention0_plan()
    first_unit = [sum(len(u) for u in units[:n]) for n in range(len(items))]
    NS, NU, NI = len(steps), sum(map(len, units)), len(items)
    NDMA = 2 * 3 * 2
    QSLOT = (0, 1, 0, 2)

    with ExitStack() as ctx:
        m = Mem(nc, ctx, "a0")
        xh = m.sb("xh", [P, ND, S], F32R)
        xl = m.sb("xl", [P, ND, S], F32R)
        cos = m.sb("cos", [P, S])
        sin = m.sb("sin", [P, S])
        kst = m.sb("kst", [P, GH, S], F32R)
        qst = m.sb("qst", [P, 3, GH, CH], F32R)
        vaug = m.sb("vaug", [P, NT, GH, 2 * HD0])
        wst = m.sb("wst", [P, 3, ND, P])
        wh = m.sb("wh", [P, 3, ND, P], F32R)
        wl = m.sb("wl", [P, 3, ND, P], F32R)
        probs = m.sb("probs", [P, 2, 2, CH])
        qkf = m.sb("qkf", [P, 2, CH])
        t1 = m.sb("t1", [P, 2, CH])
        t2 = m.sb("t2", [P, 2, CH])
        hl = m.sb("hl", [P, 2, 2, CH], F32R)
        avs = m.sb("avs", [P, CH])
        osb = m.sb("osb", [P, 2, TC, 2 * HD0])
        rec = m.sb("rec", [P, TC * 2])
        rotf = m.sb("rotf", [P, P])
        identr = m.sb("identr", [P, P], F32R)
        maskr = m.sb("maskr", [P, 2, P], F32R)
        mparts = m.sb("mparts", [P, 2, 2, TC, NC])
        nm = m.sb("nm", [P, 2, TC])
        mt = m.sb("mt", [P, 2, TC, 98], F32R)
        xst = probs
        ident_in, masks_in = t2[:, 0, 0:P], t2[:, 1, 0:2 * P].rearrange("p (a n) -> p a n", a=2)
        sbank = m.ps("sbank", [P, 2, CH])
        stb = m.ps("stb", [P, 2, 2, CH])
        avb = m.ps("avb", [P, CH])
        misc = m.ps("misc", [P, CH])

        names = ("consts cready xhi xlo wload wsplit_hi wsplit projqk projv projr qkf_ok v_ok "
                 "t1_ok t2_ok sum_ok hi_ok lo_ok stacked0 stacked1 unit_ok unit_max nm_ok mh_ok mt_ok turned "
                 "shifted st_ok exp_ok av_ok avs_ok avt_ok rec_ok out_ok inits mt_zero stored0 stored1").split()
        s = {k: m.sem(k) for k in names}
        stacked = (s["stacked0"], s["stacked1"])
        stored = (s["stored0"], s["stored1"])
        block = ctx.enter_context(nc.Block())

        def groups(eng, run):
            run(0, before)
            with eng.Fori(0, NG - 1) as g:
                run(g, middle)
            run(NG - 1, final)

        @block.sync
        def _(sp):
            for i in range(ND * NC):
                if i >= 4:
                    sp.wait_ge(s["xlo"], i - 3)
                d, c = i % ND, i // ND
                sp.dma_start(xst[:, i // 2 % 2, i % 2, :], xT[d * P:(d + 1) * P, c * CH:(c + 1) * CH])\
                  .then_inc(loads.sems[i % 4], 16)

            def run(g, events):
                for ev in events:
                    gd = g + ev[1]
                    if ev[0] == "split":
                        c = ev[2]
                        wait_alone(sp, s["lo_ok"], gd * NC + c + 1, s["xlo"], 1)
                        if ev[1]:
                            sp.wait_ge(s["st_ok"], g * NS + first_step[NI - 1] + (c + 1) * TC)
                        elif c == 2:
                            sp.wait_ge(s["st_ok"], g * NS + first_step[2])
                        for h in range(GH):
                            rows = slice(h * HD0, (h + 1) * HD0)
                            for r, (qp, kp) in enumerate(((0, 0), (0, 1), (1, 0))):
                                to = slice(r * HD0, (r + 1) * HD0)
                                sp.dma_start(f32(qst[to, QSLOT[c], h, :]), f32(hl[rows, qp, 0, :]))\
                                  .then_inc(stacked[h // 2], 16)
                                sp.dma_start(f32(kst[to, h, c * CH:(c + 1) * CH]), f32(hl[rows, kp, 1, :]))\
                                  .then_inc(stacked[h // 2], 16)

            groups(sp, run)

        @block.gpsimd
        def _(pool):
            def split_weights(g):
                wait_alone(pool, s["wload"], g * 16 + 16, s["wload"], 16)
                nc.gpsimd.tensor_copy(wh[:], wst[:]).then_inc(s["wsplit_hi"], 1)
                pool.wait_ge(s["wsplit_hi"], g + 1)
                nc.gpsimd.tensor_tensor(wl[:], wst[:], f32(wh[:]), ALU.subtract).then_inc(s["wsplit"], 1)

            pool.dma_start(wst[:], wqkv[0]).then_inc(s["wload"], 16)
            split_weights(0)
            pool.wait_ge(s["wsplit"], 1)
            nc.gpsimd.memset(kst[96:128, :, :].bitcast(F32), 0.0).then_inc(s["inits"], 1)
            pool.wait_ge(s["inits"], 1)
            nc.gpsimd.memset(kst[96:98, :, :].bitcast(F32), 1.0).then_inc(s["inits"], 1)
            pool.wait_ge(s["inits"], 2)
            nc.gpsimd.memset(qst[96:128, :, :, :].bitcast(F32), 0.0).then_inc(s["inits"], 1)
            pool.wait_ge(s["inits"], 3)

            def run(g, events):
                for ev in events:
                    if ev[0] == "rotate":
                        k = (g + ev[1]) * NC + ev[2]
                        c = ev[2]
                        pool.wait_ge(s["qkf_ok"], k + 1)
                        if events is not before or c > 0:
                            pool.wait_ge(s["lo_ok"], k)
                        nc.gpsimd.tensor_tensor(
                            t1[:], qkf[:], cos[:, c * CH:(c + 1) * CH].unsqueeze(1).broadcast_to([P, 2, CH]),
                            ALU.mult).then_inc(s["t1_ok"], 1)
                        if c == NC - 1 and events is middle:
                            pool.wait_ge(s["projv"], (g + 1) * NC)
                            split_weights(g + 1)
                    elif ev[0] == "turn":
                        n = ev[2]
                        c, p = items[n]
                        pool.wait_ge(s["out_ok"], g * NI + n + 1)
                        dst = attn_out[c * CH:(c + 1) * CH,
                                       bass.ds(g * P + p * 2 * HD0, 2 * HD0)]
                        pool.dma_start(dst.rearrange("(t q) d -> q t d", q=P), osb[:, n % 2, :, :])\
                            .then_inc(stored[n % 2], 16)
                    elif ev[0] == "step" and ev[3] == 0 and events is middle:
                        pool.wait_ge(s["wsplit"], g + 1)
                        pool.dma_start(wst[:], wqkv[bass.ds(g + 1, 1)].rearrange("o p a d n -> (o p) a d n"))\
                            .then_inc(s["wload"], 16)

            pool.wait_ge(s["consts"], 80)
            groups(pool, run)
            for b in range(2):
                pool.wait_ge(stored[b], 16 * (NG * NI // 2))

        @block.scalar
        def _(act):
            for dst, src in ((ident_in, eye), (masks_in, masks), (rotf[:], rot), (cos[:], rope[0]),
                             (sin[:], rope[1])):
                act.dma_start(dst, src).then_inc(s["consts"], 16)

            def run(g, events):
                for ev in events:
                    gd = g + ev[1]
                    if ev[0] == "x":
                        c = ev[2]
                        for d in range(ND):
                            i = c * ND + d
                            loads.wait(act, i % 4, i // 4 + 1)
                            nc.scalar.activation(xh[:, d, c * CH:(c + 1) * CH], xst[:, i // 2 % 2, i % 2, :],
                                                 ACT.Copy).then_inc(s["xhi"], 1)
                    elif ev[0] == "queries":
                        c = ev[2]
                        act.wait_ge(s["projqk"], gd * NC + c + 1)
                        nc.scalar.activation(qkf[:], sbank[:], ACT.Copy).then_inc(s["qkf_ok"], 1)
                    elif ev[0] == "values":
                        c = ev[2]
                        act.wait_ge(s["projv"], gd * NC + c + 1)
                        nc.scalar.activation(
                            vaug[:, c * TC:(c + 1) * TC, :, 0:HD0],
                            misc[:].rearrange("p (t h d) -> p t h d", t=TC, h=GH), ACT.Copy)\
                            .then_inc(s["v_ok"], 1)
                    elif ev[0] == "split":
                        c = ev[2]
                        act.wait_ge(s["sum_ok"], gd * NC + c + 1)
                        if events is not before or c > 0:
                            for sem in stacked:
                                act.wait_ge(sem, (gd * NC + c) * NDMA * 16)
                        nc.scalar.activation(hl[:, 0, :, :], t1[:], ACT.Copy).then_inc(s["hi_ok"], 1)
                    elif ev[0] == "shift":
                        n = ev[2]
                        c, p = items[n]
                        if events is before:
                            act.wait_ge(s["inits"], 3)
                        for h in range(2):
                            act.wait_ge(s["turned"], gd * 2 * NI + 2 * n + h + 1)
                            nc.scalar.activation(qst[96:98, QSLOT[c], 2 * p + h, :], sbank[96:98, h, :],
                                                 ACT.Copy).then_inc(s["shifted"], 1)
                    elif ev[0] == "step":
                        i = ev[3]
                        c, p, kt = steps[i]
                        w0 = max(0, kt - TC * c) * P
                        act.wait_ge(s["st_ok"], gd * NS + i + 1)
                        if i >= 2:
                            act.wait_ge(s["av_ok"], gd * NS + i - 1)
                        nc.scalar.activation(probs[:, i % 2, :, w0:], stb[:, i % 2, :, w0:], ACT.Exp,
                                             scale=SCALE0).then_inc(s["exp_ok"], 1)
                    elif ev[0] == "out":
                        n = ev[2]
                        act.wait_ge(s["av_ok"], gd * NS + first_step[n] + TC * (items[n][0] + 1))
                        nc.scalar.activation(avs[:], avb[:], ACT.Copy).then_inc(s["avs_ok"], 1)

            act.wait_ge(s["consts"], 80)
            nc.scalar.activation(identr[:], ident_in, ACT.Copy).then_inc(s["cready"], 1)
            nc.scalar.activation(maskr[:], masks_in, ACT.Copy).then_inc(s["cready"], 1)
            groups(act, run)

        @block.vector
        def _(dve):
            nc.vector.memset(mt[:].bitcast(F32), 0.0).then_inc(s["mt_zero"], 1)
            nc.vector.memset(vaug[:, :, :, HD0:2 * HD0], 1.0).then_inc(s["mt_zero"], 1)
            dve.wait_ge(s["mt_zero"], 2)

            def run(g, events):
                for ev in events:
                    gd = g + ev[1]
                    if ev[0] == "x":
                        c = ev[2]
                        for d in range(ND):
                            i = c * ND + d
                            dve.wait_ge(s["xhi"], i + 1)
                            nc.vector.tensor_tensor(xl[:, d, c * CH:(c + 1) * CH], xst[:, i // 2 % 2, i % 2, :],
                                                    f32(xh[:, d, c * CH:(c + 1) * CH]), ALU.subtract)\
                                .then_inc(s["xlo"], 1)
                    elif ev[0] == "rotate":
                        c = ev[2]
                        if events is before and c == 0:
                            dve.wait_ge(s["cready"], 2)
                        dve.wait_ge(s["projr"], gd * NC + c + 1)
                        nc.vector.tensor_tensor(
                            t2[:], sbank[:], sin[:, c * CH:(c + 1) * CH].unsqueeze(1).broadcast_to([P, 2, CH]),
                            ALU.mult).then_inc(s["t2_ok"], 1)
                    elif ev[0] == "addrot":
                        c = ev[2]
                        dve.wait_ge(s["t2_ok"], gd * NC + c + 1)
                        dve.wait_ge(s["t1_ok"], gd * NC + c + 1)
                        nc.vector.tensor_tensor(t1[:], t1[:], t2[:], ALU.add).then_inc(s["sum_ok"], 1)
                    elif ev[0] == "split":
                        c = ev[2]
                        dve.wait_ge(s["hi_ok"], gd * NC + c + 1)
                        nc.vector.tensor_tensor(hl[:, 1, :, :], t1[:], f32(hl[:, 0, :, :]),
                                                ALU.subtract).then_inc(s["lo_ok"], 1)
                    elif ev[0] == "unit":
                        n, i = ev[2:]
                        c, _ = items[n]
                        h, t, u = units[n][i]
                        w = CH if u < c else (t + 1) * P
                        dve.wait_ge(s["unit_ok"], gd * NU + first_unit[n] + i + 1)
                        nc.vector.reduce_max(mparts[:, n % 2, h, t, u:u + 1], sbank[:, i % 2, 0:w], AX)\
                            .then_inc(s["unit_max"], 1)
                    elif ev[0] == "max":
                        n = ev[2]
                        c, _ = items[n]
                        dve.wait_ge(s["unit_max"], gd * NU + first_unit[n] + len(units[n]))
                        nc.vector.tensor_reduce(nm[:], mparts[:, n % 2, :, :, 0:c + 1], AX, ALU.max,
                                                negate=True).then_inc(s["nm_ok"], 1)
                        dve.wait_ge(s["nm_ok"], gd * NI + n + 1)
                        if events is not before:
                            dve.wait_ge(s["turned"], gd * 2 * NI + 2 * n)
                        nc.vector.tensor_copy(mt[:, :, :, 96], nm[:]).then_inc(s["mh_ok"], 1)
                        dve.wait_ge(s["mh_ok"], gd * NI + n + 1)
                        nc.vector.tensor_tensor(mt[:, :, :, 97], nm[:], f32(mt[:, :, :, 96]),
                                                ALU.subtract).then_inc(s["mt_ok"], 1)
                    elif ev[0] == "turn":
                        n = ev[2]
                        tv = misc[:].rearrange("p (a b) -> p a b", b=2 * HD0)
                        dve.wait_ge(s["avt_ok"], gd * NI + n + 1)
                        nc.vector.reciprocal(rec[:], tv[:, :, HD0]).then_inc(s["rec_ok"], 1)
                        dve.wait_ge(s["rec_ok"], gd * NI + n + 1)
                        if n >= 2:
                            dve.wait_ge(stored[n % 2], 16 * (gd * (NI // 2) + n // 2))
                        nc.vector.tensor_tensor(
                            osb[:, n % 2, :, :].rearrange("p t (h d) -> p (t h) d", h=2),
                            tv[:, :, 0:HD0],
                            rec[:].unsqueeze(2).broadcast_to([P, TC * 2, HD0]),
                            ALU.mult).then_inc(s["out_ok"], 1)
                        if n == NI - 1:
                            for b in range(2):
                                dve.wait_ge(stored[b], 16 * ((gd + 1) * (NI // 2)))

            groups(dve, run)

        @block.tensor
        def _(pe):
            def run(g, events):
                if events is before:
                    bank, values_bank = [None, None], None
                else:
                    bank = [("shifted", g * 2 * NI + 1), ("shifted", g * 2 * NI + 2)]
                    values_bank = ("v_ok", g * NC + 2)

                def free(held):
                    if held is not None:
                        pe.wait_ge(s[held[0]], held[1])

                for ev in events:
                    gd = g + ev[1]
                    if ev[0] == "queries":
                        c = ev[2]
                        cs = slice(c * CH, (c + 1) * CH)
                        if c == 0:
                            pe.wait_ge(s["wsplit"], gd + 1)
                        if events is before:
                            pe.wait_ge(s["xlo"], ND * (c + 1))
                        free(bank[0])
                        free(bank[1])
                        for a in range(2):
                            for d in range(ND):
                                last = mm3(nc, sbank[:, a, :], wh[:, a, d, :], wl[:, a, d, :],
                                           xh[:, d, cs], xl[:, d, cs], d == 0, d == ND - 1)
                        last.then_inc(s["projqk"], 1)
                        bank = [("qkf_ok", gd * NC + c + 1)] * 2
                    elif ev[0] == "values":
                        c = ev[2]
                        free(values_bank)
                        for t in range(TC):
                            ts = slice(c * CH + t * P, c * CH + (t + 1) * P)
                            for d in range(ND):
                                last = mm3(nc, misc[:, t * P:(t + 1) * P], xh[:, d, ts], xl[:, d, ts],
                                           wh[:, 2, d, :], wl[:, 2, d, :], d == 0, d == ND - 1)
                        last.then_inc(s["projv"], 1)
                        values_bank = ("v_ok", gd * NC + c + 1)
                    elif ev[0] == "rotate":
                        c = ev[2]
                        if events is before and c == 0:
                            pe.wait_ge(s["cready"], 2)
                        pe.wait_ge(s["qkf_ok"], gd * NC + c + 1)
                        free(bank[0])
                        free(bank[1])
                        for a in range(2):
                            last = nc.tensor.matmul(sbank[:, a, :], rotf[:], qkf[:, a, :],
                                                    start=True, stop=True)
                        last.then_inc(s["projr"], 1)
                        bank = [("t2_ok", gd * NC + c + 1)] * 2
                    elif ev[0] == "unit":
                        n, i = ev[2:]
                        c, p = items[n]
                        h, t, u = units[n][i]
                        w = CH if u < c else (t + 1) * P
                        k = gd * NU + first_unit[n] + i
                        if i == 0:
                            pe.wait_ge(stacked[p], (gd * NC + c + 1) * NDMA * 16)
                        free(bank[i % 2])
                        last = nc.tensor.matmul(sbank[:, i % 2, 0:w],
                                                qst[0:96, QSLOT[c], 2 * p + h, t * P:(t + 1) * P],
                                                kst[0:96, 2 * p + h, u * CH:u * CH + w],
                                                start=True, stop=u < c)
                        if u == c:
                            last = nc.tensor.matmul(sbank[:, i % 2, t * P:w], identr[:], maskr[:, 0, :],
                                                    start=False, stop=True)
                        last.then_inc(s["unit_ok"], 1)
                        bank[i % 2] = ("unit_max", k + 1)
                    elif ev[0] == "shift":
                        n = ev[2]
                        pe.wait_ge(s["mt_ok"], gd * NI + n + 1)
                        for h in range(2):
                            free(bank[h])
                            for t in range(TC):
                                last = nc.tensor.transpose(sbank[0:98, h, t * P:(t + 1) * P],
                                                           f32(mt[:, h, t, :]), f32(identr[:]))
                            last.then_inc(s["turned"], 1)
                            bank[h] = ("shifted", gd * 2 * NI + 2 * n + h + 1)
                    elif ev[0] == "step":
                        n, i = ev[2:]
                        c, p, kt = steps[i]
                        w0 = max(0, kt - TC * c) * P
                        if kt == 0:
                            pe.wait_ge(s["shifted"], gd * 2 * NI + 2 * n + 2)
                        if i >= 2:
                            pe.wait_ge(s["exp_ok"], gd * NS + i - 1)
                        for h in range(2):
                            last = nc.tensor.matmul(stb[:, i % 2, h, w0:],
                                                    kst[:, 2 * p + h, kt * P:(kt + 1) * P],
                                                    qst[:, QSLOT[c], 2 * p + h, w0:],
                                                    start=True, stop=kt < TC * c)
                            if kt >= TC * c:
                                last = nc.tensor.matmul(stb[:, i % 2, h, w0:w0 + P], identr[:],
                                                        maskr[:, 1, :], start=False, stop=True)
                        last.then_inc(s["st_ok"], 1)
                    elif ev[0] == "probs":
                        i, h = ev[2:]
                        c, p, kt = steps[i]
                        w0 = max(0, kt - TC * c) * P
                        if h == 0:
                            pe.wait_ge(s["exp_ok"], g * NS + i + 1)
                            if kt == 0:
                                pe.wait_ge(s["v_ok"], g * NC + c + 1)
                                if c + p > 0:
                                    pe.wait_ge(s["avs_ok"], g * NI + items.index((c, p)))
                        last = nc.tensor.matmul(avb[64 * h:64 * h + 64, w0:], vaug[:, kt, 2 * p + h, :],
                                                probs[:, i % 2, h, w0:], start=kt == 0,
                                                stop=kt == TC * (c + 1) - 1, tile_position=(0, 64 * h),
                                                skip_group_check=True)
                        if h == 1:
                            last.then_inc(s["av_ok"], 1)
                    elif ev[0] == "turn":
                        n = ev[2]
                        pe.wait_ge(s["avs_ok"], gd * NI + n + 1)
                        free(values_bank)
                        for t in range(TC):
                            last = nc.tensor.transpose(misc[:, t * P:(t + 1) * P],
                                                       avs[:, t * P:(t + 1) * P], f32(identr[:]))
                        last.then_inc(s["avt_ok"], 1)
                        values_bank = ("out_ok", gd * NI + n + 1)
                if events is before:
                    pe.wait_ge(s["xlo"], ND * NC)
                    pe.wait_ge(s["inits"], 3)
                    pe.wait_ge(s["mt_zero"], 2)
                else:
                    free(values_bank)

            groups(pe, run)


class Norm:
    def __init__(self, nc, ctx):
        m = Mem(nc, ctx, "norm")
        self.nc, self.before = nc, 0
        self.stats = m.sb("stats", [P, TC, 6])
        self.mv = m.sb("mv", [P, TC, 2])
        self.std = m.sb("std", [P, TC])
        self.rstd = m.sb("rstd", [P, TC])
        self.eps = m.sb("eps", [P, 1])
        self.eps_ok, self.stats_ok, self.mv_ok, self.std_ok, self.rstd_ok, self.done = (
            m.sem(x) for x in ("eps_ok", "stats_ok", "mv_ok", "std_ok", "rstd_ok", "norm_done"))

    def init(self, dve):
        self.nc.vector.memset(self.eps[:], EPS).then_inc(self.eps_ok, 1)
        dve.wait_ge(self.eps_ok, 1)

    def stage_over(self):
        self.before += NT

    def mean_and_var(self, dve, src, t, k):
        self.nc.vector.bn_stats(self.stats[:, t, :], src).then_inc(self.stats_ok, 1)
        wait_alone(dve, self.stats_ok, self.before + k + 1, self.eps_ok, 1)
        self.nc.vector.bn_aggr(self.mv[:, t, :], self.stats[:, t, :]).then_inc(self.mv_ok, 1)

    def root(self, act, t, k):
        act.wait_ge(self.mv_ok, self.before + k + 1)
        self.nc.scalar.activation(self.std[:, t:t + 1], self.mv[:, t, 1:2], ACT.Sqrt,
                                  bias=self.eps[:]).then_inc(self.std_ok, 1)

    def apply(self, dve, dst, src, t, k):
        dve.wait_ge(self.std_ok, self.before + k + 1)
        self.nc.vector.reciprocal(self.rstd[:, t:t + 1], self.std[:, t:t + 1]).then_inc(self.rstd_ok, 1)
        dve.wait_ge(self.rstd_ok, self.before + k + 1)
        self.nc.vector.tensor_scalar(dst, src, self.mv[:, t, 0:1], self.rstd[:, t:t + 1],
                                     ALU.subtract, ALU.mult).then_inc(self.done, 1)

    def wait(self, eng, k):
        eng.wait_ge(self.done, self.before + k)


def layer0_project(nc, nrm, loads, loads2, x_in, attn_out, wo, gate_w, bias, lower, eye, X, xh, xl, weights_t):
    with ExitStack() as ctx:
        m = Mem(nc, ctx, "p0")
        wst = m.sb("wst", [P, ND, D])
        woh = m.sb("woh", [P, ND, D], F32R)
        wol = m.sb("wol", [P, ND, D], F32R)
        gst = m.sb("gst", [P, ND, NE])
        gh = m.sb("gh", [P, ND, NE], F32R)
        gl = m.sb("gl", [P, ND, NE], F32R)
        ident = m.sb("ident", [P, P])
        low = m.sb("low", [P, NE * NE])
        brow = m.sb("brow", [P, NE])
        oin = m.sb("oin", [P, TC, D])
        xin = m.sb("xin", [P, TC, D])
        oth = m.sb("oth", [P, 2, ND, P], F32R)
        otl = m.sb("otl", [P, 2, ND, P], F32R)
        y = m.sb("y", [P, TC, D])
        xn = m.sb("xn", [P, TC, D])
        gsb = m.sb("gsb", [NE, CH])
        sig = m.sb("sig", [P, TC, NE])
        val = m.sb("val", [P, TC, NE])
        gt = m.sb("gt", [P, TC, NE * NE])
        eq = m.sb("eq", [P, TC, NE * NE])
        rank = m.sb("rank", [P, TC, NE])
        sm = m.sb("sm", [P, TC, NE])
        smt = m.sb("smt", [NE, CH])
        ta = m.ps("ta", [P, 2, ND * P])
        yb = m.ps("yb", [P, 2, D])
        tb = m.ps("tb", [P, 2, ND * P])
        gb = m.ps("gb", [P, CH])
        sb8 = m.ps("sb8", [P, CH])
        names = ("consts w_hi w_lo ot_ok oh_ok ol_ok y_ok sum_ok xt_ok xh_ok xl_ok copied "
                 "g_ok gsb_ok gt_ok sig_ok val_ok cmp_ok eqm_ok add_ok rank_ok sm_ok smt_ok smts_ok stored").split()
        s = {k: m.sem(k) for k in names}
        block = ctx.enter_context(nc.Block())
        order = [("o", 0)]
        for t in range(TC):
            order += [("o", t + 1)] * (t + 1 < TC) + [("w", t)] + [("b", t - 1)] * (t > 0)
        order.append(("b", TC - 1))

        @block.sync
        def _(sp):
            sp.dma_start(wst[:], wo).then_inc(s["consts"], 16)
            sp.dma_start(gst[:], gate_w).then_inc(s["consts"], 16)
            sp.dma_start(ident[:], eye).then_inc(s["consts"], 16)
            sp.dma_start(low[:], lower.partition_broadcast(P)).then_inc(s["consts"], 16)
            sp.dma_start(brow[:], bias.partition_broadcast(P)).then_inc(s["consts"], 16)

            def body(c, first):
                for t in range(TC):
                    rows = bass.ds(c * CH + t * P, P)
                    if not first:
                        sp.wait_ge(s["ot_ok"], c * TC - TC + t + 1)
                    sp.dma_start(oin[:, t, :], attn_out[rows, :]).then_inc(loads.sems[t], 16)
                    if not first:
                        sp.wait_ge(s["sum_ok"], c * TC - TC + t + 1)
                    sp.dma_start(xin[:, t, :], x_in[rows, :]).then_inc(loads2.sems[t], 16)

            def store(c):
                sp.wait_ge(s["smts_ok"], c + 1)
                sp.dma_start(weights_t[:, bass.ds(c * CH, CH)], smt[:]).then_inc(s["stored"], 16)

            body(0, True)
            with sp.Fori(1, NC) as c:
                body(c, False)
                store(c - 1)
            store(NC - 1)
            sp.wait_ge(s["stored"], 16 * NC)

        @block.gpsimd
        def _(pool):
            pool.wait_ge(s["consts"], 80)
            nc.gpsimd.tensor_copy(woh[:], wst[:]).then_inc(s["w_hi"], 1)
            nc.gpsimd.tensor_copy(gh[:], gst[:]).then_inc(s["w_hi"], 1)
            pool.wait_ge(s["w_hi"], 2)
            nc.gpsimd.tensor_tensor(wol[:], wst[:], f32(woh[:]), ALU.subtract).then_inc(s["w_lo"], 1)
            nc.gpsimd.tensor_tensor(gl[:], gst[:], f32(gh[:]), ALU.subtract).then_inc(s["w_lo"], 1)
            with pool.Fori(0, NC) as c:
                for t in range(TC):
                    nrm.wait(pool, c * TC + t + 1)
                    nc.gpsimd.tensor_copy(X[:, bass.ds(c * TC + t, 1), :], xn[:, t:t + 1, :])\
                        .then_inc(s["copied"], 1)

        @block.scalar
        def _(act):
            with act.Fori(0, NC) as c:
                for kind, t in order:
                    k = c * TC + t
                    if kind == "o":
                        act.wait_ge(s["ot_ok"], k + 1)
                        if t >= 2:
                            act.wait_ge(s["y_ok"], k - 1)
                        nc.scalar.activation(oth[:, t % 2, :, :].rearrange("p d t -> p (d t)"),
                                             ta[:, t % 2, :], ACT.Copy).then_inc(s["oh_ok"], 1)
                    elif kind == "w":
                        nrm.root(act, t, k)
                    else:
                        act.wait_ge(s["xt_ok"], k + 1)
                        nc.scalar.activation(xh[:, :, bass.ds(c * CH + t * P, P)],
                                             tb[:, t % 2, :].rearrange("p (d t) -> p d t", d=ND),
                                             ACT.Copy).then_inc(s["xh_ok"], 1)
                act.wait_ge(s["g_ok"], c + 1)
                nc.scalar.activation(gsb[:], gb[0:NE, :], ACT.Copy).then_inc(s["gsb_ok"], 1)
                act.wait_ge(s["gt_ok"], c + 1)
                nc.scalar.activation(sig[:].rearrange("p t e -> p (t e)"), sb8[:, 0:TC * NE],
                                     ACT.Sigmoid).then_inc(s["sig_ok"], 1)
                act.wait_ge(s["smt_ok"], c + 1)
                nc.scalar.activation(smt[:], gb[0:NE, :], ACT.Copy).then_inc(s["smts_ok"], 1)
                act.wait_ge(s["stored"], (c + 1) * 16)

        @block.vector
        def _(dve):
            nrm.init(dve)
            dve.wait_ge(s["consts"], 80)
            with dve.Fori(0, NC) as c:
                for kind, t in order:
                    k = c * TC + t
                    if kind == "o":
                        dve.wait_ge(s["oh_ok"], k + 1)
                        nc.vector.tensor_tensor(
                            otl[:, t % 2, :, :].rearrange("p d t -> p (d t)"), ta[:, t % 2, :],
                            f32(oth[:, t % 2, :, :]).rearrange("p d t -> p (d t)"),
                            ALU.subtract).then_inc(s["ol_ok"], 1)
                    elif kind == "w":
                        dve.wait_ge(s["y_ok"], k + 1)
                        loads2.wait(dve, t, c + 1)
                        nc.vector.tensor_tensor(y[:, t, :], yb[:, t % 2, :], xin[:, t, :], ALU.add)\
                            .then_inc(s["sum_ok"], 1)
                        dve.wait_ge(s["sum_ok"], k + 1)
                        nrm.mean_and_var(dve, y[:, t, :], t, k)
                        nrm.apply(dve, xn[:, t, :], y[:, t, :], t, k)
                    else:
                        dve.wait_ge(s["xh_ok"], k + 1)
                        nc.vector.tensor_tensor(
                            xl[:, :, bass.ds(c * CH + t * P, P)],
                            tb[:, t % 2, :].rearrange("p (d t) -> p d t", d=ND),
                            f32(xh[:, :, bass.ds(c * CH + t * P, P)]), ALU.subtract)\
                            .then_inc(s["xl_ok"], 1)
                dve.wait_ge(s["sig_ok"], c + 1)
                nc.vector.tensor_tensor(val[:], sig[:], brow[:].unsqueeze(1).broadcast_to([P, TC, NE]),
                                        ALU.add).then_inc(s["val_ok"], 1)
                dve.wait_ge(s["val_ok"], c + 1)
                other = val[:].unsqueeze(2).broadcast_to([P, TC, NE, NE])
                own = val[:].unsqueeze(3).broadcast_to([P, TC, NE, NE])
                g4 = gt[:].rearrange("p t (a b) -> p t a b", a=NE)
                e4 = eq[:].rearrange("p t (a b) -> p t a b", a=NE)
                nc.vector.tensor_tensor(g4, other, own, ALU.is_gt).then_inc(s["cmp_ok"], 1)
                nc.vector.tensor_tensor(e4, other, own, ALU.is_equal).then_inc(s["cmp_ok"], 1)
                dve.wait_ge(s["cmp_ok"], 2 * c + 2)
                nc.vector.tensor_tensor(eq[:], eq[:], low[:].unsqueeze(1).broadcast_to([P, TC, NE * NE]),
                                        ALU.mult).then_inc(s["eqm_ok"], 1)
                dve.wait_ge(s["eqm_ok"], c + 1)
                nc.vector.tensor_tensor(gt[:], gt[:], eq[:], ALU.add).then_inc(s["add_ok"], 1)
                dve.wait_ge(s["add_ok"], c + 1)
                nc.vector.tensor_reduce(rank[:], g4, AX, ALU.add).then_inc(s["rank_ok"], 1)
                dve.wait_ge(s["rank_ok"], c + 1)
                nc.vector.scalar_tensor_tensor(out=sm[:], in0=rank[:], scalar=2.0, in1=sig[:],
                                               op0=ALU.is_lt, op1=ALU.mult).then_inc(s["sm_ok"], 1)
                dve.wait_ge(s["copied"], (c + 1) * TC)

        @block.tensor
        def _(pe):
            pe.wait_ge(s["consts"], 80)
            pe.wait_ge(s["w_lo"], 2)
            with pe.Fori(0, NC) as c:
                for kind, t in order:
                    k = c * TC + t
                    if kind == "o":
                        loads.wait(pe, t, c + 1)
                        if t >= 2:
                            pe.wait_ge(s["ol_ok"], k - 1)
                        for d in range(ND):
                            last = nc.tensor.transpose(ta[:, t % 2, d * P:(d + 1) * P],
                                                       oin[:, t, d * P:(d + 1) * P], ident[:])
                        last.then_inc(s["ot_ok"], 1)
                    elif kind == "w":
                        pe.wait_ge(s["ol_ok"], k + 1)
                        if t >= 2:
                            pe.wait_ge(s["sum_ok"], k - 1)
                        for d in range(ND):
                            last = mm3(nc, yb[:, t % 2, :], oth[:, t % 2, d, :], otl[:, t % 2, d, :],
                                       woh[:, d, :], wol[:, d, :], d == 0, d == ND - 1)
                        last.then_inc(s["y_ok"], 1)
                    else:
                        nrm.wait(pe, k + 1)
                        if t >= 2:
                            pe.wait_ge(s["xl_ok"], k - 1)
                        for d in range(ND):
                            last = nc.tensor.transpose(tb[:, t % 2, d * P:(d + 1) * P],
                                                       xn[:, t, d * P:(d + 1) * P], ident[:])
                        last.then_inc(s["xt_ok"], 1)
                pe.wait_ge(s["xl_ok"], c * TC + TC)
                for d in range(ND):
                    cols = bass.ds(c * CH, CH)
                    last = mm3(nc, gb[0:NE, :], gh[:, d, :], gl[:, d, :], xh[:, d, cols], xl[:, d, cols],
                               d == 0, d == ND - 1)
                last.then_inc(s["g_ok"], 1)
                wait_alone(pe, s["gsb_ok"], c + 1, s["consts"], 80)
                for t in range(TC):
                    last = nc.tensor.transpose(sb8[:, t * NE:(t + 1) * NE], gsb[:, t * P:(t + 1) * P],
                                               ident[0:NE, 0:NE])
                last.then_inc(s["gt_ok"], 1)
                pe.wait_ge(s["sm_ok"], c + 1)
                for t in range(TC):
                    last = nc.tensor.transpose(gb[0:NE, t * P:(t + 1) * P], sm[:, t, :], ident[:])
                last.then_inc(s["smt_ok"], 1)
                pe.wait_ge(s["smts_ok"], c + 1)


def layer0_experts(nc, loads2, w_exp, weights_t, X, xh, xl):
    with ExitStack() as ctx:
        m = Mem(nc, ctx, "e0")
        wst = m.sb("wst", [P, EW])
        wh = m.sb("wh", [P, 2, EW], F32R)
        wl = m.sb("wl", [P, 2, EW], F32R)
        sbc = m.sb("sbc", [P, 2, S])
        sa = m.sb("sa", [P, CH])
        sg = m.sb("sg", [P, CH])
        sbb = m.sb("sbb", [P, CH])
        h = m.sb("h", [P, CH])
        hh = m.sb("hh", [P, 2, NJ, CH], F32R)
        hl = m.sb("hl", [P, 2, NJ, CH], F32R)
        ab = m.ps("ab", [P, 2, 2, CH])
        yb = m.ps("yb", [P, 4, D])
        names = ("wload wsplit_hi wsplit ab_ok sa_ok sg_ok sbb_ok h_ok hh_ok hl_ok y_ok acc_ok").split()
        s = {k: m.sem(k) for k in names}
        block = ctx.enter_context(nc.Block())
        NCH = NC * NJ

        def w13(w, b, which, d, j):
            at = (which * ND + d) * HID + j * P
            return w[:, b, at:at + P]

        def w2(w, b, j):
            at = 2 * ND * HID + j * D
            return w[:, b, at:at + D]

        def order(r):
            ev = []
            q = [(e, c) for e in range(r) for c in range(NC)]
            for i, (e, c) in enumerate(q):
                for j in range(NJ):
                    ev.append(("up", e, c, j))
                    if i > 0:
                        ev.append(("down", *q[i - 1], j))
            return ev + [("down", *q[-1], j) for j in range(NJ)]

        def each(eng, work):
            work(0, 1, True)
            with eng.Fori(0, NE // 2) as i:
                work(i * 2 + 1, 2, False)

        @block.gpsimd
        def _(pool):
            def load(e):
                pool.dma_start(wst[:], w_exp[bass.ds(e, 1)].rearrange("o p n -> (o p) n"))\
                    .then_inc(s["wload"], 16)

            def split(e, half):
                wait_alone(pool, s["wload"], e * 16 + 16, s["wload"], 16)
                nc.gpsimd.tensor_copy(wh[:, half, :], wst[:]).then_inc(s["wsplit_hi"], 1)
                pool.wait_ge(s["wsplit_hi"], e + 1)
                nc.gpsimd.tensor_tensor(wl[:, half, :], wst[:], f32(wh[:, half, :]), ALU.subtract)\
                    .then_inc(s["wsplit"], 1)
                pool.wait_ge(s["wsplit"], e + 1)

            load(0)
            split(0, 0)
            load(1)
            split(1, 1)
            load(2)

            def body(i, more):
                pool.wait_ge(s["y_ok"], (i * 2 + 1) * NC * TC)
                split(i * 2 + 2, 0)
                if more:
                    load(i * 2 + 3)
                    pool.wait_ge(s["y_ok"], (i * 2 + 2) * NC * TC)
                    split(i * 2 + 3, 1)
                    load(i * 2 + 4)

            with pool.Fori(0, NE // 2 - 1) as i:
                body(i, True)
            body(NE // 2 - 1, False)

        @block.sync
        def _(sp):
            def load(e, half):
                row = weights_t[bass.ds(e - 1, 1), :].rearrange("o n -> (o n)")
                sp.dma_start(sbc[:, half, :], row.partition_broadcast(P))\
                    .then_inc(loads2.sems[half], 16)

            load(1, 0)
            load(2, 1)
            with sp.Fori(0, NE // 2 - 1) as i:
                sp.wait_ge(s["h_ok"], (i * 2 + 2) * NCH)
                load(i * 2 + 3, 0)
                sp.wait_ge(s["h_ok"], (i * 2 + 3) * NCH)
                load(i * 2 + 4, 1)

        @block.scalar
        def _(act):
            def work(e0, r, shared):
                for ev, e, c, j in order(r):
                    if ev != "up":
                        continue
                    u = c * NJ + j + e * NCH
                    act.wait_ge(s["ab_ok" if shared else "sa_ok"], e0 * NCH + u + 1 - (0 if shared else NCH))
                    if not (shared and u == 0):
                        act.wait_ge(s["h_ok"], e0 * NCH + u)
                    nc.scalar.activation(sg[:], ab[:, u % 2, 0, :] if shared else sa[:], ACT.Silu)\
                        .then_inc(s["sg_ok"], 1)
                    act.wait_ge(s["h_ok"], e0 * NCH + u + 1)
                    if not (shared and c < 2):
                        act.wait_ge(s["y_ok"], ((e0 + e) * NC + c - 1) * TC)
                    nc.scalar.activation(hh[:, c % 2, j, :], h[:], ACT.Copy).then_inc(s["hh_ok"], 1)
            each(act, work)

        @block.vector
        def _(dve):
            def work(e0, r, shared):
                for ev, e, c, j in order(r):
                    u = c * NJ + j + e * NCH
                    k = e0 * NCH + u
                    if ev == "up":
                        cs = slice(c * CH, (c + 1) * CH)
                        if shared:
                            dve.wait_ge(s["sg_ok"], k + 1)
                            if u > 0:
                                dve.wait_ge(s["hl_ok"], k)
                            nc.vector.tensor_tensor(h[:], sg[:], ab[:, u % 2, 1, :], ALU.mult)\
                                .then_inc(s["h_ok"], 1)
                            dve.wait_ge(s["hh_ok"], k + 1)
                            nc.vector.tensor_tensor(hl[:, c % 2, j, :], h[:], f32(hh[:, c % 2, j, :]),
                                                    ALU.subtract).then_inc(s["hl_ok"], 1)
                            continue
                        dve.wait_ge(s["ab_ok"], k + 1)
                        loads2.wait_turn(dve, e % 2, e0 + e - 1)
                        nc.vector.tensor_tensor(sa[:], ab[:, u % 2, 0, :], sbc[:, e % 2, cs], ALU.mult)\
                            .then_inc(s["sa_ok"], 1)
                        nc.vector.tensor_tensor(sbb[:], ab[:, u % 2, 1, :], sbc[:, e % 2, cs], ALU.mult)\
                            .then_inc(s["sbb_ok"], 1)
                        dve.wait_ge(s["hl_ok"], k)
                        dve.wait_ge(s["sbb_ok"], k + 1 - NCH)
                        dve.wait_ge(s["sg_ok"], k + 1)
                        nc.vector.tensor_tensor(h[:], sg[:], sbb[:], ALU.mult).then_inc(s["h_ok"], 1)
                        dve.wait_ge(s["hh_ok"], k + 1)
                        nc.vector.tensor_tensor(hl[:, c % 2, j, :], h[:], f32(hh[:, c % 2, j, :]),
                                                ALU.subtract).then_inc(s["hl_ok"], 1)
                    else:
                        for t in (2 * j, 2 * j + 1):
                            dve.wait_ge(s["y_ok"], ((e0 + e) * NC + c) * TC + t + 1)
                            nc.vector.tensor_tensor(X[:, c * TC + t, :], X[:, c * TC + t, :], yb[:, t, :],
                                                    ALU.add).then_inc(s["acc_ok"], 1)
            each(dve, work)

        @block.tensor
        def _(pe):
            def work(e0, r, shared):
                for ev, e, c, j in order(r):
                    u = c * NJ + j + e * NCH
                    half = 0 if shared else (e + 1) % 2
                    k = e0 * NCH + u
                    if ev == "up":
                        if c == 0 and j == 0:
                            pe.wait_ge(s["wsplit"], e0 + e + 1)
                        if not (shared and u < 2):
                            pe.wait_ge(s["h_ok"], k - 1)
                        cs = slice(c * CH, (c + 1) * CH)
                        for which in range(2):
                            for d in range(ND):
                                last = mm3(nc, ab[:, u % 2, which, :], w13(wh, half, which, d, j),
                                           w13(wl, half, which, d, j), xh[:, d, cs], xl[:, d, cs],
                                           d == 0, d == ND - 1)
                        last.then_inc(s["ab_ok"], 1)
                    else:
                        pe.wait_ge(s["hl_ok"], (e0 + e) * NCH + (c + 1) * NJ)
                        for t in (2 * j, 2 * j + 1):
                            if not (shared and c == 0):
                                pe.wait_ge(s["acc_ok"], ((e0 + e) * NC + c - 1) * TC + t + 1)
                            for i in range(NJ):
                                last = mm3(nc, yb[:, t, :], hh[:, c % 2, i, t * P:(t + 1) * P],
                                           hl[:, c % 2, i, t * P:(t + 1) * P], w2(wh, half, i),
                                           w2(wl, half, i), i == 0, i == NJ - 1)
                            last.then_inc(s["y_ok"], 1)
            each(pe, work)


def layer1_qkv(nc, nrm, w_qkv, qk_bias, v_bias, rope, rot, eye, X, kth, ktl, x2, q_dram, v_dram):
    with ExitStack() as ctx:
        m = Mem(nc, ctx, "q1")
        wst = m.sb("wst", [P, D])
        wh = m.sb("wh", [P, 3, ND, D], F32R)
        wl = m.sb("wl", [P, 3, ND, D], F32R)
        xch = m.sb("xch", [P, ND, CH], F32R)
        xcl = m.sb("xcl", [P, ND, CH], F32R)
        xn = m.sb("xn", [P, TC, D])
        cs = m.sb("cs", [P, 2, CH])
        ident = m.sb("ident", [P, P])
        rotf = m.sb("rotf", [P, P])
        bqk = m.sb("bqk", [P, 2, ND])
        bv = m.sb("bv", [P, D])
        qkf = m.sb("qkf", [P, 2, CH])
        t1 = m.sb("t1", [P, 2, CH])
        t2 = m.sb("t2", [P, 2, CH])
        vf, vhl = t2[:, 0, :], m.sb("vhl", [P, 2, D], F32R)
        qhl = m.sb("qhl", [P, 2, CH], F32R)
        qk = m.ps("qk", [P, 2, CH])
        rb = m.ps("rb", [P, 2, CH])
        vb = m.ps("vb", [P, 2, D])
        tb = m.ps("tb", [P, 2, ND * P])
        names = ("consts wload whi wlo csload xt_ok xh_ok xl_ok qk_ok qkf_ok r_ok t1_ok t2_ok sum_ok hi_ok "
                 "lo_ok v_ok vf_ok vh_ok vl_ok qstore vstore xstore").split()
        s = {k: m.sem(k) for k in names}
        block = ctx.enter_context(nc.Block())
        NW = 3 * ND

        @block.sync
        def _(sp):
            for dst, src in ((ident[:], eye), (rotf[:], rot), (bqk[:], qk_bias),
                             (bv[:], v_bias.partition_broadcast(P))):
                sp.dma_start(dst, src).then_inc(s["consts"], 16)
            sp.dma_start(cs[:], rope[:, :, 0:CH].rearrange("a p n -> p a n")).then_inc(s["csload"], 16)
            for i in range(NW):
                if i > 0:
                    sp.wait_ge(s["wlo"], i)
                sp.dma_start(wst[:], w_qkv[i // ND, :, i % ND, :]).then_inc(s["wload"], 16)

            def body(c, more):
                for t in range(TC):
                    nrm.wait(sp, c * TC + t + 1)
                    sp.dma_start(x2[bass.ds(c * CH + t * P, P), :], xn[:, t, :]).then_inc(s["xstore"], 16)
                for j in range(ND):
                    wait_alone(sp, s["lo_ok"], c * ND + j + 1, s["consts"], 16)
                    sp.dma_start(q_dram[:, :, j, bass.ds(c * CH, CH)].rearrange("a p n -> p a n"),
                                 f32(qhl[:])).then_inc(s["qstore"], 16)
                if more:
                    sp.dma_start(cs[:], rope[:, :, bass.ds((c + 1) * CH, CH)].rearrange("a p n -> p a n"))\
                        .then_inc(s["csload"], 16)
                for t in range(TC):
                    sp.wait_ge(s["vl_ok"], c * TC + t + 1)
                    sp.dma_start(v_dram[:, :, bass.ds(c * TC + t, 1), :]
                                 .rearrange("a p o n -> p a (o n)"), f32(vhl[:])).then_inc(s["vstore"], 16)

            with sp.Fori(0, NC - 1) as c:
                body(c, True)
            body(NC - 1, False)
            sp.wait_ge(s["qstore"], 16 * NC * ND)
            sp.wait_ge(s["vstore"], 16 * NC * TC)
            sp.wait_ge(s["xstore"], 16 * NC * TC)

        @block.gpsimd
        def _(pool):
            for i in range(NW):
                pool.wait_ge(s["wload"], 16 * i + 16)
                nc.gpsimd.tensor_copy(wh[:, i // ND, i % ND, :], wst[:]).then_inc(s["whi"], 1)
                pool.wait_ge(s["whi"], i + 1)
                nc.gpsimd.tensor_tensor(wl[:, i // ND, i % ND, :], wst[:], f32(wh[:, i // ND, i % ND, :]),
                                        ALU.subtract).then_inc(s["wlo"], 1)
            with pool.Fori(0, NC) as c:
                for j in range(ND):
                    k = c * ND + j
                    pool.wait_ge(s["qkf_ok"], k + 1)
                    pool.wait_ge(s["csload"], 16 * c + 16)
                    if j > 0:
                        pool.wait_ge(s["lo_ok"], k)
                    nc.gpsimd.tensor_tensor(t1[:], qkf[:], cs[:, 0, :].unsqueeze(1).broadcast_to([P, 2, CH]),
                                            ALU.mult).then_inc(s["t1_ok"], 1)

        @block.scalar
        def _(act):
            act.wait_ge(s["consts"], 64)
            with act.Fori(0, NC) as c:
                for t in range(TC):
                    nrm.root(act, t, c * TC + t)
                for t in range(TC):
                    act.wait_ge(s["xt_ok"], c * TC + t + 1)
                    nc.scalar.activation(xch[:, :, t * P:(t + 1) * P],
                                         tb[:, t % 2, :].rearrange("p (d t) -> p d t", d=ND),
                                         ACT.Copy).then_inc(s["xh_ok"], 1)

                def evict(j):
                    act.wait_ge(s["qk_ok"], c * ND + j + 1)
                    if j > 0:
                        act.wait_ge(s["sum_ok"], c * ND + j)
                    for a in range(2):
                        last = nc.scalar.activation(qkf[:, a, :], qk[:, a, :], ACT.Identity,
                                                    bias=bqk[:, a, j:j + 1])
                    last.then_inc(s["qkf_ok"], 1)

                for j in range(ND):
                    evict(j)
                    act.wait_ge(s["sum_ok"], c * ND + j + 1)
                    if j > 0:
                        act.wait_ge(s["qstore"], 16 * (c * ND + j))
                    nc.scalar.activation(qhl[:, 0, :], t1[:, 0, :], ACT.Copy)
                    nc.scalar.activation(kth[:, j, bass.ds(c * CH, CH)], t1[:, 1, :], ACT.Copy)\
                        .then_inc(s["hi_ok"], 1)
                for t in range(TC):
                    act.wait_ge(s["vf_ok"], c * TC + t + 1)
                    if t > 0:
                        act.wait_ge(s["vstore"], 16 * (c * TC + t))
                    nc.scalar.activation(vhl[:, 0, :], vf, ACT.Copy).then_inc(s["vh_ok"], 1)
                act.wait_ge(s["qstore"], 16 * (c + 1) * ND)
                act.wait_ge(s["vstore"], 16 * (c + 1) * TC)

        @block.vector
        def _(dve):
            dve.wait_ge(s["consts"], 64)
            with dve.Fori(0, NC) as c:
                for t in range(TC):
                    nrm.mean_and_var(dve, X[:, bass.ds(c * TC + t, 1), :].rearrange("p o n -> p (o n)"), t,
                                c * TC + t)
                for t in range(TC):
                    nrm.apply(dve, xn[:, t, :], X[:, bass.ds(c * TC + t, 1), :]
                              .rearrange("p o n -> p (o n)"), t, c * TC + t)
                for t in range(TC):
                    dve.wait_ge(s["xh_ok"], c * TC + t + 1)
                    nc.vector.tensor_tensor(xcl[:, :, t * P:(t + 1) * P],
                                            tb[:, t % 2, :].rearrange("p (d t) -> p d t", d=ND),
                                            f32(xch[:, :, t * P:(t + 1) * P]), ALU.subtract)\
                        .then_inc(s["xl_ok"], 1)
                dve.wait_ge(s["csload"], 16 * c + 16)
                for j in range(ND):
                    k = c * ND + j
                    dve.wait_ge(s["r_ok"], k + 1)
                    nc.vector.tensor_tensor(t2[:], rb[:], cs[:, 1, :].unsqueeze(1).broadcast_to([P, 2, CH]),
                                            ALU.mult).then_inc(s["t2_ok"], 1)
                    dve.wait_ge(s["t2_ok"], k + 1)
                    dve.wait_ge(s["t1_ok"], k + 1)
                    nc.vector.tensor_tensor(t1[:], t1[:], t2[:], ALU.add).then_inc(s["sum_ok"], 1)
                    dve.wait_ge(s["hi_ok"], k + 1)
                    nc.vector.tensor_tensor(qhl[:, 1, :], t1[:, 0, :], f32(qhl[:, 0, :]), ALU.subtract)
                    nc.vector.tensor_tensor(ktl[:, j, bass.ds(c * CH, CH)], t1[:, 1, :],
                                            f32(kth[:, j, bass.ds(c * CH, CH)]), ALU.subtract)\
                        .then_inc(s["lo_ok"], 1)
                for t in range(TC):
                    k = c * TC + t
                    dve.wait_ge(s["v_ok"], k + 1)
                    if t > 0:
                        dve.wait_ge(s["vl_ok"], k)
                    nc.vector.tensor_tensor(vf, vb[:, t % 2, :], bv[:], ALU.add).then_inc(s["vf_ok"], 1)
                    dve.wait_ge(s["vh_ok"], k + 1)
                    nc.vector.tensor_tensor(vhl[:, 1, :], vf, f32(vhl[:, 0, :]), ALU.subtract)\
                        .then_inc(s["vl_ok"], 1)
                dve.wait_ge(s["vl_ok"], (c + 1) * TC)
                dve.wait_ge(s["xstore"], 16 * (c + 1) * TC)

        @block.tensor
        def _(pe):
            pe.wait_ge(s["consts"], 64)
            with pe.Fori(0, NC) as c:
                for t in range(TC):
                    nrm.wait(pe, c * TC + t + 1)
                    if t >= 2:
                        pe.wait_ge(s["xl_ok"], c * TC + t - 1)
                    for d in range(ND):
                        last = nc.tensor.transpose(tb[:, t % 2, d * P:(d + 1) * P],
                                                   xn[:, t, d * P:(d + 1) * P], ident[:])
                    last.then_inc(s["xt_ok"], 1)
                pe.wait_ge(s["xl_ok"], (c + 1) * TC)
                pe.wait_ge(s["wlo"], NW)

                def rotate(j):
                    pe.wait_ge(s["qkf_ok"], c * ND + j + 1)
                    if j > 0:
                        pe.wait_ge(s["t2_ok"], c * ND + j)
                    for a in range(2):
                        last = nc.tensor.matmul(rb[:, a, :], rotf[:], qkf[:, a, :], start=True, stop=True)
                    last.then_inc(s["r_ok"], 1)

                def value(t):
                    if t >= 2:
                        pe.wait_ge(s["vf_ok"], c * TC + t - 1)
                    for d in range(ND):
                        last = mm3(nc, vb[:, t % 2, :], xch[:, d, t * P:(t + 1) * P],
                                   xcl[:, d, t * P:(t + 1) * P], wh[:, 2, d, :], wl[:, 2, d, :],
                                   d == 0, d == ND - 1)
                    last.then_inc(s["v_ok"], 1)

                for j in range(ND):
                    if j > 0:
                        pe.wait_ge(s["qkf_ok"], c * ND + j)
                    for a in range(2):
                        for d in range(ND):
                            last = mm3(nc, qk[:, a, :], wh[:, a, d, j * P:(j + 1) * P],
                                       wl[:, a, d, j * P:(j + 1) * P], xch[:, d, :], xcl[:, d, :],
                                       d == 0, d == ND - 1)
                    last.then_inc(s["qk_ok"], 1)
                    rotate(j)
                for t in range(TC):
                    value(t)


def layer1_attention(nc, loads, loads2, stores, wo, eye, kth, ktl, x2, q_dram, v_dram, y_dram):
    with ExitStack() as ctx:
        m = Mem(nc, ctx, "a1")
        vh = m.sb("vh", [P, NT, D], F32R)
        vl = m.sb("vl", [P, NT, D], F32R)
        woh = m.sb("woh", [P, ND, D], F32R)
        wol = m.sb("wol", [P, ND, D], F32R)
        q = m.sb("q", [P, 2, 2, ND, P], F32R)
        pr = m.sb("pr", [P, S])
        pth = m.sb("pth", [P, NT, P], F32R)
        ptl = m.sb("ptl", [P, NT, P], F32R)
        xin = m.sb("xin", [P, 2, D])
        ident = m.sb("ident", [P, P])
        nm = m.sb("nm", [P, 1])
        bias = m.sb("bias", [P, 1])
        rsum = m.sb("rsum", [P, 1])
        rinv = m.sb("rinv", [P, 1])
        o = m.sb("o", [P, D])
        oth = m.sb("oth", [P, ND, P], F32R)
        otl = m.sb("otl", [P, ND, P], F32R)
        y = m.sb("y", [P, 2, D])
        wst = pr
        sc = m.ps("sc", [P, S])
        tb = m.ps("tb", [P, 2, 4 * P])
        av = m.ps("av", [P, D])
        yb = m.ps("yb", [P, D])
        names = ("consts vload w_hi w_lo s_ok nm_ok bias_ok exp_ok rinv_ok pt_ok ph_ok pl_ok "
                 "av_ok o_ok ot_ok oh_ok ol_ok y_ok sum_ok").split()
        s = {k: m.sem(k) for k in names}
        block = ctx.enter_context(nc.Block())

        def loop(eng, tile):
            with eng.Fori(0, NT // 2 - 1) as i:
                tile(i * 2, 0, False)
                tile(i * 2 + 1, 1, False)
            tile(NT - 2, 0, False)
            tile(NT - 1, 1, True)

        @block.sync
        def _(sp):
            sp.dma_start(ident[:], eye).then_inc(s["consts"], 16)
            sp.dma_start(wst[:], wo.rearrange("p a n -> p (a n)")).then_inc(s["consts"], 16)

            def load(n, r):
                cols = bass.ds(n * P, P)
                for a in range(2):
                    sp.dma_start(f32(q[:, r, a, :, :]), q_dram[a, :, :, cols])\
                        .then_inc(loads.sems[r], 16)

            load(0, 0)
            load(1, 1)
            for a, dst in ((0, vh), (1, vl)):
                for c in range(NC):
                    ts = slice(c * TC, (c + 1) * TC)
                    sp.dma_start(f32(dst[:, ts, :]), v_dram[a, :, ts, :]).then_inc(s["vload"], 16)
            sp.dma_start(xin[:, 0, :], x2[0:P, :]).then_inc(loads2.sems[0], 16)

            def store(n, r):
                sp.wait_ge(s["sum_ok"], n + 1)
                sp.dma_start(y_dram[bass.ds(n * P, P), :], y[:, r, :]).then_inc(stores.sems[r], 16)

            def tile(n, r, first, more):
                if more:
                    sp.wait_ge(s["s_ok"], n + 1)
                    load(n + 2, r)
                if not first:
                    store(n - 1, 1 - r)
                sp.dma_start(xin[:, 1 - r, :], x2[bass.ds((n + 1) * P, P), :])\
                  .then_inc(loads2.sems[1 - r], 16)

            tile(0, 0, True, True)
            tile(1, 1, False, True)
            with sp.Fori(1, NT // 2 - 1) as i:
                tile(i * 2, 0, False, True)
                tile(i * 2 + 1, 1, False, True)
            tile(NT - 2, 0, False, False)
            store(NT - 2, 0)
            store(NT - 1, 1)
            for r in range(2):
                stores.wait(sp, r, NT // 2)

        @block.gpsimd
        def _(pool):
            pool.wait_ge(s["consts"], 32)
            flat = "p d n -> p (d n)"
            nc.gpsimd.tensor_copy(woh[:].rearrange(flat), wst[:]).then_inc(s["w_hi"], 1)
            pool.wait_ge(s["w_hi"], 1)
            nc.gpsimd.tensor_tensor(wol[:].rearrange(flat), wst[:], f32(woh[:]).rearrange(flat),
                                    ALU.subtract).then_inc(s["w_lo"], 1)

        def exps(act, n):
            act.wait_ge(s["bias_ok"], n + 1)
            nc.scalar.activation(pr[:], sc[:], ACT.Exp, bias=bias[:], scale=SCALE1,
                                 accum_out=rsum[:]).then_inc(s["exp_ok"], 1)

        @block.scalar
        def _(act):
            act.wait_ge(s["w_lo"], 1)
            exps(act, 0)

            def tile(n, r, last):
                hi_out(n, r, act)
                for g in range(4):
                    act.wait_ge(s["pt_ok"], n * 4 + g + 1)
                    nc.scalar.activation(pth[:, 4 * g:4 * g + 4, :].rearrange("p a b -> p (a b)"),
                                         tb[:, (g + 1) % 2, :], ACT.Copy).then_inc(s["ph_ok"], 1)
                if not last:
                    exps(act, n + 1)

            def hi_out(n, r, act):
                act.wait_ge(s["ot_ok"], n)
                nc.scalar.activation(oth[:].rearrange("p a b -> p (a b)"), tb[:, 0, :], ACT.Copy)\
                    .then_inc(s["oh_ok"], 1)

            def first(n, r, last):
                for g in range(4):
                    act.wait_ge(s["pt_ok"], n * 4 + g + 1)
                    nc.scalar.activation(pth[:, 4 * g:4 * g + 4, :].rearrange("p a b -> p (a b)"),
                                         tb[:, (g + 1) % 2, :], ACT.Copy).then_inc(s["ph_ok"], 1)
                exps(act, n + 1)

            first(0, 0, False)
            tile(1, 1, False)
            with act.Fori(1, NT // 2 - 1) as i:
                tile(i * 2, 0, False)
                tile(i * 2 + 1, 1, False)
            tile(NT - 2, 0, False)
            tile(NT - 1, 1, True)
            hi_out(NT, 0, act)

        @block.vector
        def _(dve):
            def peak(n):
                dve.wait_ge(s["s_ok"], n + 1)
                nc.vector.tensor_reduce(nm[:], sc[:], AX, ALU.max, negate=True).then_inc(s["nm_ok"], 1)
                dve.wait_ge(s["nm_ok"], n + 1)
                nc.vector.tensor_scalar(bias[:], nm[:], SCALE1, None, ALU.mult).then_inc(s["bias_ok"], 1)

            def lo_out(n):
                dve.wait_ge(s["oh_ok"], n)
                nc.vector.tensor_tensor(otl[:].rearrange("p a b -> p (a b)"), tb[:, 0, :],
                                        f32(oth[:]).rearrange("p a b -> p (a b)"), ALU.subtract)\
                    .then_inc(s["ol_ok"], 1)

            def add(n, r, first):
                dve.wait_ge(s["y_ok"], n + 1)
                loads2.wait_turn(dve, r, n)
                if not first:
                    stores.wait_turn(dve, r, n - 2)
                nc.vector.tensor_tensor(y[:, r, :], yb[:], xin[:, r, :], ALU.add).then_inc(s["sum_ok"], 1)

            def tile(n, r, last, no=99):
                if no > 0:
                    lo_out(n)
                for g in range(4):
                    dve.wait_ge(s["ph_ok"], n * 4 + g + 1)
                    nc.vector.tensor_tensor(ptl[:, 4 * g:4 * g + 4, :].rearrange("p a b -> p (a b)"),
                                            tb[:, (g + 1) % 2, :],
                                            f32(pth[:, 4 * g:4 * g + 4, :]).rearrange("p a b -> p (a b)"),
                                            ALU.subtract).then_inc(s["pl_ok"], 1)
                    if g == 2 and no > 0:
                        add(n - 1, 1 - r, no < 3)
                dve.wait_ge(s["exp_ok"], n + 1)
                nc.vector.reciprocal(rinv[:], rsum[:]).then_inc(s["rinv_ok"], 1)
                if not last:
                    dve.wait_ge(s["rinv_ok"], n + 1)
                    peak(n + 1)
                dve.wait_ge(s["rinv_ok"], n + 1)
                dve.wait_ge(s["av_ok"], n + 1)
                nc.vector.tensor_scalar(o[:], av[:], rinv[:], None, ALU.mult).then_inc(s["o_ok"], 1)

            peak(0)
            tile(0, 0, False, 0)
            tile(1, 1, False, 1)
            tile(2, 0, False, 2)
            tile(3, 1, False, 3)
            with dve.Fori(2, NT // 2 - 1) as i:
                tile(i * 2, 0, False)
                tile(i * 2 + 1, 1, False)
            tile(NT - 2, 0, False)
            tile(NT - 1, 1, True)
            lo_out(NT)
            add(NT - 1, 1, False)

        @block.tensor
        def _(pe):
            pe.wait_ge(s["consts"], 32)

            def scores(n, r, b):
                ks = slice(b * CH, (b + 1) * CH)
                if b == 0:
                    loads.wait_turn(pe, r, n, 2)
                for d in range(ND):
                    last = mm3(nc, sc[:, ks], q[:, r, 0, d, :], q[:, r, 1, d, :], kth[:, d, ks],
                               ktl[:, d, ks], d == 0, d == ND - 1)
                if b == 3:
                    last.then_inc(s["s_ok"], 1)

            def turn_out(n):
                pe.wait_ge(s["o_ok"], n)
                for d in range(ND):
                    last = nc.tensor.transpose(tb[:, 0, d * P:(d + 1) * P], o[:, d * P:(d + 1) * P], ident[:])
                last.then_inc(s["ot_ok"], 1)

            def project(n, no=99):
                pe.wait_ge(s["ol_ok"], n)
                if no > 1:
                    pe.wait_ge(s["sum_ok"], n - 1)
                for d in range(ND):
                    last = mm3(nc, yb[:], oth[:, d, :], otl[:, d, :], woh[:, d, :], wol[:, d, :],
                               d == 0, d == ND - 1)
                last.then_inc(s["y_ok"], 1)

            def tile(n, r, last, no=99):
                pe.wait_ge(s["exp_ok"], n + 1)
                for b in range(4):
                    if b == 0 and no > 0:
                        pe.wait_ge(s["pl_ok"], 4 * n)
                        turn_out(n)
                    if not last:
                        scores(n + 1, 1 - r, b)
                    if b == 1 and no > 0:
                        pe.wait_ge(s["ol_ok"], n)
                    if b >= 2:
                        pe.wait_ge(s["pl_ok"], 4 * n + b - 1)
                    for a in range(4):
                        kt = 4 * b + a
                        end = nc.tensor.transpose(tb[:, (b + 1) % 2, a * P:(a + 1) * P],
                                                  pr[:, kt * P:(kt + 1) * P], ident[:])
                    end.then_inc(s["pt_ok"], 1)
                    if b == 2 and no > 0:
                        project(n, no)
                if no == 0:
                    pe.wait_ge(s["vload"], 16 * 2 * NC)
                for kt in range(NT):
                    if kt % 4 == 0:
                        pe.wait_ge(s["pl_ok"], 4 * n + kt // 4 + 1)
                    end = mm3(nc, av[:], pth[:, kt, :], ptl[:, kt, :], vh[:, kt, :], vl[:, kt, :],
                              kt == 0, kt == NT - 1)
                end.then_inc(s["av_ok"], 1)

            pe.wait_ge(s["w_lo"], 1)
            for b in range(4):
                scores(0, 0, b)
            tile(0, 0, False, 0)
            tile(1, 1, False, 1)
            with pe.Fori(1, NT // 2 - 1) as i:
                tile(i * 2, 0, False)
                tile(i * 2 + 1, 1, False)
            tile(NT - 2, 0, False)
            tile(NT - 1, 1, True)
            turn_out(NT)
            project(NT)


def layer1_norm(nc, nrm, loads, y_dram, eye, X, xh, xl):
    with ExitStack() as ctx:
        m = Mem(nc, ctx, "n1")
        ident = m.sb("ident", [P, P])
        yin = m.sb("yin", [P, TC, D])
        xn = m.sb("xn", [P, TC, D])
        tb = m.ps("tb", [P, TC, ND * P])
        names = "consts copied xt_ok xh_ok xl_ok".split()
        s = {k: m.sem(k) for k in names}
        block = ctx.enter_context(nc.Block())

        @block.sync
        def _(sp):
            sp.dma_start(ident[:], eye).then_inc(s["consts"], 16)

            def body(c, first):
                for t in range(TC):
                    if not first:
                        nrm.wait(sp, c * TC - TC + t + 1)
                    sp.dma_start(yin[:, t, :], y_dram[bass.ds(c * CH + t * P, P), :])\
                      .then_inc(loads.sems[t], 16)

            body(0, True)
            with sp.Fori(1, NC) as c:
                body(c, False)

        @block.gpsimd
        def _(pool):
            with pool.Fori(0, NC) as c:
                for t in range(TC):
                    nrm.wait(pool, c * TC + t + 1)
                    nc.gpsimd.tensor_copy(X[:, bass.ds(c * TC + t, 1), :], xn[:, t:t + 1, :])\
                        .then_inc(s["copied"], 1)

        @block.scalar
        def _(act):
            with act.Fori(0, NC) as c:
                for t in range(TC):
                    nrm.root(act, t, c * TC + t)
                for t in range(TC):
                    act.wait_ge(s["xt_ok"], c * TC + t + 1)
                    nc.scalar.activation(xh[:, :, bass.ds(c * CH + t * P, P)],
                                         tb[:, t, :].rearrange("p (d t) -> p d t", d=ND),
                                         ACT.Copy).then_inc(s["xh_ok"], 1)

        @block.vector
        def _(dve):
            with dve.Fori(0, NC) as c:
                for t in range(TC):
                    loads.wait(dve, t, c + 1)
                    nrm.mean_and_var(dve, yin[:, t, :], t, c * TC + t)
                for t in range(TC):
                    nrm.apply(dve, xn[:, t, :], yin[:, t, :], t, c * TC + t)
                for t in range(TC):
                    dve.wait_ge(s["xh_ok"], c * TC + t + 1)
                    nc.vector.tensor_tensor(
                        xl[:, :, bass.ds(c * CH + t * P, P)],
                        tb[:, t, :].rearrange("p (d t) -> p d t", d=ND),
                        f32(xh[:, :, bass.ds(c * CH + t * P, P)]), ALU.subtract).then_inc(s["xl_ok"], 1)
                dve.wait_ge(s["copied"], (c + 1) * TC)

        @block.tensor
        def _(pe):
            pe.wait_ge(s["consts"], 16)
            with pe.Fori(0, NC) as c:
                for t in range(TC):
                    nrm.wait(pe, c * TC + t + 1)
                    for d in range(ND):
                        last = nc.tensor.transpose(tb[:, t, d * P:(d + 1) * P],
                                                   xn[:, t, d * P:(d + 1) * P], ident[:])
                    last.then_inc(s["xt_ok"], 1)


def layer1_mlp(nc, loads, w_mlp, X, xh, xl):
    with ExitStack() as ctx:
        m = Mem(nc, ctx, "m1")
        PW = 2 * D
        wst = m.sb("wst", [P, 2, PW])
        wh = m.sb("wh", [P, 6, PW], F32R)
        wl = m.sb("wl", [P, 6, PW], F32R)
        sg = m.sb("sg", [P, CH])
        h = m.sb("h", [P, 4, CH])
        a = m.sb("a", [P, 4, CH])
        c0 = m.sb("c0", [P, 3, CH], BF16)
        c1 = m.sb("c1", [P, 2, CH], BF16)
        c2 = m.sb("c2", [P, CH], BF16)
        k = m.sb("k", [P, 4, CH], BF16)
        hh = m.sb("hh", [P, 4, CH], F32R)
        hl = m.sb("hl", [P, 4, CH], F32R)
        gu = m.ps("gu", [P, 2, 2, CH])
        yb = m.ps("yb", [P, 4, D])
        names = ("whi wlo gu_ok sg_ok h_ok a_ok cmp_ok k1_ok k2_ok hs_ok hh_ok hl_ok y_ok "
                 "acc_ok").split()
        s = {n: m.sem(n) for n in names}
        block = ctx.enter_context(nc.Block())
        NPC = 6

        def group(q, first):
            ev = []
            for c in range(NC):
                ev += [("up", c, q, r) for r in range(4)]
                if c > 0:
                    ev += [("down", c - 1, q, 0), ("pick", c, q, 0), ("add", c - 1, q, 0)]
                elif not first:
                    ev += [("down", NC - 1, q - 1, 0), ("pick", c, q, 0), ("add", NC - 1, q - 1, 0)]
                else:
                    ev.append(("pick", c, q, 0))
            return ev

        def groups(eng, run):
            run(group(0, True))
            with eng.Fori(1, NQ) as q:
                run(group(q, False))
            run([("down", NC - 1, NQ - 1, 0), ("add", NC - 1, NQ - 1, 0)])

        @block.sync
        def _(sp):
            def load(q, i):
                sp.dma_start(wst[:, i % 2, :], w_mlp[bass.ds(q, 1), i, :, :].rearrange("o p n -> (o p) n"))\
                    .then_inc(loads.sems[i % 2], 16)

            for i in range(NPC):
                if i >= 2:
                    sp.wait_ge(s["wlo"], i - 1)
                load(0, i)
            with sp.Fori(1, NQ) as q:
                for i in range(NPC):
                    sp.wait_ge(s["wlo"], q * NPC + i - 1)
                    load(q, i)

        @block.gpsimd
        def _(pool):
            def split(q, i, first):
                if not first:
                    if i < 4:
                        wait_alone(pool, s["gu_ok"], q * NC * 4 - 3 + i, s["wlo"], 1)
                    else:
                        wait_alone(pool, s["y_ok"], q * NC * TC, s["wlo"], 1)
                wait_alone(pool, loads.sems[i % 2], 16 * (loads.before[i % 2] + i // 2 + 1) + q * (8 * NPC),
                           loads.sems[i % 2], 16)
                nc.gpsimd.tensor_copy(wh[:, i, :], wst[:, i % 2, :]).then_inc(s["whi"], 1)
                pool.wait_ge(s["whi"], q * NPC + i + 1)
                nc.gpsimd.tensor_tensor(wl[:, i, :], wst[:, i % 2, :], f32(wh[:, i, :]), ALU.subtract)\
                    .then_inc(s["wlo"], 1)

            for i in range(NPC):
                split(0, i, True)
            with pool.Fori(1, NQ) as q:
                for i in range(NPC):
                    split(q, i, False)

        @block.scalar
        def _(act):
            def run(ev):
                for what, c, q, r in ev:
                    i = q * NC + c
                    start = ev[0][2] is q and c == 0 and isinstance(q, int)
                    if what == "up":
                        act.wait_ge(s["gu_ok"], i * 4 + r + 1)
                        if not (start and r == 0):
                            act.wait_ge(s["h_ok"], i * 4 + r)
                        nc.scalar.activation(sg[:], gu[:, r % 2, 0, :], ACT.Silu).then_inc(s["sg_ok"], 1)
                    elif what == "pick":
                        act.wait_ge(s["h_ok"], (i + 1) * 4)
                        nc.scalar.activation(a[:], h[:], ACT.Abs).then_inc(s["a_ok"], 1)
                        if not start:
                            act.wait_ge(s["y_ok"], i * TC)
                        for r in range(4):
                            act.wait_ge(s["hs_ok"], i * 4 + r + 1)
                            nc.scalar.activation(hh[:, r, :], h[:, r, :], ACT.Copy).then_inc(s["hh_ok"], 1)
            groups(act, run)

        @block.vector
        def _(dve):
            tt, stt = nc.vector.tensor_tensor, nc.vector.scalar_tensor_tensor

            def run(ev):
                for what, c, q, r in ev:
                    i = q * NC + c
                    if what == "up":
                        if r == 0 and not (c == 0 and isinstance(q, int)):
                            dve.wait_ge(s["hl_ok"], i * 4)
                        dve.wait_ge(s["sg_ok"], i * 4 + r + 1)
                        tt(h[:, r, :], sg[:], gu[:, r % 2, 1, :], ALU.mult).then_inc(s["h_ok"], 1)
                    elif what == "add":
                        for t in range(TC):
                            dve.wait_ge(s["y_ok"], i * TC + t + 1)
                            tt(X[:, c * TC + t, :], X[:, c * TC + t, :], yb[:, t, :], ALU.add)\
                                .then_inc(s["acc_ok"], 1)
                    elif what == "pick":
                        dve.wait_ge(s["a_ok"], i + 1)
                        tt(c0[:], a[:, 1:4, :], a[:, 0:1, :].broadcast_to([P, 3, CH]), ALU.is_gt)\
                            .then_inc(s["cmp_ok"], 1)
                        tt(c1[:], a[:, 2:4, :], a[:, 1:2, :].broadcast_to([P, 2, CH]), ALU.is_gt)\
                            .then_inc(s["cmp_ok"], 1)
                        tt(c2[:], a[:, 3, :], a[:, 2, :], ALU.is_gt).then_inc(s["cmp_ok"], 1)
                        dve.wait_ge(s["cmp_ok"], 3 * i + 3)
                        tt(k[:, 0, :], c0[:, 0, :], c0[:, 1, :], ALU.add).then_inc(s["k1_ok"], 1)
                        tt(k[:, 1, :], c1[:, 0, :], c1[:, 1, :], ALU.add).then_inc(s["k1_ok"], 1)
                        tt(k[:, 2:4, :], c0[:, 1:3, :], c1[:], ALU.add).then_inc(s["k1_ok"], 1)
                        dve.wait_ge(s["k1_ok"], 3 * i + 3)
                        tt(k[:, 0, :], k[:, 0, :], c0[:, 2, :], ALU.add).then_inc(s["k2_ok"], 1)
                        tt(k[:, 1, :], k[:, 1, :], c0[:, 0, :], ALU.subtract).then_inc(s["k2_ok"], 1)
                        tt(k[:, 2, :], c2[:], k[:, 2, :], ALU.subtract).then_inc(s["k2_ok"], 1)
                        tt(k[:, 3, :], k[:, 3, :], c2[:], ALU.add).then_inc(s["k2_ok"], 1)
                        dve.wait_ge(s["k2_ok"], 4 * i + 4)
                        keep = ((ALU.is_lt, 2.0), (ALU.is_lt, 1.0), (ALU.is_lt, 0.0), (ALU.is_gt, 1.0))
                        for r, (op, than) in enumerate(keep):
                            stt(out=h[:, r, :], in0=k[:, r, :], scalar=than, in1=h[:, r, :], op0=op,
                                op1=ALU.mult).then_inc(s["hs_ok"], 1)
                        for r in range(4):
                            dve.wait_ge(s["hh_ok"], 4 * i + r + 1)
                            tt(hl[:, r, :], h[:, r, :], f32(hh[:, r, :]), ALU.subtract)\
                                .then_inc(s["hl_ok"], 1)
            groups(dve, run)

        @block.tensor
        def _(pe):
            def run(ev):
                for what, c, q, r in ev:
                    i = q * NC + c
                    start = c == 0 and isinstance(q, int)
                    if what == "up":
                        u = i * 4 + r
                        cs = slice(c * CH, (c + 1) * CH)
                        if not (start and r < 2):
                            pe.wait_ge(s["h_ok"], u - 1)
                        if c == 0:
                            pe.wait_ge(s["wlo"], q * NPC + r + 1)
                        for which in range(2):
                            for d in range(ND):
                                at = (which * ND + d) * P
                                last = mm3(nc, gu[:, r % 2, which, :], wh[:, r, at:at + P],
                                           wl[:, r, at:at + P], xh[:, d, cs], xl[:, d, cs],
                                           d == 0, d == ND - 1)
                        last.then_inc(s["gu_ok"], 1)
                    elif what == "down":
                        pe.wait_ge(s["hl_ok"], (i + 1) * 4)
                        if c == 0:
                            pe.wait_ge(s["wlo"], (q + 1) * NPC)
                        for t in range(TC):
                            if not start:
                                pe.wait_ge(s["acc_ok"], (i - 1) * TC + t + 1)
                            for r in range(4):
                                ts = slice(t * P, (t + 1) * P)
                                at = r % 2 * D
                                last = mm3(nc, yb[:, t, :], hh[:, r, ts], hl[:, r, ts],
                                           wh[:, 4 + r // 2, at:at + D], wl[:, 4 + r // 2, at:at + D],
                                           r == 0, r == 3)
                            last.then_inc(s["y_ok"], 1)
            groups(pe, run)


def final_norm(nc, nrm, stores, X, out):
    with ExitStack() as ctx:
        m = Mem(nc, ctx, "fn")
        xo = m.sb("xo", [P, TC, D])
        block = ctx.enter_context(nc.Block())

        @block.sync
        def _(sp):
            with sp.Fori(0, NC) as c:
                for t in range(TC):
                    nrm.wait(sp, c * TC + t + 1)
                    sp.dma_start(out[bass.ds(c * CH + t * P, P), :], xo[:, t, :])\
                      .then_inc(stores.sems[t], 16)
            for t in range(TC):
                stores.wait(sp, t, NC)

        @block.scalar
        def _(act):
            with act.Fori(0, NC) as c:
                for t in range(TC):
                    nrm.root(act, t, c * TC + t)

        @block.vector
        def _(dve):

            def body(c, first):
                rows = [X[:, bass.ds(c * TC + t, 1), :].rearrange("p o n -> p (o n)") for t in range(TC)]
                for t in range(TC):
                    nrm.mean_and_var(dve, rows[t], t, c * TC + t)
                for t in range(TC):
                    if not first:
                        stores.wait(dve, t, c)
                    nrm.apply(dve, xo[:, t, :], rows[t], t, c * TC + t)

            body(0, True)
            with dve.Fori(1, NC) as c:
                body(c, False)


_INPUTS = ("xT x wqkv0 rope0 rot0 eye masks wo0 gate_w gate_bias lower w_exp wqkv1 qk_bias v_bias rope1 "
           "rot1 wo1 w_mlp").split()


def build(nc, ins, out):
    def dram(name, shape):
        return nc.dram_tensor(name, shape, F32).ap()

    attn_out = dram("attn_out", (S, D))
    weights_t = dram("weights_t", (NE, S))
    x2, y_dram = dram("x2", (S, D)), dram("y1", (S, D))
    q_dram = dram("q1", (2, P, ND, S))
    v_dram = dram("v1", (2, P, NT, D))
    with ExitStack() as ctx:
        nrm = Norm(nc, ctx)
        loads, loads2, stores = Ring(nc, "loads"), Ring(nc, "loads2"), Ring(nc, "stores")
        layer0_attention(nc, loads, ins["xT"], ins["wqkv0"], ins["rope0"], ins["rot0"],
                         ins["eye"], ins["masks"], attn_out)
        loads.stage_over(4, ND * NC // 4)
        hi = ctx.enter_context(nc.sbuf_tensor("hi", [P, ND, S], F32R))
        lo = ctx.enter_context(nc.sbuf_tensor("lo", [P, ND, S], F32R))
        with nc.sbuf_tensor("X", [P, NT, D], F32) as X:
            layer0_project(nc, nrm, loads, loads2, ins["x"], attn_out, ins["wo0"], ins["gate_w"],
                           ins["gate_bias"], ins["lower"], ins["eye"], X, hi, lo, weights_t)
            nrm.stage_over()
            loads.stage_over(TC, NC)
            loads2.stage_over(TC, NC)
            layer0_experts(nc, loads2, ins["w_exp"], weights_t, X, hi, lo)
            loads2.stage_over(2, NE // 2)
            layer1_qkv(nc, nrm, ins["wqkv1"], ins["qk_bias"], ins["v_bias"], ins["rope1"], ins["rot1"],
                       ins["eye"], X, hi, lo, x2, q_dram, v_dram)
            nrm.stage_over()
        layer1_attention(nc, loads, loads2, stores, ins["wo1"], ins["eye"], hi, lo, x2, q_dram, v_dram,
                         y_dram)
        loads.stage_over(2, NT)
        loads2.stage_over(2, NT // 2)
        stores.stage_over(2, NT // 2)
        with nc.sbuf_tensor("X1", [P, NT, D], F32) as X:
            layer1_norm(nc, nrm, loads, y_dram, ins["eye"], X, hi, lo)
            nrm.stage_over()
            loads.stage_over(TC, NC)
            layer1_mlp(nc, loads, ins["w_mlp"], X, hi, lo)
            final_norm(nc, nrm, stores, X, out)


def rotary(dims, freqs, base_rows):
    import numpy as np
    f = freqs[:, None] * np.arange(S, dtype=np.float32)[None, :]
    cos, sin = np.ones((P, S), np.float32), np.zeros((P, S), np.float32)
    swap = np.zeros((P, P), np.float32)
    for b in base_rows:
        for i in range(dims):
            lo, up = b + i, b + dims + i
            cos[lo], sin[lo], cos[up], sin[up] = np.cos(f[i]), np.sin(f[i]), np.cos(f[i]), np.sin(f[i])
            swap[up, lo], swap[lo, up] = -1.0, 1.0
    return np.stack([cos, sin]), swap


def layout(inputs):
    import numpy as np
    a = {k: np.asarray(v) for k, v in inputs.items()}
    x = a["L0_attn_x"].reshape(S, D)

    def turned(w, n):
        return w.T.reshape(-1, P, n).transpose(1, 0, 2)

    half = HD0 // 2
    order = np.concatenate([np.r_[h * half:(h + 1) * half, H0 * half + h * half:H0 * half + (h + 1) * half]
                            for h in range(H0)])
    q0 = np.concatenate([a["L0_attn_Wq_sem"], a["L0_attn_Wq_geo"]])[order]
    k0 = np.concatenate([a["L0_attn_Wk_sem"], a["L0_attn_Wk_geo"]])[order]
    qkv0 = np.stack([w.reshape(NG, P, ND, P).transpose(0, 3, 2, 1) for w in (q0, k0, a["L0_attn_Wv"])], 2)
    freqs0 = (1.0 / np.float32(10000.0) ** (np.arange(0, half, 2, dtype=np.float32) / np.float32(half)))
    rope0, rot0 = rotary(half // 2, freqs0.astype(np.float32), [h * HD0 + half for h in range(GH)])
    freqs1 = (1.0 / np.float32(10000.0) ** (np.arange(0, 64, dtype=np.float32) / np.float32(64)))
    rope1, rot1 = rotary(64, freqs1.astype(np.float32), [0])
    i = np.arange(P)
    hidden = i[None, :] > i[:, None]
    masks = np.stack([np.where(hidden, np.float32(BIG), np.float32(0)),
                      np.where(hidden.T, np.float32(BIG), np.float32(0))], 1).astype(np.float32)
    lower = (np.arange(NE)[None, :] < np.arange(NE)[:, None]).astype(np.float32).reshape(-1)

    def expert(w1, w3, w2):
        return np.concatenate([turned(w1, HID).reshape(P, -1), turned(w3, HID).reshape(P, -1),
                               turned(w2, D).reshape(P, -1)], 1)

    w_exp = np.stack([expert(a["L0_ffn_sw1"], a["L0_ffn_sw3"], a["L0_ffn_sw2"])] +
                     [expert(a["L0_ffn_w1"][e], a["L0_ffn_w3"][e], a["L0_ffn_w2"][e]) for e in range(NE)])
    qw, kvw = a["L1_attn_q_w"], a["L1_attn_kv_w"]
    qkv1 = np.stack([turned(w, D) for w in (qw, kvw[:D], kvw[D:])])
    kvb = a["L1_attn_kv_b"]
    qk_bias = np.stack([a["L1_attn_q_b"].reshape(ND, P).T, kvb[:D].reshape(ND, P).T], 1)

    def up(w):
        return w.reshape(ND, P, NQ, P, 4).transpose(2, 4, 1, 0, 3).reshape(NQ, 4, P, ND * P)

    gate_up = np.concatenate([up(a["L1_ffn_w_gate"]), up(a["L1_ffn_w_up"])], 3)
    down = a["L1_ffn_w_down"].reshape(NQ, P, 2, 2 * D).transpose(0, 2, 1, 3)
    laid = dict(xT=x.T, x=x, wqkv0=qkv0, rope0=rope0, rot0=rot0, eye=np.eye(P, dtype=np.float32),
                masks=masks, wo0=turned(a["L0_attn_Wo"], D), gate_w=turned(a["L0_ffn_gate_w"], NE),
                gate_bias=a["L0_ffn_expert_bias"], lower=lower, w_exp=w_exp, wqkv1=qkv1,
                qk_bias=qk_bias, v_bias=kvb[D:], rope1=rope1, rot1=rot1, wo1=turned(a["L1_attn_o_w"], D),
                w_mlp=np.concatenate([gate_up, down], 1))
    return {k: np.ascontiguousarray(v) for k, v in laid.items()}


def kernel(**inputs):
    import numpy as np
    import concourse.bacc as bacc
    from concourse.bass_utils import run_bass_kernel_spmd as run

    laid = layout(inputs)
    nc = bacc.Bacc("TRN2", target_bir_lowering=False, num_devices=1)
    ins = {n: nc.dram_tensor(f"in_{n}", laid[n].shape, mybir.dt.from_np(laid[n].dtype),
                             kind="ExternalInput").ap() for n in _INPUTS}
    out = nc.dram_tensor("out", (S, D), F32, kind="ExternalOutput").ap()
    build(nc, ins, out)
    r = run(nc, [{f"in_{n}": laid[n] for n in _INPUTS}], core_ids=[0])
    return r.results[0]["out"].reshape(1, S, D)
```

```python
import concourse.bass as bass
from concourse import mybir
from concourse.alu_op_type import AluOpType as ALU
from contextlib import ExitStack

F32 = mybir.dt.float32
F32R = mybir.dt.float32r
BF16 = mybir.dt.bfloat16
ACT = mybir.ActivationFunctionType
AX = mybir.AxisListType.X

P = 128
S = 2048
D = 512
ND = D // P
CH = 512
NC = S // CH
TC = CH // P
NT = S // P
EPS = 1e-5

H0, HD0 = 16, 32
GH = P // HD0
NG = H0 // GH
SCALE0 = float(HD0) ** -0.5
BIG = -float(2 ** 100)

NE, HID = 8, 256
NJ = HID // P
EW = ND * HID * 2 + NJ * D

SCALE1 = 128.0 ** -0.5

INTER = 2048
NQ = INTER // (4 * P)


def mm3(nc, out, wh, wl, xh, xl, start=True, stop=True):
    nc.tensor.matmul(out, wh, xh, start=start, stop=False, skip_group_check=True)
    nc.tensor.matmul(out, wh, xl, start=False, stop=False, skip_group_check=True)
    return nc.tensor.matmul(out, wl, xh, start=False, stop=stop, skip_group_check=True)


def f32(ap):
    return ap.bitcast(F32)


class Mem:

    def __init__(self, nc, ctx, stage):
        self.nc, self.ctx, self.stage = nc, ctx, stage

    def sb(self, name, shape, dt=F32):
        return self.ctx.enter_context(self.nc.sbuf_tensor(f"{self.stage}_{name}", shape, dt))

    def ps(self, name, shape):
        return self.ctx.enter_context(self.nc.psum_tensor(f"{self.stage}_{name}", shape, F32))

    def sem(self, name):
        return self.nc.alloc_semaphore(name=f"{self.stage}_{name}")


class Ring:

    def __init__(self, nc, name):
        self.sems = [nc.alloc_semaphore(name=f"{name}{i}") for i in range(TC)]
        self.before = [0] * TC

    def wait(self, eng, buf, k):
        eng.wait_ge(self.sems[buf], 16 * (self.before[buf] + k))

    def wait_turn(self, eng, buf, n, each=1):
        eng.wait_ge(self.sems[buf], 16 * self.before[buf] + 8 * each * (n - buf) + 16 * each)

    def stage_over(self, bufs, k):
        for i in range(bufs):
            self.before[i] += k


def wait_alone(eng, sem, value, held, at_least):
    if not isinstance(value, int):
        eng.compute_val(value)
    eng.wait_ge(held, at_least)
    eng.wait_ge(sem, value)


def attention0_plan():
    steps = [(c, p, kt) for c in range(NC) for p in range(2) for kt in range(TC * (c + 1))]
    items = [(c, p) for c in range(NC) for p in range(2)]
    units = [[(h, t, u) for h in range(2) for t in range(TC) for u in range(c + 1)] for c, p in items]
    first_step = [steps.index((c, p, 0)) for c, p in items]

    def proj(d, c):
        return [("queries", d, c), ("rotate", d, c), ("values", d, c), ("addrot", d, c), ("split", d, c)]

    def unit_list(d, n):
        return [("unit", d, n, i) for i in range(len(units[n]))]

    before = ([("x", 0, 0), ("x", 0, 1)] + proj(0, 0) + [("x", 0, 2), ("x", 0, 3)] + proj(0, 1)[:4] +
              unit_list(0, 0) + [("max", 0, 0), ("split", 0, 1), ("shift", 0, 0)] + unit_list(0, 1))

    def iteration(more):
        side, held = [[] for _ in range(3 * len(steps))], set()

        def at(name, d, which, k, empties=0):
            side[int(3 * k)].append((name, d, which))
            held.update(range(int(3 * k), int(3 * k) + empties))

        def spread(work, start, stop):
            gaps = [g for g in range(int(3 * start), int(3 * stop)) if g not in held]
            for i, ev in enumerate(work):
                side[gaps[len(gaps) * i // len(work)]].append(ev)

        def project(d, c, queries, rotate, addrot, split, values):
            at("queries", d, c, queries, 3)
            at("rotate", d, c, rotate, 3)
            at("addrot", d, c, addrot)
            at("split", d, c, split)
            at("values", d, c, values)

        project(0, 2, 3.4, 5.4, 6.4, 8.4, 4.4)
        project(0, 3, 15.4, 17.4, 18.4, 19.4, 16.4)
        if more:
            project(1, 0, 63.4, 65.1, 66.1, 68.4, 69.0)
            project(1, 1, 70.0, 71.7, 72.7, 79.0, 73.4)
        work = ((1, 0, 0), (2, 0.4, 5.0), (3, 5.4, 11.0), (4, 12.4, 19.7), (5, 20.0, 29.0),
                (6, 29.4, 43.4), (7, 43.7, 58.0))
        for n, start, stop in work:
            at("max", 0, n, stop)
            at("shift", 0, n, stop + 0.7, 2)
        for n, start, stop in work[1:]:
            spread(unit_list(0, n), start, stop)
        if more:
            at("max", 1, 0, 77.4)
            at("shift", 1, 0, 78.0, 1)
            spread(unit_list(1, 0), 74.4, 77.4)
            spread(unit_list(1, 1), 77.4, 80.0)
        events = []
        for k, (c, p, kt) in enumerate(steps):
            n = items.index((c, p))
            events.append(("step", 0, n, k))
            events += side[3 * k]
            if k > 0:
                events.append(("probs", 0, k - 1, 0))
            events += side[3 * k + 1]
            if k > 0:
                events.append(("probs", 0, k - 1, 1))
            if n > 0 and kt == 0:
                events.append(("out", 0, n - 1))
            if n > 0 and kt == 2:
                events.append(("turn", 0, n - 1))
            events += side[3 * k + 2]
        last = len(items) - 1
        events += [("probs", 0, len(steps) - 1, 0), ("probs", 0, len(steps) - 1, 1), ("out", 0, last)]
        return events + [("turn", 0, last)]

    return steps, items, units, first_step, before, iteration(True), iteration(False)


def layer0_attention(nc, loads, xT, wqkv, rope, rot, eye, masks, attn_out):
    steps, items, units, first_step, before, middle, final = attention0_plan()
    first_unit = [sum(len(u) for u in units[:n]) for n in range(len(items))]
    NS, NU, NI = len(steps), sum(map(len, units)), len(items)
    NDMA = 2 * 3 * 2
    QSLOT = (0, 1, 0, 2)

    with ExitStack() as ctx:
        m = Mem(nc, ctx, "a0")
        xh = m.sb("xh", [P, ND, S], F32R)
        xl = m.sb("xl", [P, ND, S], F32R)
        cos = m.sb("cos", [P, S])
        sin = m.sb("sin", [P, S])
        kst = m.sb("kst", [P, GH, S], F32R)
        qst = m.sb("qst", [P, 3, GH, CH], F32R)
        vaug = m.sb("vaug", [P, NT, GH, 2 * HD0])
        wst = m.sb("wst", [P, 3, ND, P])
        wh = m.sb("wh", [P, 3, ND, P], F32R)
        wl = m.sb("wl", [P, 3, ND, P], F32R)
        probs = m.sb("probs", [P, 2, 2, CH])
        qkf = m.sb("qkf", [P, 2, CH])
        t1 = m.sb("t1", [P, 2, CH])
        t2 = m.sb("t2", [P, 2, CH])
        hl = m.sb("hl", [P, 2, 2, CH], F32R)
        avs = m.sb("avs", [P, CH])
        osb = m.sb("osb", [P, 2, TC, 2 * HD0])
        rec = m.sb("rec", [P, TC * 2])
        rotf = m.sb("rotf", [P, P])
        identr = m.sb("identr", [P, P], F32R)
        maskr = m.sb("maskr", [P, 2, P], F32R)
        mparts = m.sb("mparts", [P, 2, 2, TC, NC])
        nm = m.sb("nm", [P, 2, TC])
        mt = m.sb("mt", [P, 2, TC, 98], F32R)
        xst = probs
        ident_in, masks_in = t2[:, 0, 0:P], t2[:, 1, 0:2 * P].rearrange("p (a n) -> p a n", a=2)
        sbank = m.ps("sbank", [P, 2, CH])
        stb = m.ps("stb", [P, 2, 2, CH])
        avb = m.ps("avb", [P, CH])
        misc = m.ps("misc", [P, CH])

        names = ("consts rope_load cready xhi xlo wload_first wload wsplit_hi wsplit projqk projv projr qkf_ok v_ok "
                 "t1_ok t2_ok sum_ok hi_ok lo_ok stacked0 stacked1 unit_ok unit_max nm_ok mh_ok mt_ok turned "
                 "shifted st_ok exp_ok av_ok avs_ok avt_ok rec_ok out_ok inits mt_zero stored0 stored1").split()
        s = {k: m.sem(k) for k in names}
        stacked = (s["stacked0"], s["stacked1"])
        stored = (s["stored0"], s["stored1"])
        block = ctx.enter_context(nc.Block())

        def groups(eng, run):
            run(0, before)
            with eng.Fori(0, NG - 1) as g:
                run(g, middle)
            run(NG - 1, final)

        @block.sync
        def _(sp):
            for i in range(ND * NC):
                if i >= 4:
                    sp.wait_ge(s["xlo"], i - 3)
                d, c = i % ND, i // ND
                sp.dma_start(xst[:, i // 2 % 2, i % 2, :], xT[d * P:(d + 1) * P, c * CH:(c + 1) * CH])\
                  .then_inc(loads.sems[i % 4], 16)

            def run(g, events):
                for ev in events:
                    gd = g + ev[1]
                    if ev[0] == "split":
                        c = ev[2]
                        wait_alone(sp, s["lo_ok"], gd * NC + c + 1, s["xlo"], 1)
                        if ev[1]:
                            sp.wait_ge(s["st_ok"], g * NS + first_step[NI - 1] + (c + 1) * TC)
                        elif c == 2:
                            sp.wait_ge(s["st_ok"], g * NS + first_step[2])
                        for h in range(GH):
                            rows = slice(h * HD0, (h + 1) * HD0)
                            for r, (qp, kp) in enumerate(((0, 0), (0, 1), (1, 0))):
                                to = slice(r * HD0, (r + 1) * HD0)
                                sp.dma_start(f32(qst[to, QSLOT[c], h, :]), f32(hl[rows, qp, 0, :]))\
                                  .then_inc(stacked[h // 2], 16)
                                sp.dma_start(f32(kst[to, h, c * CH:(c + 1) * CH]), f32(hl[rows, kp, 1, :]))\
                                  .then_inc(stacked[h // 2], 16)

            groups(sp, run)

        @block.gpsimd
        def _(pool):
            def split_weights(g):
                wait_alone(pool, s["wload"], g * 16, s["wload"], 16)
                nc.gpsimd.tensor_copy(wh[:], wst[:]).then_inc(s["wsplit_hi"], 1)
                pool.wait_ge(s["wsplit_hi"], g + 1)
                nc.gpsimd.tensor_tensor(wl[:], wst[:], f32(wh[:]), ALU.subtract).then_inc(s["wsplit"], 1)

            nc.gpsimd.memset(kst[96:128, :, :].bitcast(F32), 0.0).then_inc(s["inits"], 1)
            pool.wait_ge(s["inits"], 1)
            nc.gpsimd.memset(kst[96:98, :, :].bitcast(F32), 1.0).then_inc(s["inits"], 1)
            pool.wait_ge(s["inits"], 2)
            nc.gpsimd.memset(qst[96:128, :, :, :].bitcast(F32), 0.0).then_inc(s["inits"], 1)
            pool.wait_ge(s["inits"], 3)

            def run(g, events):
                for ev in events:
                    if ev[0] == "rotate":
                        k = (g + ev[1]) * NC + ev[2]
                        c = ev[2]
                        pool.wait_ge(s["qkf_ok"], k + 1)
                        if events is not before or c > 0:
                            pool.wait_ge(s["lo_ok"], k)
                        nc.gpsimd.tensor_tensor(
                            t1[:], qkf[:], cos[:, c * CH:(c + 1) * CH].unsqueeze(1).broadcast_to([P, 2, CH]),
                            ALU.mult).then_inc(s["t1_ok"], 1)
                        if c == NC - 1 and events is middle:
                            pool.wait_ge(s["projv"], (g + 1) * NC)
                            split_weights(g + 1)
                    elif ev[0] == "turn":
                        n = ev[2]
                        c, p = items[n]
                        pool.wait_ge(s["out_ok"], g * NI + n + 1)
                        dst = attn_out[c * CH:(c + 1) * CH,
                                       bass.ds(g * P + p * 2 * HD0, 2 * HD0)]
                        pool.dma_start(dst.rearrange("(t q) d -> q t d", q=P), osb[:, n % 2, :, :])\
                            .then_inc(stored[n % 2], 16)
                    elif ev[0] == "step" and ev[3] == 0 and events is middle:
                        pool.wait_ge(s["wsplit"], g + 1)
                        pool.dma_start(wst[:], wqkv[bass.ds(g + 1, 1)].rearrange("o p a d n -> (o p) a d n"))\
                            .then_inc(s["wload"], 16)

            pool.wait_ge(s["rope_load"], 32)
            groups(pool, run)
            for b in range(2):
                pool.wait_ge(stored[b], 16 * (NG * NI // 2))

        @block.scalar
        def _(act):
            act.dma_start(wst[:], wqkv[0]).then_inc(s["wload_first"], 16)
            for dst, src in ((ident_in, eye), (masks_in, masks), (rotf[:], rot)):
                act.dma_start(dst, src).then_inc(s["consts"], 16)
            for dst, src in ((cos, rope[0]), (sin, rope[1])):
                act.dma_start(dst[:], src).then_inc(s["rope_load"], 16)
            act.wait_ge(s["wload_first"], 16)
            nc.scalar.activation(wh[:], wst[:], ACT.Copy).then_inc(s["wsplit_hi"], 1)

            def run(g, events):
                for ev in events:
                    gd = g + ev[1]
                    if ev[0] == "x":
                        c = ev[2]
                        for d in range(ND):
                            i = c * ND + d
                            loads.wait(act, i % 4, i // 4 + 1)
                            nc.scalar.activation(xh[:, d, c * CH:(c + 1) * CH], xst[:, i // 2 % 2, i % 2, :],
                                                 ACT.Copy).then_inc(s["xhi"], 1)
                        if c == 0:
                            act.wait_ge(s["consts"], 48)
                            nc.scalar.activation(identr[:], ident_in, ACT.Copy).then_inc(s["cready"], 1)
                            nc.scalar.activation(maskr[:], masks_in, ACT.Copy).then_inc(s["cready"], 1)
                    elif ev[0] == "queries":
                        c = ev[2]
                        act.wait_ge(s["projqk"], gd * NC + c + 1)
                        nc.scalar.activation(qkf[:], sbank[:], ACT.Copy).then_inc(s["qkf_ok"], 1)
                    elif ev[0] == "values":
                        c = ev[2]
                        act.wait_ge(s["projv"], gd * NC + c + 1)
                        nc.scalar.activation(
                            vaug[:, c * TC:(c + 1) * TC, :, 0:HD0],
                            misc[:].rearrange("p (t h d) -> p t h d", t=TC, h=GH), ACT.Copy)\
                            .then_inc(s["v_ok"], 1)
                    elif ev[0] == "split":
                        c = ev[2]
                        act.wait_ge(s["sum_ok"], gd * NC + c + 1)
                        if events is not before or c > 0:
                            for sem in stacked:
                                act.wait_ge(sem, (gd * NC + c) * NDMA * 16)
                        nc.scalar.activation(hl[:, 0, :, :], t1[:], ACT.Copy).then_inc(s["hi_ok"], 1)
                    elif ev[0] == "shift":
                        n = ev[2]
                        c, p = items[n]
                        if events is before:
                            act.wait_ge(s["inits"], 3)
                        for h in range(2):
                            act.wait_ge(s["turned"], gd * 2 * NI + 2 * n + h + 1)
                            nc.scalar.activation(qst[96:98, QSLOT[c], 2 * p + h, :], sbank[96:98, h, :],
                                                 ACT.Copy).then_inc(s["shifted"], 1)
                    elif ev[0] == "step":
                        i = ev[3]
                        c, p, kt = steps[i]
                        w0 = max(0, kt - TC * c) * P
                        act.wait_ge(s["st_ok"], gd * NS + i + 1)
                        if i >= 2:
                            act.wait_ge(s["av_ok"], gd * NS + i - 1)
                        nc.scalar.activation(probs[:, i % 2, :, w0:], stb[:, i % 2, :, w0:], ACT.Exp,
                                             scale=SCALE0).then_inc(s["exp_ok"], 1)
                    elif ev[0] == "out":
                        n = ev[2]
                        act.wait_ge(s["av_ok"], gd * NS + first_step[n] + TC * (items[n][0] + 1))
                        nc.scalar.activation(avs[:], avb[:], ACT.Copy).then_inc(s["avs_ok"], 1)

            groups(act, run)

        @block.vector
        def _(dve):
            nc.vector.memset(mt[:].bitcast(F32), 0.0).then_inc(s["mt_zero"], 1)
            nc.vector.memset(vaug[:, :, :, HD0:2 * HD0], 1.0).then_inc(s["mt_zero"], 1)
            dve.wait_ge(s["mt_zero"], 2)
            dve.wait_ge(s["wsplit_hi"], 1)
            nc.vector.tensor_tensor(wl[:], wst[:], f32(wh[:]), ALU.subtract).then_inc(s["wsplit"], 1)

            def run(g, events):
                for ev in events:
                    gd = g + ev[1]
                    if ev[0] == "x":
                        c = ev[2]
                        for d in range(ND):
                            i = c * ND + d
                            dve.wait_ge(s["xhi"], i + 1)
                            nc.vector.tensor_tensor(xl[:, d, c * CH:(c + 1) * CH], xst[:, i // 2 % 2, i % 2, :],
                                                    f32(xh[:, d, c * CH:(c + 1) * CH]), ALU.subtract)\
                                .then_inc(s["xlo"], 1)
                    elif ev[0] == "rotate":
                        c = ev[2]
                        if events is before and c == 0:
                            dve.wait_ge(s["cready"], 2)
                            dve.wait_ge(s["rope_load"], 32)
                        dve.wait_ge(s["projr"], gd * NC + c + 1)
                        nc.vector.tensor_tensor(
                            t2[:], sbank[:], sin[:, c * CH:(c + 1) * CH].unsqueeze(1).broadcast_to([P, 2, CH]),
                            ALU.mult).then_inc(s["t2_ok"], 1)
                    elif ev[0] == "addrot":
                        c = ev[2]
                        dve.wait_ge(s["t2_ok"], gd * NC + c + 1)
                        dve.wait_ge(s["t1_ok"], gd * NC + c + 1)
                        nc.vector.tensor_tensor(t1[:], t1[:], t2[:], ALU.add).then_inc(s["sum_ok"], 1)
                    elif ev[0] == "split":
                        c = ev[2]
                        dve.wait_ge(s["hi_ok"], gd * NC + c + 1)
                        nc.vector.tensor_tensor(hl[:, 1, :, :], t1[:], f32(hl[:, 0, :, :]),
                                                ALU.subtract).then_inc(s["lo_ok"], 1)
                    elif ev[0] == "unit":
                        n, i = ev[2:]
                        c, _ = items[n]
                        h, t, u = units[n][i]
                        w = CH if u < c else (t + 1) * P
                        dve.wait_ge(s["unit_ok"], gd * NU + first_unit[n] + i + 1)
                        nc.vector.reduce_max(mparts[:, n % 2, h, t, u:u + 1], sbank[:, i % 2, 0:w], AX)\
                            .then_inc(s["unit_max"], 1)
                    elif ev[0] == "max":
                        n = ev[2]
                        c, _ = items[n]
                        dve.wait_ge(s["unit_max"], gd * NU + first_unit[n] + len(units[n]))
                        nc.vector.tensor_reduce(nm[:], mparts[:, n % 2, :, :, 0:c + 1], AX, ALU.max,
                                                negate=True).then_inc(s["nm_ok"], 1)
                        dve.wait_ge(s["nm_ok"], gd * NI + n + 1)
                        if events is not before:
                            dve.wait_ge(s["turned"], gd * 2 * NI + 2 * n)
                        nc.vector.tensor_copy(mt[:, :, :, 96], nm[:]).then_inc(s["mh_ok"], 1)
                        dve.wait_ge(s["mh_ok"], gd * NI + n + 1)
                        nc.vector.tensor_tensor(mt[:, :, :, 97], nm[:], f32(mt[:, :, :, 96]),
                                                ALU.subtract).then_inc(s["mt_ok"], 1)
                    elif ev[0] == "turn":
                        n = ev[2]
                        tv = misc[:].rearrange("p (a b) -> p a b", b=2 * HD0)
                        dve.wait_ge(s["avt_ok"], gd * NI + n + 1)
                        nc.vector.reciprocal(rec[:], tv[:, :, HD0]).then_inc(s["rec_ok"], 1)
                        dve.wait_ge(s["rec_ok"], gd * NI + n + 1)
                        if n >= 2:
                            dve.wait_ge(stored[n % 2], 16 * (gd * (NI // 2) + n // 2))
                        nc.vector.tensor_tensor(
                            osb[:, n % 2, :, :].rearrange("p t (h d) -> p (t h) d", h=2),
                            tv[:, :, 0:HD0],
                            rec[:].unsqueeze(2).broadcast_to([P, TC * 2, HD0]),
                            ALU.mult).then_inc(s["out_ok"], 1)
                        if n == NI - 1:
                            for b in range(2):
                                dve.wait_ge(stored[b], 16 * ((gd + 1) * (NI // 2)))

            groups(dve, run)

        @block.tensor
        def _(pe):
            def run(g, events):
                if events is before:
                    bank, values_bank = [None, None], None
                else:
                    at = g * NU + first_unit[1] + len(units[1])
                    bank = [("unit_max", at - 1), ("unit_max", at)]
                    values_bank = ("v_ok", g * NC + 2)

                def free(held):
                    if held is not None:
                        pe.wait_ge(s[held[0]], held[1])

                for ev in events:
                    gd = g + ev[1]
                    if ev[0] == "queries":
                        c = ev[2]
                        cs = slice(c * CH, (c + 1) * CH)
                        if c == 0:
                            pe.wait_ge(s["wsplit"], gd + 1)
                        if events is before:
                            pe.wait_ge(s["xlo"], ND * (c + 1))
                        free(bank[0])
                        free(bank[1])
                        for a in range(2):
                            for d in range(ND):
                                last = mm3(nc, sbank[:, a, :], wh[:, a, d, :], wl[:, a, d, :],
                                           xh[:, d, cs], xl[:, d, cs], d == 0, d == ND - 1)
                        last.then_inc(s["projqk"], 1)
                        bank = [("qkf_ok", gd * NC + c + 1)] * 2
                    elif ev[0] == "values":
                        c = ev[2]
                        free(values_bank)
                        for t in range(TC):
                            ts = slice(c * CH + t * P, c * CH + (t + 1) * P)
                            for d in range(ND):
                                last = mm3(nc, misc[:, t * P:(t + 1) * P], xh[:, d, ts], xl[:, d, ts],
                                           wh[:, 2, d, :], wl[:, 2, d, :], d == 0, d == ND - 1)
                        last.then_inc(s["projv"], 1)
                        values_bank = ("v_ok", gd * NC + c + 1)
                    elif ev[0] == "rotate":
                        c = ev[2]
                        if events is before and c == 0:
                            pe.wait_ge(s["cready"], 2)
                        pe.wait_ge(s["qkf_ok"], gd * NC + c + 1)
                        free(bank[0])
                        free(bank[1])
                        for a in range(2):
                            last = nc.tensor.matmul(sbank[:, a, :], rotf[:], qkf[:, a, :],
                                                    start=True, stop=True)
                        last.then_inc(s["projr"], 1)
                        bank = [("t2_ok", gd * NC + c + 1)] * 2
                    elif ev[0] == "unit":
                        n, i = ev[2:]
                        c, p = items[n]
                        h, t, u = units[n][i]
                        w = CH if u < c else (t + 1) * P
                        k = gd * NU + first_unit[n] + i
                        if i == 0:
                            pe.wait_ge(stacked[p], (gd * NC + c + 1) * NDMA * 16)
                        free(bank[i % 2])
                        last = nc.tensor.matmul(sbank[:, i % 2, 0:w],
                                                qst[0:96, QSLOT[c], 2 * p + h, t * P:(t + 1) * P],
                                                kst[0:96, 2 * p + h, u * CH:u * CH + w],
                                                start=True, stop=u < c)
                        if u == c:
                            last = nc.tensor.matmul(sbank[:, i % 2, t * P:w], identr[:], maskr[:, 0, :],
                                                    start=False, stop=True)
                        last.then_inc(s["unit_ok"], 1)
                        bank[i % 2] = ("unit_max", k + 1)
                    elif ev[0] == "shift":
                        n = ev[2]
                        pe.wait_ge(s["mt_ok"], gd * NI + n + 1)
                        for h in range(2):
                            free(bank[h])
                            for t in range(TC):
                                last = nc.tensor.transpose(sbank[0:98, h, t * P:(t + 1) * P],
                                                           f32(mt[:, h, t, :]), f32(identr[:]))
                            last.then_inc(s["turned"], 1)
                            bank[h] = ("shifted", gd * 2 * NI + 2 * n + h + 1)
                    elif ev[0] == "step":
                        n, i = ev[2:]
                        c, p, kt = steps[i]
                        w0 = max(0, kt - TC * c) * P
                        if kt == 0:
                            pe.wait_ge(s["shifted"], gd * 2 * NI + 2 * n + 2)
                        if i >= 2:
                            pe.wait_ge(s["exp_ok"], gd * NS + i - 1)
                        for h in range(2):
                            last = nc.tensor.matmul(stb[:, i % 2, h, w0:],
                                                    kst[:, 2 * p + h, kt * P:(kt + 1) * P],
                                                    qst[:, QSLOT[c], 2 * p + h, w0:],
                                                    start=True, stop=kt < TC * c)
                            if kt >= TC * c:
                                last = nc.tensor.matmul(stb[:, i % 2, h, w0:w0 + P], identr[:],
                                                        maskr[:, 1, :], start=False, stop=True)
                        last.then_inc(s["st_ok"], 1)
                    elif ev[0] == "probs":
                        i, h = ev[2:]
                        c, p, kt = steps[i]
                        w0 = max(0, kt - TC * c) * P
                        if h == 0:
                            pe.wait_ge(s["exp_ok"], g * NS + i + 1)
                            if kt == 0:
                                pe.wait_ge(s["v_ok"], g * NC + c + 1)
                                if c + p > 0:
                                    pe.wait_ge(s["avs_ok"], g * NI + items.index((c, p)))
                        last = nc.tensor.matmul(avb[64 * h:64 * h + 64, w0:], vaug[:, kt, 2 * p + h, :],
                                                probs[:, i % 2, h, w0:], start=kt == 0,
                                                stop=kt == TC * (c + 1) - 1, tile_position=(0, 64 * h),
                                                skip_group_check=True)
                        if h == 1:
                            last.then_inc(s["av_ok"], 1)
                    elif ev[0] == "turn":
                        n = ev[2]
                        pe.wait_ge(s["avs_ok"], gd * NI + n + 1)
                        free(values_bank)
                        for t in range(TC):
                            last = nc.tensor.transpose(misc[:, t * P:(t + 1) * P],
                                                       avs[:, t * P:(t + 1) * P], f32(identr[:]))
                        last.then_inc(s["avt_ok"], 1)
                        values_bank = ("out_ok", gd * NI + n + 1)
                if events is before:
                    pe.wait_ge(s["xlo"], ND * NC)
                    pe.wait_ge(s["inits"], 3)
                    pe.wait_ge(s["mt_zero"], 2)
                else:
                    free(values_bank)

            groups(pe, run)


class Norm:
    def __init__(self, nc, ctx):
        m = Mem(nc, ctx, "norm")
        self.nc, self.before = nc, 0
        self.stats = m.sb("stats", [P, TC, 6])
        self.mv = m.sb("mv", [P, TC, 2])
        self.std = m.sb("std", [P, TC])
        self.rstd = m.sb("rstd", [P, TC])
        self.eps = m.sb("eps", [P, 1])
        self.eps_ok, self.stats_ok, self.mv_ok, self.std_ok, self.rstd_ok, self.done = (
            m.sem(x) for x in ("eps_ok", "stats_ok", "mv_ok", "std_ok", "rstd_ok", "norm_done"))

    def init(self, dve):
        self.nc.vector.memset(self.eps[:], EPS).then_inc(self.eps_ok, 1)
        dve.wait_ge(self.eps_ok, 1)

    def stage_over(self):
        self.before += NT

    def mean_and_var(self, dve, src, t, k):
        self.nc.vector.bn_stats(self.stats[:, t, :], src).then_inc(self.stats_ok, 1)
        wait_alone(dve, self.stats_ok, self.before + k + 1, self.eps_ok, 1)
        self.nc.vector.bn_aggr(self.mv[:, t, :], self.stats[:, t, :]).then_inc(self.mv_ok, 1)

    def root(self, act, t, k):
        act.wait_ge(self.mv_ok, self.before + k + 1)
        self.nc.scalar.activation(self.std[:, t:t + 1], self.mv[:, t, 1:2], ACT.Sqrt,
                                  bias=self.eps[:]).then_inc(self.std_ok, 1)

    def apply(self, dve, dst, src, t, k):
        dve.wait_ge(self.std_ok, self.before + k + 1)
        self.nc.vector.reciprocal(self.rstd[:, t:t + 1], self.std[:, t:t + 1]).then_inc(self.rstd_ok, 1)
        dve.wait_ge(self.rstd_ok, self.before + k + 1)
        self.nc.vector.tensor_scalar(dst, src, self.mv[:, t, 0:1], self.rstd[:, t:t + 1],
                                     ALU.subtract, ALU.mult).then_inc(self.done, 1)

    def wait(self, eng, k):
        eng.wait_ge(self.done, self.before + k)


def layer0_project(nc, nrm, loads, loads2, x_in, attn_out, wo, gate_w, bias, lower, eye, w_exp, X, xh, xl,
                   w0h, w0l, weights_t):
    with ExitStack() as ctx:
        m = Mem(nc, ctx, "p0")
        wst = m.sb("wst", [P, ND, D])
        woh = m.sb("woh", [P, ND, D], F32R)
        wol = m.sb("wol", [P, ND, D], F32R)
        gst = m.sb("gst", [P, ND, NE])
        gh = m.sb("gh", [P, ND, NE], F32R)
        gl = m.sb("gl", [P, ND, NE], F32R)
        ident = m.sb("ident", [P, P])
        low = m.sb("low", [P, NE * NE])
        brow = m.sb("brow", [P, NE])
        oin = m.sb("oin", [P, TC, D])
        xin = m.sb("xin", [P, TC, D])
        oth = m.sb("oth", [P, 2, ND, P], F32R)
        otl = m.sb("otl", [P, 2, ND, P], F32R)
        y = m.sb("y", [P, TC, D])
        xn = m.sb("xn", [P, TC, D])
        gsb = m.sb("gsb", [NE, CH])
        sig = m.sb("sig", [P, TC, NE])
        val = m.sb("val", [P, TC, NE])
        gt = m.sb("gt", [P, TC, NE * NE])
        eq = m.sb("eq", [P, TC, NE * NE])
        rank = m.sb("rank", [P, TC, NE])
        sm = m.sb("sm", [P, TC, NE])
        smt = m.sb("smt", [NE, CH])
        ta = m.ps("ta", [P, 2, ND * P])
        yb = m.ps("yb", [P, 2, D])
        tb = m.ps("tb", [P, 2, ND * P])
        gb = m.ps("gb", [P, CH])
        sb8 = m.ps("sb8", [P, CH])
        names = ("consts w_hi w_lo ot_ok oh_ok ol_ok y_ok sum_ok xt_ok xh_ok xl_ok copied "
                 "g_ok gsb_ok gt_ok sig_ok val_ok cmp_ok eqm_ok add_ok rank_ok sm_ok smt_ok smts_ok stored w0load w0hi w0lo").split()
        s = {k: m.sem(k) for k in names}
        block = ctx.enter_context(nc.Block())

        def chunk(first, last):
            before = not first
            ev = [("o", 1, 0), ("w", 0, 0)] + [("b", 3, -1)] * before + [("o", 2, 0), ("w", 1, 0)]
            ev += [("gates", 0, -1)] * before + [("b", 0, 0), ("o", 3, 0), ("w", 2, 0)]
            ev += [("ranks", 0, -1)] * before + [("b", 1, 0)] + [("o", 0, 1)] * (not last) + [("w", 3, 0)]
            return ev + [("b", 2, 0)] + [("weights", 0, -1)] * before

        def chunks(eng, run):
            run(0, [("o", 0, 0)] + chunk(True, False), True)
            with eng.Fori(1, NC - 1) as c:
                run(c, chunk(False, False), False)
            run(NC - 1, chunk(False, True), False)
            run(NC - 1, [("b", 3, 0), ("gates", 0, 0), ("ranks", 0, 0), ("weights", 0, 0)], False)

        @block.sync
        def _(sp):
            sp.dma_start(wst[:], wo).then_inc(s["consts"], 16)
            sp.dma_start(gst[:], gate_w).then_inc(s["consts"], 16)
            sp.dma_start(ident[:], eye).then_inc(s["consts"], 16)
            sp.dma_start(low[:], lower.partition_broadcast(P)).then_inc(s["consts"], 16)
            sp.dma_start(brow[:], bias.partition_broadcast(P)).then_inc(s["consts"], 16)

            def store(c):
                sp.wait_ge(s["smts_ok"], c + 1)
                sp.dma_start(weights_t[:, bass.ds(c * CH, CH)], smt[:]).then_inc(s["stored"], 16)

            def body(c, first, ready):
                for t in range(TC):
                    rows = bass.ds(c * CH + t * P, P)
                    if not first:
                        sp.wait_ge(s["ot_ok"], c * TC - TC + t + 1)
                    sp.dma_start(oin[:, t, :], attn_out[rows, :]).then_inc(loads.sems[t], 16)
                    if not first:
                        sp.wait_ge(s["sum_ok"], c * TC - TC + t + 1)
                    sp.dma_start(xin[:, t, :], x_in[rows, :]).then_inc(loads2.sems[t], 16)
                    if t == 3 and ready:
                        store(c - 2)

            body(0, True, False)
            body(1, False, False)
            with sp.Fori(2, NC) as c:
                body(c, False, True)
            store(NC - 2)
            store(NC - 1)
            sp.wait_ge(s["stored"], 16 * NC)

        @block.gpsimd
        def _(pool):
            def copy(c):
                for t in range(TC):
                    nrm.wait(pool, c * TC + t + 1)
                    nc.gpsimd.tensor_copy(X[:, bass.ds(c * TC + t, 1), :], xn[:, t:t + 1, :])\
                        .then_inc(s["copied"], 1)

            def split(i):
                piece, staged = slice(i * ND * P, (i + 1) * ND * P), wst[:, 0, :]
                if i == 0:
                    pool.wait_ge(s["w_lo"], 2)
                else:
                    pool.wait_ge(s["w0lo"], i)
                pool.dma_start(staged, w_exp[0, :, piece]).then_inc(s["w0load"], 16)
                pool.wait_ge(s["w0load"], 16 * (i + 1))
                nc.gpsimd.tensor_copy(w0h[:, piece], staged).then_inc(s["w0hi"], 1)
                pool.wait_ge(s["w0hi"], i + 1)
                nc.gpsimd.tensor_tensor(w0l[:, piece], staged, f32(w0h[:, piece]), ALU.subtract)\
                    .then_inc(s["w0lo"], 1)

            copy(0)
            for i in range(EW // (ND * P)):
                split(i)
                if i % 2 == 1:
                    copy(i // 2 + 1)

        @block.scalar
        def _(act):
            act.wait_ge(s["consts"], 80)
            nc.scalar.activation(woh[:], wst[:], ACT.Copy).then_inc(s["w_hi"], 1)
            nc.scalar.activation(gh[:], gst[:], ACT.Copy).then_inc(s["w_hi"], 1)

            def run(c, events, first):
                for what, t, off in events:
                    g = c + off
                    k = g * TC + t
                    opening = first and off == 0
                    if what == "o":
                        act.wait_ge(s["ot_ok"], k + 1)
                        if not (opening and t < 2):
                            act.wait_ge(s["y_ok"], k - 1)
                        nc.scalar.activation(oth[:, t % 2, :, :].rearrange("p d t -> p (d t)"),
                                             ta[:, t % 2, :], ACT.Copy).then_inc(s["oh_ok"], 1)
                    elif what == "w":
                        nrm.root(act, t, k)
                    elif what == "b":
                        act.wait_ge(s["xt_ok"], k + 1)
                        nc.scalar.activation(xh[:, :, bass.ds(g * CH + t * P, P)],
                                             tb[:, t % 2, :].rearrange("p (d t) -> p d t", d=ND),
                                             ACT.Copy).then_inc(s["xh_ok"], 1)
                    elif what == "gates":
                        act.wait_ge(s["g_ok"], g + 1)
                        nc.scalar.activation(gsb[:], gb[0:NE, :], ACT.Copy).then_inc(s["gsb_ok"], 1)
                    elif what == "ranks":
                        act.wait_ge(s["gt_ok"], g + 1)
                        nc.scalar.activation(sig[:].rearrange("p t e -> p (t e)"), sb8[:, 0:TC * NE],
                                             ACT.Sigmoid).then_inc(s["sig_ok"], 1)
                    elif what == "weights":
                        act.wait_ge(s["smt_ok"], g + 1)
                        nc.scalar.activation(smt[:], gb[0:NE, :], ACT.Copy).then_inc(s["smts_ok"], 1)
                if not first:
                    act.wait_ge(s["stored"], c * 16)

            chunks(act, run)

        @block.vector
        def _(dve):
            nrm.init(dve)
            dve.wait_ge(s["consts"], 80)
            dve.wait_ge(s["w_hi"], 2)
            nc.vector.tensor_tensor(wol[:], wst[:], f32(woh[:]), ALU.subtract).then_inc(s["w_lo"], 1)
            nc.vector.tensor_tensor(gl[:], gst[:], f32(gh[:]), ALU.subtract).then_inc(s["w_lo"], 1)

            def run(c, events, first):
                for what, t, off in events:
                    g = c + off
                    k = g * TC + t
                    opening = first and off == 0
                    if what == "o":
                        dve.wait_ge(s["oh_ok"], k + 1)
                        nc.vector.tensor_tensor(
                            otl[:, t % 2, :, :].rearrange("p d t -> p (d t)"), ta[:, t % 2, :],
                            f32(oth[:, t % 2, :, :]).rearrange("p d t -> p (d t)"),
                            ALU.subtract).then_inc(s["ol_ok"], 1)
                    elif what == "w":
                        dve.wait_ge(s["y_ok"], k + 1)
                        loads2.wait(dve, t, g + 1)
                        nc.vector.tensor_tensor(y[:, t, :], yb[:, t % 2, :], xin[:, t, :], ALU.add)\
                            .then_inc(s["sum_ok"], 1)
                        dve.wait_ge(s["sum_ok"], k + 1)
                        nrm.mean_and_var(dve, y[:, t, :], t, k)
                        if not opening:
                            dve.wait_ge(s["copied"], k - TC + 1)
                            dve.wait_ge(s["xt_ok"], k - TC + 1)
                        nrm.apply(dve, xn[:, t, :], y[:, t, :], t, k)
                    elif what == "b":
                        dve.wait_ge(s["xh_ok"], k + 1)
                        nc.vector.tensor_tensor(
                            xl[:, :, bass.ds(g * CH + t * P, P)],
                            tb[:, t % 2, :].rearrange("p (d t) -> p d t", d=ND),
                            f32(xh[:, :, bass.ds(g * CH + t * P, P)]), ALU.subtract)\
                            .then_inc(s["xl_ok"], 1)
                    elif what == "ranks":
                        dve.wait_ge(s["sig_ok"], g + 1)
                        nc.vector.tensor_tensor(val[:], sig[:], brow[:].unsqueeze(1).broadcast_to([P, TC, NE]),
                                                ALU.add).then_inc(s["val_ok"], 1)
                        dve.wait_ge(s["val_ok"], g + 1)
                        other = val[:].unsqueeze(2).broadcast_to([P, TC, NE, NE])
                        own = val[:].unsqueeze(3).broadcast_to([P, TC, NE, NE])
                        g4 = gt[:].rearrange("p t (a b) -> p t a b", a=NE)
                        e4 = eq[:].rearrange("p t (a b) -> p t a b", a=NE)
                        nc.vector.tensor_tensor(g4, other, own, ALU.is_gt).then_inc(s["cmp_ok"], 1)
                        nc.vector.tensor_tensor(e4, other, own, ALU.is_equal).then_inc(s["cmp_ok"], 1)
                        dve.wait_ge(s["cmp_ok"], 2 * g + 2)
                        nc.vector.tensor_tensor(eq[:], eq[:], low[:].unsqueeze(1).broadcast_to([P, TC, NE * NE]),
                                                ALU.mult).then_inc(s["eqm_ok"], 1)
                        dve.wait_ge(s["eqm_ok"], g + 1)
                        nc.vector.tensor_tensor(gt[:], gt[:], eq[:], ALU.add).then_inc(s["add_ok"], 1)
                        dve.wait_ge(s["add_ok"], g + 1)
                        nc.vector.tensor_reduce(rank[:], g4, AX, ALU.add).then_inc(s["rank_ok"], 1)
                        dve.wait_ge(s["rank_ok"], g + 1)
                        nc.vector.scalar_tensor_tensor(out=sm[:], in0=rank[:], scalar=2.0, in1=sig[:],
                                                       op0=ALU.is_lt, op1=ALU.mult).then_inc(s["sm_ok"], 1)

            chunks(dve, run)

        @block.tensor
        def _(pe):
            pe.wait_ge(s["consts"], 80)
            pe.wait_ge(s["w_lo"], 2)

            def run(c, events, first):
                for what, t, off in events:
                    g = c + off
                    k = g * TC + t
                    opening = first and off == 0
                    if what == "o":
                        loads.wait(pe, t, g + 1)
                        if not (opening and t < 2):
                            pe.wait_ge(s["ol_ok"], k - 1)
                        for d in range(ND):
                            last = nc.tensor.transpose(ta[:, t % 2, d * P:(d + 1) * P],
                                                       oin[:, t, d * P:(d + 1) * P], ident[:])
                        last.then_inc(s["ot_ok"], 1)
                    elif what == "w":
                        pe.wait_ge(s["ol_ok"], k + 1)
                        if not (opening and t < 2):
                            pe.wait_ge(s["sum_ok"], k - 1)
                        for d in range(ND):
                            last = mm3(nc, yb[:, t % 2, :], oth[:, t % 2, d, :], otl[:, t % 2, d, :],
                                       woh[:, d, :], wol[:, d, :], d == 0, d == ND - 1)
                        last.then_inc(s["y_ok"], 1)
                    elif what == "b":
                        nrm.wait(pe, k + 1)
                        if not (opening and t < 2):
                            pe.wait_ge(s["xl_ok"], k - 1)
                        for d in range(ND):
                            last = nc.tensor.transpose(tb[:, t % 2, d * P:(d + 1) * P],
                                                       xn[:, t, d * P:(d + 1) * P], ident[:])
                        last.then_inc(s["xt_ok"], 1)
                    elif what == "gates":
                        pe.wait_ge(s["xl_ok"], g * TC + TC)
                        cols = bass.ds(g * CH, CH)
                        for d in range(ND):
                            last = mm3(nc, gb[0:NE, :], gh[:, d, :], gl[:, d, :], xh[:, d, cols],
                                       xl[:, d, cols], d == 0, d == ND - 1)
                        last.then_inc(s["g_ok"], 1)
                    elif what == "ranks":
                        wait_alone(pe, s["gsb_ok"], g + 1, s["consts"], 80)
                        for i in range(TC):
                            last = nc.tensor.transpose(sb8[:, i * NE:(i + 1) * NE], gsb[:, i * P:(i + 1) * P],
                                                       ident[0:NE, 0:NE])
                        last.then_inc(s["gt_ok"], 1)
                    elif what == "weights":
                        pe.wait_ge(s["sm_ok"], g + 1)
                        for i in range(TC):
                            last = nc.tensor.transpose(gb[0:NE, i * P:(i + 1) * P], sm[:, i, :], ident[:])
                        last.then_inc(s["smt_ok"], 1)
                if not first:
                    pe.wait_ge(s["smts_ok"], c)

            chunks(pe, run)


def layer0_experts(nc, loads2, w_exp, weights_t, X, xh, xl, w0h, w0l):
    with ExitStack() as ctx:
        m = Mem(nc, ctx, "e0")
        wst = m.sb("wst", [P, EW])
        wh = [w0h, m.sb("wh", [P, EW], F32R)]
        wl = [w0l, m.sb("wl", [P, EW], F32R)]
        sbc = m.sb("sbc", [P, 2, S])
        sa = m.sb("sa", [P, CH])
        sg = m.sb("sg", [P, CH])
        sbb = m.sb("sbb", [P, CH])
        h = m.sb("h", [P, CH])
        hh = m.sb("hh", [P, 2, NJ, CH], F32R)
        hl = m.sb("hl", [P, 2, NJ, CH], F32R)
        ab = m.ps("ab", [P, 2, 2, CH])
        yb = m.ps("yb", [P, 4, D])
        names = ("wload wsplit_hi wsplit ab_ok sa_ok sg_ok sbb_ok h_ok hh_ok hl_ok y_ok acc_ok").split()
        s = {k: m.sem(k) for k in names}
        block = ctx.enter_context(nc.Block())
        NCH = NC * NJ

        def w13(w, b, which, d, j):
            at = (which * ND + d) * HID + j * P
            return w[b][:, at:at + P]

        def w2(w, b, j):
            at = 2 * ND * HID + j * D
            return w[b][:, at:at + D]

        def order(r):
            ev = []
            q = [(e, c) for e in range(r) for c in range(NC)]
            for i, (e, c) in enumerate(q):
                for j in range(NJ):
                    ev.append(("up", e, c, j))
                    if i > 0:
                        ev.append(("down", *q[i - 1], j))
            return ev + [("down", *q[-1], j) for j in range(NJ)]

        def each(eng, work):
            work(0, 1, True)
            with eng.Fori(0, NE // 2) as i:
                work(i * 2 + 1, 2, False)

        @block.gpsimd
        def _(pool):
            def load(e):
                pool.dma_start(wst[:], w_exp[bass.ds(e, 1)].rearrange("o p n -> (o p) n"))\
                    .then_inc(s["wload"], 16)

            def split(e, half):
                wait_alone(pool, s["wload"], e * 16, s["wload"], 16)
                nc.gpsimd.tensor_copy(wh[half][:], wst[:]).then_inc(s["wsplit_hi"], 1)
                pool.wait_ge(s["wsplit_hi"], e)
                nc.gpsimd.tensor_tensor(wl[half][:], wst[:], f32(wh[half][:]), ALU.subtract)\
                    .then_inc(s["wsplit"], 1)
                pool.wait_ge(s["wsplit"], e)

            load(1)
            split(1, 1)
            load(2)

            def body(i, more):
                pool.wait_ge(s["y_ok"], (i * 2 + 1) * NC * TC)
                split(i * 2 + 2, 0)
                if more:
                    load(i * 2 + 3)
                    pool.wait_ge(s["y_ok"], (i * 2 + 2) * NC * TC)
                    split(i * 2 + 3, 1)
                    load(i * 2 + 4)

            with pool.Fori(0, NE // 2 - 1) as i:
                body(i, True)
            body(NE // 2 - 1, False)

        @block.sync
        def _(sp):
            def load(e, half):
                row = weights_t[bass.ds(e - 1, 1), :].rearrange("o n -> (o n)")
                sp.dma_start(sbc[:, half, :], row.partition_broadcast(P))\
                    .then_inc(loads2.sems[half], 16)

            load(1, 0)
            load(2, 1)
            with sp.Fori(0, NE // 2 - 1) as i:
                sp.wait_ge(s["h_ok"], (i * 2 + 2) * NCH)
                load(i * 2 + 3, 0)
                sp.wait_ge(s["h_ok"], (i * 2 + 3) * NCH)
                load(i * 2 + 4, 1)

        @block.scalar
        def _(act):
            def work(e0, r, shared):
                for ev, e, c, j in order(r):
                    if ev != "up":
                        continue
                    u = c * NJ + j + e * NCH
                    act.wait_ge(s["ab_ok" if shared else "sa_ok"], e0 * NCH + u + 1 - (0 if shared else NCH))
                    if not (shared and u == 0):
                        act.wait_ge(s["h_ok"], e0 * NCH + u)
                    nc.scalar.activation(sg[:], ab[:, u % 2, 0, :] if shared else sa[:], ACT.Silu)\
                        .then_inc(s["sg_ok"], 1)
                    act.wait_ge(s["h_ok"], e0 * NCH + u + 1)
                    if not (shared and c < 2):
                        act.wait_ge(s["y_ok"], ((e0 + e) * NC + c - 1) * TC)
                    nc.scalar.activation(hh[:, c % 2, j, :], h[:], ACT.Copy).then_inc(s["hh_ok"], 1)
            each(act, work)

        @block.vector
        def _(dve):
            def work(e0, r, shared):
                for ev, e, c, j in order(r):
                    u = c * NJ + j + e * NCH
                    k = e0 * NCH + u
                    if ev == "up":
                        cs = slice(c * CH, (c + 1) * CH)
                        if shared:
                            dve.wait_ge(s["sg_ok"], k + 1)
                            if u > 0:
                                dve.wait_ge(s["hl_ok"], k)
                            nc.vector.tensor_tensor(h[:], sg[:], ab[:, u % 2, 1, :], ALU.mult)\
                                .then_inc(s["h_ok"], 1)
                            dve.wait_ge(s["hh_ok"], k + 1)
                            nc.vector.tensor_tensor(hl[:, c % 2, j, :], h[:], f32(hh[:, c % 2, j, :]),
                                                    ALU.subtract).then_inc(s["hl_ok"], 1)
                            continue
                        dve.wait_ge(s["ab_ok"], k + 1)
                        loads2.wait_turn(dve, e % 2, e0 + e - 1)
                        nc.vector.tensor_tensor(sa[:], ab[:, u % 2, 0, :], sbc[:, e % 2, cs], ALU.mult)\
                            .then_inc(s["sa_ok"], 1)
                        nc.vector.tensor_tensor(sbb[:], ab[:, u % 2, 1, :], sbc[:, e % 2, cs], ALU.mult)\
                            .then_inc(s["sbb_ok"], 1)
                        dve.wait_ge(s["hl_ok"], k)
                        dve.wait_ge(s["sbb_ok"], k + 1 - NCH)
                        dve.wait_ge(s["sg_ok"], k + 1)
                        nc.vector.tensor_tensor(h[:], sg[:], sbb[:], ALU.mult).then_inc(s["h_ok"], 1)
                        dve.wait_ge(s["hh_ok"], k + 1)
                        nc.vector.tensor_tensor(hl[:, c % 2, j, :], h[:], f32(hh[:, c % 2, j, :]),
                                                ALU.subtract).then_inc(s["hl_ok"], 1)
                    else:
                        for t in (2 * j, 2 * j + 1):
                            dve.wait_ge(s["y_ok"], ((e0 + e) * NC + c) * TC + t + 1)
                            nc.vector.tensor_tensor(X[:, c * TC + t, :], X[:, c * TC + t, :], yb[:, t, :],
                                                    ALU.add).then_inc(s["acc_ok"], 1)
            each(dve, work)

        @block.tensor
        def _(pe):
            def work(e0, r, shared):
                for ev, e, c, j in order(r):
                    u = c * NJ + j + e * NCH
                    half = 0 if shared else (e + 1) % 2
                    k = e0 * NCH + u
                    if ev == "up":
                        if c == 0 and j == 0 and not shared:
                            pe.wait_ge(s["wsplit"], e0 + e)
                        if not (shared and u < 2):
                            pe.wait_ge(s["h_ok"], k - 1)
                        cs = slice(c * CH, (c + 1) * CH)
                        for which in range(2):
                            for d in range(ND):
                                last = mm3(nc, ab[:, u % 2, which, :], w13(wh, half, which, d, j),
                                           w13(wl, half, which, d, j), xh[:, d, cs], xl[:, d, cs],
                                           d == 0, d == ND - 1)
                        last.then_inc(s["ab_ok"], 1)
                    else:
                        pe.wait_ge(s["hl_ok"], (e0 + e) * NCH + (c + 1) * NJ)
                        for t in (2 * j, 2 * j + 1):
                            if not (shared and c == 0):
                                pe.wait_ge(s["acc_ok"], ((e0 + e) * NC + c - 1) * TC + t + 1)
                            for i in range(NJ):
                                last = mm3(nc, yb[:, t, :], hh[:, c % 2, i, t * P:(t + 1) * P],
                                           hl[:, c % 2, i, t * P:(t + 1) * P], w2(wh, half, i),
                                           w2(wl, half, i), i == 0, i == NJ - 1)
                            last.then_inc(s["y_ok"], 1)
            each(pe, work)


def layer1_qkv(nc, nrm, loads, w_qkv, qk_bias, v_bias, rope, rot, eye, X, kth, ktl, x2, q_dram, v_dram):
    with ExitStack() as ctx:
        m = Mem(nc, ctx, "q1")
        wh = m.sb("wh", [P, 3, ND, D], F32R)
        wl = m.sb("wl", [P, 3, ND, D], F32R)
        xch = m.sb("xch", [P, ND, CH], F32R)
        xcl = m.sb("xcl", [P, ND, CH], F32R)
        xn = m.sb("xn", [P, TC, D])
        cs = m.sb("cs", [P, 2, CH])
        ident = m.sb("ident", [P, P])
        rotf = m.sb("rotf", [P, P])
        bqk = m.sb("bqk", [P, 2, ND])
        bv = m.sb("bv", [P, D])
        qkf = m.sb("qkf", [P, 2, 2, CH])
        t1 = m.sb("t1", [P, 2, CH])
        t2 = m.sb("t2", [P, 2, CH])
        vf, vhl = t2[:, 0, :], m.sb("vhl", [P, 2, 2, D], F32R)
        qhl = m.sb("qhl", [P, 2, CH], F32R)
        wst = [qkf[:, a, b, :] for a in range(2) for b in range(2)]
        qk = m.ps("qk", [P, 2, CH])
        rb = m.ps("rb", [P, 2, CH])
        vb = m.ps("vb", [P, 2, D])
        tb = m.ps("tb", [P, 2, ND * P])
        names = ("consts whi wlo csload xt_ok xh_ok xl_ok qk_ok qkf_ok r_ok t1_ok t2_ok sum_ok hi_ok "
                 "lo_ok v_ok vf_ok vh_ok vl_ok qstore vstore0 vstore1 xstore").split()
        s = {k: m.sem(k) for k in names}
        vstore = (s["vstore0"], s["vstore1"])
        block = ctx.enter_context(nc.Block())
        NW = 3 * ND

        before = ([("norm", 0, 0)] + [("weight", i, 0) for i in range(4)] +
                  [("turn", 0, 0), ("turn", 1, 0)] + [("weight", i, 0) for i in range(4, 8)] +
                  [("turn", 2, 0), ("turn", 3, 0)] + [("weight", i, 0) for i in range(8, NW)])

        def chunk(more):
            ev = [("qk", 0, 0)] + [("norm", 0, 1)] * more + [("qk", 1, 0), ("rotary", 0, 0), ("qk", 2, 0)]
            ev += [("rotary", 1, 0), ("qk", 3, 0), ("rotary", 2, 0), ("v", 0, 0), ("rotary", 3, 0)]
            ev += [("v", 1, 0)] + [("turn", 0, 1), ("turn", 1, 1)] * more + [("v", 2, 0), ("v", 3, 0)]
            return ev + [("turn", 2, 1), ("turn", 3, 1)] * more

        def chunks(eng, run):
            run(0, before, True)
            run(0, chunk(True), True)
            with eng.Fori(1, NC - 1) as c:
                run(c, chunk(True), False)
            run(NC - 1, chunk(False), False)

        @block.sync
        def _(sp):
            for i in range(4):
                sp.dma_start(wst[i], w_qkv[i // ND, :, i % ND, :]).then_inc(loads.sems[i % 4], 16)
            for dst, src in ((ident[:], eye), (rotf[:], rot), (bqk[:], qk_bias),
                             (bv[:], v_bias.partition_broadcast(P))):
                sp.dma_start(dst, src).then_inc(s["consts"], 16)
            sp.dma_start(cs[:], rope[:, :, 0:CH].rearrange("a p n -> p a n")).then_inc(s["csload"], 16)

            def run(c, events, first):
                for what, j, ahead in events:
                    if what == "weight" and j + 4 < NW:
                        i = j + 4
                        sp.wait_ge(s["wlo"], j + 1)
                        sp.dma_start(wst[i % 4], w_qkv[i // ND, :, i % ND, :]).then_inc(loads.sems[i % 4], 16)
                    elif what == "norm":
                        for t in range(TC):
                            nrm.wait(sp, (c + ahead) * TC + t + 1)
                            sp.dma_start(x2[bass.ds((c + ahead) * CH + t * P, P), :], xn[:, t, :])\
                                .then_inc(s["xstore"], 16)
                    elif what == "rotary":
                        wait_alone(sp, s["lo_ok"], c * ND + j + 1, s["consts"], 16)
                        sp.dma_start(q_dram[:, :, j, bass.ds(c * CH, CH)].rearrange("a p n -> p a n"),
                                     f32(qhl[:])).then_inc(s["qstore"], 16)
                        if j == ND - 1 and events != chunk(False):
                            sp.dma_start(cs[:], rope[:, :, bass.ds((c + 1) * CH, CH)]
                                         .rearrange("a p n -> p a n")).then_inc(s["csload"], 16)
                    elif what == "v":
                        wait_alone(sp, s["vl_ok"], c * TC + j + 1, s["consts"], 16)
                        sp.dma_start(v_dram[:, :, bass.ds(c * TC + j, 1), :]
                                     .rearrange("a p o n -> p a (o n)"), f32(vhl[:, j % 2, :, :]))\
                            .then_inc(vstore[j % 2], 16)

            chunks(sp, run)
            sp.wait_ge(s["qstore"], 16 * NC * ND)
            for sem in vstore:
                sp.wait_ge(sem, 16 * NC * TC // 2)
            sp.wait_ge(s["xstore"], 16 * NC * TC)

        @block.gpsimd
        def _(pool):
            def run(c, events, first):
                for what, j, _ in events:
                    if what == "qk":
                        k = c * ND + j
                        pool.wait_ge(s["qkf_ok"], 2 * k + 2)
                        if j == 0:
                            pool.wait_ge(s["csload"], 16 * c + 16)
                        if not (first and j == 0):
                            pool.wait_ge(s["lo_ok"], k)
                        nc.gpsimd.tensor_tensor(t1[:], qkf[:, j % 2, :, :], cs[:, 0, :].unsqueeze(1).broadcast_to([P, 2, CH]),
                                                ALU.mult).then_inc(s["t1_ok"], 1)

            chunks(pool, run)

        @block.scalar
        def _(act):
            def run(c, events, first):
                for what, j, ahead in events:
                    k = c * ND + j
                    if what == "weight":
                        loads.wait(act, j % 4, j // 4 + 1)
                        nc.scalar.activation(wh[:, j // ND, j % ND, :], wst[j % 4], ACT.Copy)\
                            .then_inc(s["whi"], 1)
                    elif what == "norm":
                        for t in range(TC):
                            nrm.root(act, t, (c + ahead) * TC + t)
                    elif what == "turn":
                        act.wait_ge(s["xt_ok"], (c + ahead) * TC + j + 1)
                        if ahead:
                            act.wait_ge(s["v_ok"], (c + 1) * TC)
                        nc.scalar.activation(xch[:, :, j * P:(j + 1) * P],
                                             tb[:, j % 2, :].rearrange("p (d t) -> p d t", d=ND),
                                             ACT.Copy).then_inc(s["xh_ok"], 1)
                    elif what == "qk":
                        if first and j == 0:
                            act.wait_ge(s["consts"], 64)
                            act.wait_ge(s["wlo"], NW)
                        for a in range(2):
                            act.wait_ge(s["qk_ok"], 2 * k + a + 1)
                            if a == 0 and not (first and j < 2):
                                act.wait_ge(s["r_ok"], k - 1)
                                act.wait_ge(s["t1_ok"], k - 1)
                            nc.scalar.activation(qkf[:, j % 2, a, :], qk[:, a, :], ACT.Identity,
                                                 bias=bqk[:, a, j:j + 1]).then_inc(s["qkf_ok"], 1)
                    elif what == "rotary":
                        act.wait_ge(s["sum_ok"], k + 1)
                        if not (first and j == 0):
                            act.wait_ge(s["qstore"], 16 * k)
                        nc.scalar.activation(qhl[:, 0, :], t1[:, 0, :], ACT.Copy)
                        nc.scalar.activation(kth[:, j, bass.ds(c * CH, CH)], t1[:, 1, :], ACT.Copy)\
                            .then_inc(s["hi_ok"], 1)
                    elif what == "v":
                        act.wait_ge(s["vf_ok"], k + 1)
                        if not (first and j < 2):
                            act.wait_ge(vstore[j % 2], 16 * (c * (TC // 2) + j // 2))
                        nc.scalar.activation(vhl[:, j % 2, 0, :], vf, ACT.Copy).then_inc(s["vh_ok"], 1)

            chunks(act, run)

        @block.vector
        def _(dve):
            def run(c, events, first):
                for what, j, ahead in events:
                    k = c * ND + j
                    if what == "weight":
                        dve.wait_ge(s["whi"], j + 1)
                        nc.vector.tensor_tensor(wl[:, j // ND, j % ND, :], wst[j % 4],
                                                f32(wh[:, j // ND, j % ND, :]), ALU.subtract)\
                            .then_inc(s["wlo"], 1)
                    elif what == "norm":
                        n = c + ahead
                        rows = [X[:, bass.ds(n * TC + t, 1), :].rearrange("p o n -> p (o n)")
                                for t in range(TC)]
                        for t in range(TC):
                            nrm.mean_and_var(dve, rows[t], t, n * TC + t)
                        if ahead:
                            dve.wait_ge(s["xstore"], 16 * n * TC)
                            dve.wait_ge(s["xt_ok"], n * TC)
                        for t in range(TC):
                            nrm.apply(dve, xn[:, t, :], rows[t], t, n * TC + t)
                    elif what == "turn":
                        dve.wait_ge(s["xh_ok"], (c + ahead) * TC + j + 1)
                        nc.vector.tensor_tensor(xcl[:, :, j * P:(j + 1) * P],
                                                tb[:, j % 2, :].rearrange("p (d t) -> p d t", d=ND),
                                                f32(xch[:, :, j * P:(j + 1) * P]), ALU.subtract)\
                            .then_inc(s["xl_ok"], 1)
                    elif what == "rotary":
                        if first and j == 0:
                            dve.wait_ge(s["consts"], 64)
                        if j == 0:
                            dve.wait_ge(s["csload"], 16 * c + 16)
                            if not first:
                                dve.wait_ge(s["vl_ok"], c * TC)
                        if j == ND - 1:
                            dve.wait_ge(s["vl_ok"], c * TC + 1)
                        dve.wait_ge(s["r_ok"], k + 1)
                        nc.vector.tensor_tensor(t2[:], rb[:], cs[:, 1, :].unsqueeze(1).broadcast_to([P, 2, CH]),
                                                ALU.mult).then_inc(s["t2_ok"], 1)
                        dve.wait_ge(s["t2_ok"], k + 1)
                        dve.wait_ge(s["t1_ok"], k + 1)
                        nc.vector.tensor_tensor(t1[:], t1[:], t2[:], ALU.add).then_inc(s["sum_ok"], 1)
                        dve.wait_ge(s["hi_ok"], k + 1)
                        nc.vector.tensor_tensor(qhl[:, 1, :], t1[:, 0, :], f32(qhl[:, 0, :]), ALU.subtract)
                        nc.vector.tensor_tensor(ktl[:, j, bass.ds(c * CH, CH)], t1[:, 1, :],
                                                f32(kth[:, j, bass.ds(c * CH, CH)]), ALU.subtract)\
                            .then_inc(s["lo_ok"], 1)
                    elif what == "v":
                        dve.wait_ge(s["v_ok"], k + 1)
                        if j == 0:
                            dve.wait_ge(s["sum_ok"], c * ND + ND - 1)
                        elif j == 1:
                            dve.wait_ge(s["sum_ok"], c * ND + ND)
                        if j > 0:
                            dve.wait_ge(s["vl_ok"], k)
                        nc.vector.tensor_tensor(vf, vb[:, j % 2, :], bv[:], ALU.add).then_inc(s["vf_ok"], 1)
                        dve.wait_ge(s["vh_ok"], k + 1)
                        nc.vector.tensor_tensor(vhl[:, j % 2, 1, :], vf, f32(vhl[:, j % 2, 0, :]),
                                                ALU.subtract).then_inc(s["vl_ok"], 1)

            chunks(dve, run)

        @block.tensor
        def _(pe):
            pe.wait_ge(s["consts"], 64)

            def run(c, events, first):
                for what, j, ahead in events:
                    k = c * ND + j
                    if what == "turn":
                        n = (c + ahead) * TC + j
                        nrm.wait(pe, n + 1)
                        if j >= 2 or ahead:
                            pe.wait_ge(s["xl_ok"], n - 1)
                        for d in range(ND):
                            last = nc.tensor.transpose(tb[:, j % 2, d * P:(d + 1) * P],
                                                       xn[:, j, d * P:(d + 1) * P], ident[:])
                        last.then_inc(s["xt_ok"], 1)
                    elif what == "qk":
                        if j == 0:
                            pe.wait_ge(s["xl_ok"], (c + 1) * TC)
                            if first:
                                pe.wait_ge(s["wlo"], NW)
                        for a in range(2):
                            if not (first and j == 0):
                                pe.wait_ge(s["qkf_ok"], 2 * k + a - 1)
                            for d in range(ND):
                                last = mm3(nc, qk[:, a, :], wh[:, a, d, j * P:(j + 1) * P],
                                           wl[:, a, d, j * P:(j + 1) * P], xch[:, d, :], xcl[:, d, :],
                                           d == 0, d == ND - 1)
                            last.then_inc(s["qk_ok"], 1)
                    elif what == "rotary":
                        pe.wait_ge(s["qkf_ok"], 2 * k + 2)
                        if not (first and j == 0):
                            pe.wait_ge(s["t2_ok"], k)
                        for a in range(2):
                            last = nc.tensor.matmul(rb[:, a, :], rotf[:], qkf[:, j % 2, a, :], start=True, stop=True)
                        last.then_inc(s["r_ok"], 1)
                    elif what == "v":
                        if not (first and j < 2):
                            pe.wait_ge(s["vf_ok"], k - 1)
                        for d in range(ND):
                            last = mm3(nc, vb[:, j % 2, :], xch[:, d, j * P:(j + 1) * P],
                                       xcl[:, d, j * P:(j + 1) * P], wh[:, 2, d, :], wl[:, 2, d, :],
                                       d == 0, d == ND - 1)
                        last.then_inc(s["v_ok"], 1)

            chunks(pe, run)


def layer1_attention(nc, loads, loads2, stores, wo, eye, kth, ktl, x2, q_dram, v_dram, y_dram):
    with ExitStack() as ctx:
        m = Mem(nc, ctx, "a1")
        vh = m.sb("vh", [P, NT, D], F32R)
        vl = m.sb("vl", [P, NT, D], F32R)
        woh = m.sb("woh", [P, ND, D], F32R)
        wol = m.sb("wol", [P, ND, D], F32R)
        q = m.sb("q", [P, 2, 2, ND, P], F32R)
        pr = m.sb("pr", [P, S])
        pth = m.sb("pth", [P, NT, P], F32R)
        ptl = m.sb("ptl", [P, NT, P], F32R)
        xin = m.sb("xin", [P, 2, D])
        ident = m.sb("ident", [P, P])
        nm = m.sb("nm", [P, 1])
        bias = m.sb("bias", [P, 1])
        rsum = m.sb("rsum", [P, 1])
        rinv = m.sb("rinv", [P, 1])
        o = m.sb("o", [P, D])
        oth = m.sb("oth", [P, ND, P], F32R)
        otl = m.sb("otl", [P, ND, P], F32R)
        y = m.sb("y", [P, 2, D])
        wst = pr
        sc = m.ps("sc", [P, S])
        tb = m.ps("tb", [P, 2, 4 * P])
        av = m.ps("av", [P, D])
        yb = m.ps("yb", [P, D])
        names = ("consts vload w_hi w_lo s_ok nm_ok bias_ok exp_ok rinv_ok pt_ok ph_ok pl_ok "
                 "av_ok o_ok ot_ok oh_ok ol_ok y_ok sum_ok").split()
        s = {k: m.sem(k) for k in names}
        block = ctx.enter_context(nc.Block())

        def loop(eng, tile):
            with eng.Fori(0, NT // 2 - 1) as i:
                tile(i * 2, 0, False)
                tile(i * 2 + 1, 1, False)
            tile(NT - 2, 0, False)
            tile(NT - 1, 1, True)

        @block.sync
        def _(sp):

            def load(n, r):
                cols = bass.ds(n * P, P)
                for a in range(2):
                    sp.dma_start(f32(q[:, r, a, :, :]), q_dram[a, :, :, cols])\
                        .then_inc(loads.sems[r], 16)

            load(0, 0)
            sp.dma_start(wst[:], wo.rearrange("p a n -> p (a n)")).then_inc(s["consts"], 16)
            sp.dma_start(ident[:], eye).then_inc(s["consts"], 16)
            load(1, 1)
            for a, dst in ((0, vh), (1, vl)):
                for c in range(NC):
                    ts = slice(c * TC, (c + 1) * TC)
                    sp.dma_start(f32(dst[:, ts, :]), v_dram[a, :, ts, :]).then_inc(s["vload"], 16)
            sp.dma_start(xin[:, 0, :], x2[0:P, :]).then_inc(loads2.sems[0], 16)

            def store(n, r):
                sp.wait_ge(s["sum_ok"], n + 1)
                sp.dma_start(y_dram[bass.ds(n * P, P), :], y[:, r, :]).then_inc(stores.sems[r], 16)

            def tile(n, r, first, more):
                if more:
                    sp.wait_ge(s["s_ok"], n + 1)
                    load(n + 2, r)
                if not first:
                    store(n - 1, 1 - r)
                sp.dma_start(xin[:, 1 - r, :], x2[bass.ds((n + 1) * P, P), :])\
                  .then_inc(loads2.sems[1 - r], 16)

            tile(0, 0, True, True)
            tile(1, 1, False, True)
            with sp.Fori(1, NT // 2 - 1) as i:
                tile(i * 2, 0, False, True)
                tile(i * 2 + 1, 1, False, True)
            tile(NT - 2, 0, False, False)
            store(NT - 2, 0)
            store(NT - 1, 1)
            for r in range(2):
                stores.wait(sp, r, NT // 2)

        def exps(act, n):
            act.wait_ge(s["bias_ok"], n + 1)
            nc.scalar.activation(pr[:], sc[:], ACT.Exp, bias=bias[:], scale=SCALE1,
                                 accum_out=rsum[:]).then_inc(s["exp_ok"], 1)

        @block.scalar
        def _(act):
            act.wait_ge(s["consts"], 32)
            nc.scalar.activation(woh[:].rearrange("p d n -> p (d n)"), wst[:], ACT.Copy).then_inc(s["w_hi"], 1)
            act.wait_ge(s["w_lo"], 1)
            exps(act, 0)

            def tile(n, r, last):
                hi_out(n, r, act)
                for g in range(4):
                    act.wait_ge(s["pt_ok"], n * 4 + g + 1)
                    nc.scalar.activation(pth[:, 4 * g:4 * g + 4, :].rearrange("p a b -> p (a b)"),
                                         tb[:, (g + 1) % 2, :], ACT.Copy).then_inc(s["ph_ok"], 1)
                if not last:
                    exps(act, n + 1)

            def hi_out(n, r, act):
                act.wait_ge(s["ot_ok"], n)
                nc.scalar.activation(oth[:].rearrange("p a b -> p (a b)"), tb[:, 0, :], ACT.Copy)\
                    .then_inc(s["oh_ok"], 1)

            def first(n, r, last):
                for g in range(4):
                    act.wait_ge(s["pt_ok"], n * 4 + g + 1)
                    nc.scalar.activation(pth[:, 4 * g:4 * g + 4, :].rearrange("p a b -> p (a b)"),
                                         tb[:, (g + 1) % 2, :], ACT.Copy).then_inc(s["ph_ok"], 1)
                exps(act, n + 1)

            first(0, 0, False)
            tile(1, 1, False)
            with act.Fori(1, NT // 2 - 1) as i:
                tile(i * 2, 0, False)
                tile(i * 2 + 1, 1, False)
            tile(NT - 2, 0, False)
            tile(NT - 1, 1, True)
            hi_out(NT, 0, act)

        @block.vector
        def _(dve):
            def peak(n):
                dve.wait_ge(s["s_ok"], n + 1)
                nc.vector.tensor_reduce(nm[:], sc[:], AX, ALU.max, negate=True).then_inc(s["nm_ok"], 1)
                dve.wait_ge(s["nm_ok"], n + 1)
                nc.vector.tensor_scalar(bias[:], nm[:], SCALE1, None, ALU.mult).then_inc(s["bias_ok"], 1)

            def lo_out(n):
                dve.wait_ge(s["oh_ok"], n)
                nc.vector.tensor_tensor(otl[:].rearrange("p a b -> p (a b)"), tb[:, 0, :],
                                        f32(oth[:]).rearrange("p a b -> p (a b)"), ALU.subtract)\
                    .then_inc(s["ol_ok"], 1)

            def add(n, r, first):
                dve.wait_ge(s["y_ok"], n + 1)
                loads2.wait_turn(dve, r, n)
                if not first:
                    stores.wait_turn(dve, r, n - 2)
                nc.vector.tensor_tensor(y[:, r, :], yb[:], xin[:, r, :], ALU.add).then_inc(s["sum_ok"], 1)

            def tile(n, r, last, no=99):
                if no > 0:
                    lo_out(n)
                for g in range(4):
                    dve.wait_ge(s["ph_ok"], n * 4 + g + 1)
                    nc.vector.tensor_tensor(ptl[:, 4 * g:4 * g + 4, :].rearrange("p a b -> p (a b)"),
                                            tb[:, (g + 1) % 2, :],
                                            f32(pth[:, 4 * g:4 * g + 4, :]).rearrange("p a b -> p (a b)"),
                                            ALU.subtract).then_inc(s["pl_ok"], 1)
                    if g == 2 and no > 0:
                        add(n - 1, 1 - r, no < 3)
                dve.wait_ge(s["exp_ok"], n + 1)
                nc.vector.reciprocal(rinv[:], rsum[:]).then_inc(s["rinv_ok"], 1)
                if not last:
                    dve.wait_ge(s["rinv_ok"], n + 1)
                    peak(n + 1)
                dve.wait_ge(s["rinv_ok"], n + 1)
                dve.wait_ge(s["av_ok"], n + 1)
                nc.vector.tensor_scalar(o[:], av[:], rinv[:], None, ALU.mult).then_inc(s["o_ok"], 1)

            dve.wait_ge(s["w_hi"], 1)
            nc.vector.tensor_tensor(wol[:].rearrange("p d n -> p (d n)"), wst[:],
                                    f32(woh[:]).rearrange("p d n -> p (d n)"),
                                    ALU.subtract).then_inc(s["w_lo"], 1)
            peak(0)
            tile(0, 0, False, 0)
            tile(1, 1, False, 1)
            tile(2, 0, False, 2)
            tile(3, 1, False, 3)
            with dve.Fori(2, NT // 2 - 1) as i:
                tile(i * 2, 0, False)
                tile(i * 2 + 1, 1, False)
            tile(NT - 2, 0, False)
            tile(NT - 1, 1, True)
            lo_out(NT)
            add(NT - 1, 1, False)

        @block.tensor
        def _(pe):
            def scores(n, r, b):
                ks = slice(b * CH, (b + 1) * CH)
                if b == 0:
                    loads.wait_turn(pe, r, n, 2)
                for d in range(ND):
                    last = mm3(nc, sc[:, ks], q[:, r, 0, d, :], q[:, r, 1, d, :], kth[:, d, ks],
                               ktl[:, d, ks], d == 0, d == ND - 1)
                if b == 3:
                    last.then_inc(s["s_ok"], 1)

            def turn_out(n):
                pe.wait_ge(s["o_ok"], n)
                for d in range(ND):
                    last = nc.tensor.transpose(tb[:, 0, d * P:(d + 1) * P], o[:, d * P:(d + 1) * P], ident[:])
                last.then_inc(s["ot_ok"], 1)

            def project(n, no=99):
                pe.wait_ge(s["ol_ok"], n)
                if no > 1:
                    pe.wait_ge(s["sum_ok"], n - 1)
                for d in range(ND):
                    last = mm3(nc, yb[:], oth[:, d, :], otl[:, d, :], woh[:, d, :], wol[:, d, :],
                               d == 0, d == ND - 1)
                last.then_inc(s["y_ok"], 1)

            def tile(n, r, last, no=99):
                pe.wait_ge(s["exp_ok"], n + 1)
                for b in range(4):
                    if b == 0 and no > 0:
                        pe.wait_ge(s["pl_ok"], 4 * n)
                        turn_out(n)
                    if not last:
                        scores(n + 1, 1 - r, b)
                    if b == 1 and no > 0:
                        pe.wait_ge(s["ol_ok"], n)
                    if b >= 2:
                        pe.wait_ge(s["pl_ok"], 4 * n + b - 1)
                    for a in range(4):
                        kt = 4 * b + a
                        end = nc.tensor.transpose(tb[:, (b + 1) % 2, a * P:(a + 1) * P],
                                                  pr[:, kt * P:(kt + 1) * P], ident[:])
                    end.then_inc(s["pt_ok"], 1)
                    if b == 2 and no > 0:
                        project(n, no)
                if no == 0:
                    pe.wait_ge(s["vload"], 16 * 2 * NC)
                for kt in range(NT):
                    if kt % 4 == 0:
                        pe.wait_ge(s["pl_ok"], 4 * n + kt // 4 + 1)
                    end = mm3(nc, av[:], pth[:, kt, :], ptl[:, kt, :], vh[:, kt, :], vl[:, kt, :],
                              kt == 0, kt == NT - 1)
                end.then_inc(s["av_ok"], 1)

            for b in range(4):
                scores(0, 0, b)
            pe.wait_ge(s["consts"], 32)
            pe.wait_ge(s["w_lo"], 1)
            tile(0, 0, False, 0)
            tile(1, 1, False, 1)
            with pe.Fori(1, NT // 2 - 1) as i:
                tile(i * 2, 0, False)
                tile(i * 2 + 1, 1, False)
            tile(NT - 2, 0, False)
            tile(NT - 1, 1, True)
            turn_out(NT)
            project(NT)


def layer1_mlp(nc, nrm, loads, loads2, stores, w_mlp, y_dram, eye, X, xh, xl, out):
    with ExitStack() as ctx:
        m = Mem(nc, ctx, "m1")
        PW = 2 * D
        wst = m.sb("wst", [P, 2, PW])
        wh = m.sb("wh", [P, 6, PW], F32R)
        wl = m.sb("wl", [P, 6, PW], F32R)
        sg = m.sb("sg", [P, CH])
        h = m.sb("h", [P, 4, CH])
        a = m.sb("a", [P, 4, CH])
        c0 = m.sb("c0", [P, 3, CH], BF16)
        c1 = m.sb("c1", [P, 2, CH], BF16)
        c2 = m.sb("c2", [P, CH], BF16)
        k = m.sb("k", [P, 4, CH], BF16)
        hh = m.sb("hh", [P, 4, CH], F32R)
        hl = m.sb("hl", [P, 4, CH], F32R)
        gu = m.ps("gu", [P, 2, 2, CH])
        yb = m.ps("yb", [P, 4, D])
        ident = m.sb("ident", [P, P])
        names = ("consts xt_ok xh_ok xl_ok whi wlo gu_ok sg_ok h_ok a_ok cmp_ok k1_ok k2_ok hs_ok hh_ok hl_ok y_ok "
                 "acc_ok").split()
        s = {n: m.sem(n) for n in names}
        block = ctx.enter_context(nc.Block())
        NPC = 6

        def group(q, first):
            ev = []
            for c in range(NC):
                ev += [("up", c, q, r) for r in range(4)]
                if c > 0:
                    ev += [("down", c - 1, q, 0), ("pick", c, q, 0), ("add", c - 1, q, 0)]
                elif not first:
                    ev += [("down", NC - 1, q - 1, 0), ("pick", c, q, 0), ("add", NC - 1, q - 1, 0)]
                else:
                    ev.append(("pick", c, q, 0))
            return ev

        def opening():
            def turn(c):
                return [("turn", c, 0, t) for t in range(TC)]

            ev = [("norm", 0, 0, 0)] + turn(0) + [("norm", 1, 0, 0)]
            beside = {0: [("norm", 2, 0, 0)], 1: turn(1), 2: [("norm", 3, 0, 0)], 4: turn(2), 6: turn(3)}
            ups = 0
            for e in group(0, True):
                ev.append(e)
                if e[0] == "up":
                    ev += beside.get(ups, [])
                    ups += 1
            return ev

        def is_first(q):
            return isinstance(q, int) and q == 0

        def groups(eng, run):
            run(opening())
            with eng.Fori(1, NQ - 1) as q:
                run(group(q, False))
            ev = []
            for e in group(NQ - 1, False) + [("down", NC - 1, NQ - 1, 0), ("add", NC - 1, NQ - 1, 0)]:
                ev.append(e)
                if e[0] == "add" and e[2] == NQ - 1:
                    ev.append(("last norm", e[1], NQ - 1, 0))
            run(ev)

        @block.sync
        def _(sp):
            def rows(c):
                sp.dma_start(X[:, c * TC:(c + 1) * TC, :],
                             y_dram[c * CH:(c + 1) * CH, :].rearrange("(t p) n -> p t n", p=P))\
                    .then_inc(loads2.sems[c], 16)

            def load(q, i):
                sp.dma_start(wst[:, i % 2, :], w_mlp[bass.ds(q, 1), i, :, :].rearrange("o p n -> (o p) n"))\
                    .then_inc(loads.sems[i % 2], 16)

            rows(0)
            load(0, 0)
            sp.dma_start(ident[:], eye).then_inc(s["consts"], 16)
            load(0, 1)
            for c in range(1, NC):
                rows(c)
            for i in range(2, NPC):
                sp.wait_ge(s["wlo"], i - 1)
                load(0, i)
            with sp.Fori(1, NQ) as q:
                for i in range(NPC):
                    sp.wait_ge(s["wlo"], q * NPC + i - 1)
                    load(q, i)
            for c in range(NC):
                nrm.wait(sp, NT + (c + 1) * TC)
                sp.dma_start(out[c * CH:(c + 1) * CH, :].rearrange("(t p) n -> p t n", p=P),
                             X[:, c * TC:(c + 1) * TC, :]).then_inc(stores.sems[c], 16)
            for c in range(NC):
                stores.wait(sp, c, 1)

        @block.gpsimd
        def _(pool):
            def split(q, i, first):
                if not first:
                    if i < 4:
                        wait_alone(pool, s["gu_ok"], q * NC * 4 - 3 + i, s["wlo"], 1)
                    else:
                        wait_alone(pool, s["y_ok"], q * NC * TC, s["wlo"], 1)
                wait_alone(pool, loads.sems[i % 2], 16 * (loads.before[i % 2] + i // 2 + 1) + q * (8 * NPC),
                           loads.sems[i % 2], 16)
                nc.gpsimd.tensor_copy(wh[:, i, :], wst[:, i % 2, :]).then_inc(s["whi"], 1)
                pool.wait_ge(s["whi"], q * NPC + i + 1)
                nc.gpsimd.tensor_tensor(wl[:, i, :], wst[:, i % 2, :], f32(wh[:, i, :]), ALU.subtract)\
                    .then_inc(s["wlo"], 1)

            for i in range(NPC):
                split(0, i, True)
            with pool.Fori(1, NQ) as q:
                for i in range(NPC):
                    split(q, i, False)

        @block.scalar
        def _(act):
            def run(ev):
                for what, c, q, r in ev:
                    i = q * NC + c
                    start = c == 0 and is_first(q)
                    if what in ("norm", "last norm"):
                        done = NT if what == "last norm" else 0
                        for t in range(TC):
                            nrm.root(act, t, done + c * TC + t)
                    elif what == "turn":
                        act.wait_ge(s["xt_ok"], c * TC + r + 1)
                        nc.scalar.activation(xh[:, :, c * CH + r * P:c * CH + (r + 1) * P],
                                             yb[:, r, :].rearrange("p (d t) -> p d t", d=ND),
                                             ACT.Copy).then_inc(s["xh_ok"], 1)
                    elif what == "up":
                        act.wait_ge(s["gu_ok"], i * 4 + r + 1)
                        if not (start and r == 0):
                            act.wait_ge(s["h_ok"], i * 4 + r)
                        nc.scalar.activation(sg[:], gu[:, r % 2, 0, :], ACT.Silu).then_inc(s["sg_ok"], 1)
                    elif what == "pick":
                        act.wait_ge(s["h_ok"], (i + 1) * 4)
                        nc.scalar.activation(a[:], h[:], ACT.Abs).then_inc(s["a_ok"], 1)
                        if not start:
                            act.wait_ge(s["y_ok"], i * TC)
                        for r in range(4):
                            act.wait_ge(s["hs_ok"], i * 4 + r + 1)
                            nc.scalar.activation(hh[:, r, :], h[:, r, :], ACT.Copy).then_inc(s["hh_ok"], 1)
            groups(act, run)

        @block.vector
        def _(dve):
            tt, stt = nc.vector.tensor_tensor, nc.vector.scalar_tensor_tensor

            def run(ev):
                for what, c, q, r in ev:
                    i = q * NC + c
                    if what in ("norm", "last norm"):
                        done = NT if what == "last norm" else 0
                        rows = [X[:, c * TC + t, :] for t in range(TC)]
                        if done:
                            dve.wait_ge(s["acc_ok"], (i + 1) * TC)
                        else:
                            loads2.wait(dve, c, 1)
                        for t in range(TC):
                            nrm.mean_and_var(dve, rows[t], t, done + c * TC + t)
                        for t in range(TC):
                            nrm.apply(dve, rows[t], rows[t], t, done + c * TC + t)
                    elif what == "turn":
                        cols = slice(c * CH + r * P, c * CH + (r + 1) * P)
                        dve.wait_ge(s["xh_ok"], c * TC + r + 1)
                        nc.vector.tensor_tensor(xl[:, :, cols], yb[:, r, :].rearrange("p (d t) -> p d t", d=ND),
                                                f32(xh[:, :, cols]), ALU.subtract).then_inc(s["xl_ok"], 1)
                    elif what == "up":
                        if r == 0 and not (c == 0 and is_first(q)):
                            dve.wait_ge(s["hl_ok"], i * 4)
                        dve.wait_ge(s["sg_ok"], i * 4 + r + 1)
                        tt(h[:, r, :], sg[:], gu[:, r % 2, 1, :], ALU.mult).then_inc(s["h_ok"], 1)
                    elif what == "add":
                        for t in range(TC):
                            dve.wait_ge(s["y_ok"], i * TC + t + 1)
                            tt(X[:, c * TC + t, :], X[:, c * TC + t, :], yb[:, t, :], ALU.add)\
                                .then_inc(s["acc_ok"], 1)
                    elif what == "pick":
                        dve.wait_ge(s["a_ok"], i + 1)
                        tt(c0[:], a[:, 1:4, :], a[:, 0:1, :].broadcast_to([P, 3, CH]), ALU.is_gt)\
                            .then_inc(s["cmp_ok"], 1)
                        tt(c1[:], a[:, 2:4, :], a[:, 1:2, :].broadcast_to([P, 2, CH]), ALU.is_gt)\
                            .then_inc(s["cmp_ok"], 1)
                        tt(c2[:], a[:, 3, :], a[:, 2, :], ALU.is_gt).then_inc(s["cmp_ok"], 1)
                        dve.wait_ge(s["cmp_ok"], 3 * i + 3)
                        tt(k[:, 0, :], c0[:, 0, :], c0[:, 1, :], ALU.add).then_inc(s["k1_ok"], 1)
                        tt(k[:, 1, :], c1[:, 0, :], c1[:, 1, :], ALU.add).then_inc(s["k1_ok"], 1)
                        tt(k[:, 2:4, :], c0[:, 1:3, :], c1[:], ALU.add).then_inc(s["k1_ok"], 1)
                        dve.wait_ge(s["k1_ok"], 3 * i + 3)
                        tt(k[:, 0, :], k[:, 0, :], c0[:, 2, :], ALU.add).then_inc(s["k2_ok"], 1)
                        tt(k[:, 1, :], k[:, 1, :], c0[:, 0, :], ALU.subtract).then_inc(s["k2_ok"], 1)
                        tt(k[:, 2, :], c2[:], k[:, 2, :], ALU.subtract).then_inc(s["k2_ok"], 1)
                        tt(k[:, 3, :], k[:, 3, :], c2[:], ALU.add).then_inc(s["k2_ok"], 1)
                        dve.wait_ge(s["k2_ok"], 4 * i + 4)
                        keep = ((ALU.is_lt, 2.0), (ALU.is_lt, 1.0), (ALU.is_lt, 0.0), (ALU.is_gt, 1.0))
                        for r, (op, than) in enumerate(keep):
                            stt(out=h[:, r, :], in0=k[:, r, :], scalar=than, in1=h[:, r, :], op0=op,
                                op1=ALU.mult).then_inc(s["hs_ok"], 1)
                        for r in range(4):
                            dve.wait_ge(s["hh_ok"], 4 * i + r + 1)
                            tt(hl[:, r, :], h[:, r, :], f32(hh[:, r, :]), ALU.subtract)\
                                .then_inc(s["hl_ok"], 1)
            groups(dve, run)

        @block.tensor
        def _(pe):
            def run(ev):
                for what, c, q, r in ev:
                    i = q * NC + c
                    start = c == 0 and is_first(q)
                    if what == "turn":
                        if c == 0 and r == 0:
                            pe.wait_ge(s["consts"], 16)
                        nrm.wait(pe, c * TC + r + 1)
                        if c > 0:
                            pe.wait_ge(s["xl_ok"], (c - 1) * TC + r + 1)
                        for d in range(ND):
                            last = nc.tensor.transpose(yb[:, r, d * P:(d + 1) * P],
                                                       X[:, c * TC + r, d * P:(d + 1) * P], ident[:])
                        last.then_inc(s["xt_ok"], 1)
                    elif what == "up":
                        u = i * 4 + r
                        cs = slice(c * CH, (c + 1) * CH)
                        if r == 0 and is_first(q):
                            pe.wait_ge(s["xl_ok"], (c + 1) * TC)
                        if not (start and r < 2):
                            pe.wait_ge(s["h_ok"], u - 1)
                        if c == 0:
                            pe.wait_ge(s["wlo"], q * NPC + r + 1)
                        for which in range(2):
                            for d in range(ND):
                                at = (which * ND + d) * P
                                last = mm3(nc, gu[:, r % 2, which, :], wh[:, r, at:at + P],
                                           wl[:, r, at:at + P], xh[:, d, cs], xl[:, d, cs],
                                           d == 0, d == ND - 1)
                        last.then_inc(s["gu_ok"], 1)
                    elif what == "down":
                        if start:
                            pe.wait_ge(s["xl_ok"], NT)
                        pe.wait_ge(s["hl_ok"], (i + 1) * 4)
                        if c == 0:
                            pe.wait_ge(s["wlo"], (q + 1) * NPC)
                        for t in range(TC):
                            if not start:
                                pe.wait_ge(s["acc_ok"], (i - 1) * TC + t + 1)
                            for r in range(4):
                                ts = slice(t * P, (t + 1) * P)
                                at = r % 2 * D
                                last = mm3(nc, yb[:, t, :], hh[:, r, ts], hl[:, r, ts],
                                           wh[:, 4 + r // 2, at:at + D], wl[:, 4 + r // 2, at:at + D],
                                           r == 0, r == 3)
                            last.then_inc(s["y_ok"], 1)
            groups(pe, run)


_INPUTS = ("xT x wqkv0 rope0 rot0 eye masks wo0 gate_w gate_bias lower w_exp wqkv1 qk_bias v_bias rope1 "
           "rot1 wo1 w_mlp").split()


def build(nc, ins, out):
    def dram(name, shape):
        return nc.dram_tensor(name, shape, F32).ap()

    attn_out = dram("attn_out", (S, D))
    weights_t = dram("weights_t", (NE, S))
    x2, y_dram = dram("x2", (S, D)), dram("y1", (S, D))
    q_dram = dram("q1", (2, P, ND, S))
    v_dram = dram("v1", (2, P, NT, D))
    with ExitStack() as ctx:
        nrm = Norm(nc, ctx)
        loads, loads2, stores = Ring(nc, "loads"), Ring(nc, "loads2"), Ring(nc, "stores")
        layer0_attention(nc, loads, ins["xT"], ins["wqkv0"], ins["rope0"], ins["rot0"],
                         ins["eye"], ins["masks"], attn_out)
        loads.stage_over(4, ND * NC // 4)
        hi = ctx.enter_context(nc.sbuf_tensor("hi", [P, ND, S], F32R))
        lo = ctx.enter_context(nc.sbuf_tensor("lo", [P, ND, S], F32R))
        with nc.sbuf_tensor("X", [P, NT, D], F32) as X, ExitStack() as ctx0:
            w0h = ctx0.enter_context(nc.sbuf_tensor("w0h", [P, EW], F32R))
            w0l = ctx0.enter_context(nc.sbuf_tensor("w0l", [P, EW], F32R))
            layer0_project(nc, nrm, loads, loads2, ins["x"], attn_out, ins["wo0"], ins["gate_w"],
                           ins["gate_bias"], ins["lower"], ins["eye"], ins["w_exp"], X, hi, lo, w0h, w0l, weights_t)
            nrm.stage_over()
            loads.stage_over(TC, NC)
            loads2.stage_over(TC, NC)
            layer0_experts(nc, loads2, ins["w_exp"], weights_t, X, hi, lo, w0h, w0l)
            ctx0.close()
            loads2.stage_over(2, NE // 2)
            layer1_qkv(nc, nrm, loads, ins["wqkv1"], ins["qk_bias"], ins["v_bias"], ins["rope1"], ins["rot1"],
                       ins["eye"], X, hi, lo, x2, q_dram, v_dram)
            nrm.stage_over()
            loads.stage_over(4, 3 * ND // 4)
        layer1_attention(nc, loads, loads2, stores, ins["wo1"], ins["eye"], hi, lo, x2, q_dram, v_dram,
                         y_dram)
        loads.stage_over(2, NT)
        loads2.stage_over(2, NT // 2)
        stores.stage_over(2, NT // 2)
        with nc.sbuf_tensor("X1", [P, NT, D], F32) as X:
            layer1_mlp(nc, nrm, loads, loads2, stores, ins["w_mlp"], y_dram, ins["eye"], X, hi, lo, out)


def rotary(dims, freqs, base_rows):
    import numpy as np
    f = freqs[:, None] * np.arange(S, dtype=np.float32)[None, :]
    cos, sin = np.ones((P, S), np.float32), np.zeros((P, S), np.float32)
    swap = np.zeros((P, P), np.float32)
    for b in base_rows:
        for i in range(dims):
            lo, up = b + i, b + dims + i
            cos[lo], sin[lo], cos[up], sin[up] = np.cos(f[i]), np.sin(f[i]), np.cos(f[i]), np.sin(f[i])
            swap[up, lo], swap[lo, up] = -1.0, 1.0
    return np.stack([cos, sin]), swap


def layout(inputs):
    import numpy as np
    a = {k: np.asarray(v) for k, v in inputs.items()}
    x = a["L0_attn_x"].reshape(S, D)

    def turned(w, n):
        return w.T.reshape(-1, P, n).transpose(1, 0, 2)

    half = HD0 // 2
    order = np.concatenate([np.r_[h * half:(h + 1) * half, H0 * half + h * half:H0 * half + (h + 1) * half]
                            for h in range(H0)])
    q0 = np.concatenate([a["L0_attn_Wq_sem"], a["L0_attn_Wq_geo"]])[order]
    k0 = np.concatenate([a["L0_attn_Wk_sem"], a["L0_attn_Wk_geo"]])[order]
    qkv0 = np.stack([w.reshape(NG, P, ND, P).transpose(0, 3, 2, 1) for w in (q0, k0, a["L0_attn_Wv"])], 2)
    freqs0 = (1.0 / np.float32(10000.0) ** (np.arange(0, half, 2, dtype=np.float32) / np.float32(half)))
    rope0, rot0 = rotary(half // 2, freqs0.astype(np.float32), [h * HD0 + half for h in range(GH)])
    freqs1 = (1.0 / np.float32(10000.0) ** (np.arange(0, 64, dtype=np.float32) / np.float32(64)))
    rope1, rot1 = rotary(64, freqs1.astype(np.float32), [0])
    i = np.arange(P)
    hidden = i[None, :] > i[:, None]
    masks = np.stack([np.where(hidden, np.float32(BIG), np.float32(0)),
                      np.where(hidden.T, np.float32(BIG), np.float32(0))], 1).astype(np.float32)
    lower = (np.arange(NE)[None, :] < np.arange(NE)[:, None]).astype(np.float32).reshape(-1)

    def expert(w1, w3, w2):
        return np.concatenate([turned(w1, HID).reshape(P, -1), turned(w3, HID).reshape(P, -1),
                               turned(w2, D).reshape(P, -1)], 1)

    w_exp = np.stack([expert(a["L0_ffn_sw1"], a["L0_ffn_sw3"], a["L0_ffn_sw2"])] +
                     [expert(a["L0_ffn_w1"][e], a["L0_ffn_w3"][e], a["L0_ffn_w2"][e]) for e in range(NE)])
    qw, kvw = a["L1_attn_q_w"], a["L1_attn_kv_w"]
    qkv1 = np.stack([turned(w, D) for w in (qw, kvw[:D], kvw[D:])])
    kvb = a["L1_attn_kv_b"]
    qk_bias = np.stack([a["L1_attn_q_b"].reshape(ND, P).T, kvb[:D].reshape(ND, P).T], 1)

    def up(w):
        return w.reshape(ND, P, NQ, P, 4).transpose(2, 4, 1, 0, 3).reshape(NQ, 4, P, ND * P)

    gate_up = np.concatenate([up(a["L1_ffn_w_gate"]), up(a["L1_ffn_w_up"])], 3)
    down = a["L1_ffn_w_down"].reshape(NQ, P, 2, 2 * D).transpose(0, 2, 1, 3)
    laid = dict(xT=x.T, x=x, wqkv0=qkv0, rope0=rope0, rot0=rot0, eye=np.eye(P, dtype=np.float32),
                masks=masks, wo0=turned(a["L0_attn_Wo"], D), gate_w=turned(a["L0_ffn_gate_w"], NE),
                gate_bias=a["L0_ffn_expert_bias"], lower=lower, w_exp=w_exp, wqkv1=qkv1,
                qk_bias=qk_bias, v_bias=kvb[D:], rope1=rope1, rot1=rot1, wo1=turned(a["L1_attn_o_w"], D),
                w_mlp=np.concatenate([gate_up, down], 1))
    return {k: np.ascontiguousarray(v) for k, v in laid.items()}


def kernel(**inputs):
    import numpy as np
    import concourse.bacc as bacc
    from concourse.bass_utils import run_bass_kernel_spmd as run

    laid = layout(inputs)
    nc = bacc.Bacc("TRN2", target_bir_lowering=False, num_devices=1)
    ins = {n: nc.dram_tensor(f"in_{n}", laid[n].shape, mybir.dt.from_np(laid[n].dtype),
                             kind="ExternalInput").ap() for n in _INPUTS}
    out = nc.dram_tensor("out", (S, D), F32, kind="ExternalOutput").ap()
    build(nc, ins, out)
    r = run(nc, [{f"in_{n}": laid[n] for n in _INPUTS}], core_ids=[0])
    return r.results[0]["out"].reshape(1, S, D)
```
